# Optimizing a Trainium2 kernel written in Bass

```python
import numpy as np
import jax
import jax.numpy as jnp

def _softmax(x, axis=-1):
    return jax.nn.softmax(x, axis=axis)

def _gelu(x):
    return jax.nn.gelu(x, approximate=True)

def _silu(x):
    return jax.nn.silu(x)

def _sigmoid(x):
    return jax.nn.sigmoid(x)

def _layernorm(x, axis=-1, eps=1e-05):
    m = jnp.mean(x, axis=axis, keepdims=True)
    v = jnp.var(x, axis=axis, keepdims=True)
    return (x - m) / jnp.sqrt(v + eps)

def _scatter_add(tgt, idx, src, axis=0):
    return tgt.at[idx].add(src)

def _segment_sum(src, seg, n):
    return jax.ops.segment_sum(src, seg, n)
kernel_name = 'mk_macaron_d2_jaxref_r4_1d1bc2'

def setup_inputs(seed: int=0):
    np.random.seed(seed)
    _w = jnp.asarray

    def _L0_attn_setup():
        import math
        import jax, jax.numpy as jnp
        import numpy as np
        HID = 512
        H = 16
        HKV = 8
        D = HID // H
        F = D
        SEQ = 512
        BATCH = 2
        THETA = 10000.0

        def _rotate_half(x):
            x1, x2 = (x[..., :x.shape[-1] // 2], x[..., x.shape[-1] // 2:])
            return jnp.concatenate((-x2, x1), axis=-1)

        def _softmax_kernel(x, R):
            n = jnp.sqrt(jnp.sum(x * x, axis=-1, keepdims=True))
            x = x / jnp.maximum(n, 1e-06)
            p = jnp.einsum('...d,ed->...e', x, R)
            feats = jnp.concatenate([jnp.sin(p), jnp.cos(p)], axis=-1)
            return feats / math.sqrt(F)
        key = jax.random.key(seed)
        ks = jax.random.split(key, 10)
        s = lambda k, shape, scale=0.02: jax.random.normal(k, shape, dtype=jnp.float32) * scale
        return {'hidden_states': jax.random.normal(ks[0], (BATCH, SEQ, HID), dtype=jnp.float32), 'Wq': s(ks[1], (HID, HID)), 'bq': s(ks[2], (HID,)), 'Wk': s(ks[3], (HKV * D, HID)), 'bk': s(ks[4], (HKV * D,)), 'Wv': s(ks[5], (HKV * D, HID)), 'bv': s(ks[6], (HKV * D,)), 'Wo': s(ks[7], (HID, HID)), 'bo': s(ks[8], (HID,)), 'rand_matrix': jax.random.normal(ks[9], (F // 2, D), dtype=jnp.float32)}
    _L0_attn_in = _L0_attn_setup()

    def _L0_ffn_setup():
        import jax, jax.numpy as jnp
        import numpy as np
        D_MODEL = 512
        NUM_TILES = 64
        D_SLICE = D_MODEL // NUM_TILES
        TILES_PER_CLUSTER = 8
        NUM_CLUSTERS = NUM_TILES // TILES_PER_CLUSTER
        GRID = 16
        LN_EPS = 1e-05
        DIMS = (np.arange(NUM_TILES)[:, None] * D_SLICE + np.arange(D_SLICE)[None, :]) % D_MODEL
        DIMS = jnp.asarray(DIMS, dtype=jnp.int32)

        def _forward(x, ln_gamma, ln_beta, spline_bases, spline_slopes, output_scale):
            B, S, D = x.shape
            N = B * S
            mu = jnp.mean(x, axis=-1, keepdims=True)
            var = jnp.mean(jnp.square(x - mu), axis=-1, keepdims=True)
            xn = (x - mu) * jax.lax.rsqrt(var + LN_EPS) * ln_gamma + ln_beta
            xf = xn.reshape(N, D)
            slope_sign = jnp.sign(jnp.mean(spline_slopes, axis=-1))
            tile_sigs = jnp.zeros((NUM_TILES, D), dtype=x.dtype)
            tile_sigs = tile_sigs.at[jnp.arange(NUM_TILES)[:, None], DIMS].set(slope_sign)
            cluster_sigs = jnp.sign(tile_sigs.reshape(NUM_CLUSTERS, TILES_PER_CLUSTER, D).mean(axis=1))
            cluster_assign = jnp.arange(NUM_TILES, dtype=jnp.int32) // TILES_PER_CLUSTER
            input_sigs = jnp.sign(xf)
            cluster_scores = input_sigs @ cluster_sigs.T
            best_cluster = jnp.argmax(cluster_scores, axis=-1)
            tile_scores = input_sigs @ tile_sigs.T
            in_cluster = cluster_assign[None, :] == best_cluster[:, None]
            tile_idx = jnp.argmax(jnp.where(in_cluster, tile_scores, -jnp.inf), axis=-1)
            tok_dims = DIMS[tile_idx]
            x_slice = jnp.take_along_axis(xf, tok_dims, axis=1)
            tok_min = x_slice.min(axis=1)
            tok_max = x_slice.max(axis=1)
            onehot = tile_idx[None, :] == jnp.arange(NUM_TILES)[:, None]
            tile_min = jnp.where(onehot, tok_min[None, :], jnp.inf).min(axis=1)
            tile_max = jnp.where(onehot, tok_max[None, :], -jnp.inf).max(axis=1)
            mn = tile_min[tile_idx][:, None]
            mx = tile_max[tile_idx][:, None]
            u = jnp.clip((x_slice - mn) / (mx - mn + 1e-08), 0.0, 1.0 - 1e-06)
            gi = jnp.clip((u * GRID).astype(jnp.int32), 0, GRID - 1)
            j = jnp.arange(D_SLICE)[None, :]
            b = spline_bases[tile_idx[:, None], j, gi]
            s = spline_slopes[tile_idx[:, None], j, gi]
            x_local = (u - gi.astype(u.dtype) / GRID) * GRID
            delta = (b + s * x_local) * output_scale[tile_idx][:, None]
            out = jnp.zeros_like(xf).at[jnp.arange(N)[:, None], tok_dims].set(delta)
            return x + out.reshape(B, S, D)
        key = jax.random.key(seed)
        k1, k2, k3, k4, k5, k6 = jax.random.split(key, 6)
        x = jax.random.normal(k1, (4, 1024, D_MODEL), dtype=jnp.float32)
        ln_gamma = 1.0 + 0.1 * jax.random.normal(k2, (D_MODEL,), dtype=jnp.float32)
        ln_beta = 0.1 * jax.random.normal(k3, (D_MODEL,), dtype=jnp.float32)
        spline_bases = 0.1 * jax.random.normal(k4, (NUM_TILES, D_SLICE, GRID), dtype=jnp.float32)
        spline_slopes = 0.1 + 0.1 * jax.random.normal(k5, (NUM_TILES, D_SLICE, GRID), dtype=jnp.float32)
        output_scale = 1.0 + 0.1 * jax.random.normal(k6, (NUM_TILES,), dtype=jnp.float32)
        return {'x': x, 'ln_gamma': ln_gamma, 'ln_beta': ln_beta, 'spline_bases': spline_bases, 'spline_slopes': spline_slopes, 'output_scale': output_scale}
    _L0_ffn_in = _L0_ffn_setup()

    def _L1_attn_setup():
        import math
        import jax, jax.numpy as jnp
        import numpy as np
        B, T, E = (2, 512, 512)
        NUM_HEADS = 16
        H = NUM_HEADS // 2
        D = E // NUM_HEADS
        DEPTH = 12
        LAMBDA_INIT = 0.8 - 0.6 * math.exp(-0.3 * DEPTH)
        EPS = 1e-05

        def _forward(x, Wq, Wk, Wv, Wo, lq1, lk1, lq2, lk2, g):
            Bz, Tl, _ = x.shape
            q = (x @ Wq).reshape(Bz, Tl, H, 2, D)
            k = (x @ Wk).reshape(Bz, Tl, H, 2, D)
            v = (x @ Wv).reshape(Bz, Tl, H, 2 * D)
            scale = D ** (-0.5)
            causal = jnp.tril(jnp.ones((Tl, Tl), dtype=bool))

            def attend(qc, kc):
                s = jnp.einsum('bthd,bshd->bhts', qc, kc) * scale
                s = jnp.where(causal, s, -jnp.inf)
                a = jax.nn.softmax(s, axis=-1)
                return jnp.einsum('bhts,bshe->bthe', a, v)
            o1 = attend(q[..., 0, :], k[..., 0, :])
            o2 = attend(q[..., 1, :], k[..., 1, :])
            lam = jnp.exp(jnp.sum(lq1 * lk1)) - jnp.exp(jnp.sum(lq2 * lk2)) + LAMBDA_INIT
            o = o1 - lam * o2
            o = o * jax.lax.rsqrt(jnp.mean(o * o, axis=-1, keepdims=True) + EPS) * g
            o = o * (1.0 - LAMBDA_INIT)
            return o.reshape(Bz, Tl, E) @ Wo
        key = jax.random.key(seed)
        ks = jax.random.split(key, 10)
        sc = lambda k, shape, std: jax.random.normal(k, shape, dtype=jnp.float32) * std
        return {'x': jax.random.normal(ks[0], (B, T, E), dtype=jnp.float32), 'Wq': sc(ks[1], (E, E), 0.02), 'Wk': sc(ks[2], (E, E), 0.02), 'Wv': sc(ks[3], (E, E), 0.02), 'Wo': sc(ks[4], (E, E), 0.02), 'lambda_q1': sc(ks[5], (D,), 0.1), 'lambda_k1': sc(ks[6], (D,), 0.1), 'lambda_q2': sc(ks[7], (D,), 0.1), 'lambda_k2': sc(ks[8], (D,), 0.1), 'g': jnp.ones((2 * D,), dtype=jnp.float32)}
    _L1_attn_in = _L1_attn_setup()

    def _L1_ffn_setup():
        import jax, jax.numpy as jnp
        import numpy as np
        HIDDEN = 512
        INTER = 2048
        SCALE = 64.0

        def fwht(x):
            orig_shape = x.shape
            n = orig_shape[-1]
            x = x.reshape(-1, n)
            h = 1
            while h < n:
                x = x.reshape(-1, n // (2 * h), 2, h)
                a, b = (x[:, :, 0, :], x[:, :, 1, :])
                x = jnp.stack([a + b, a - b], axis=2).reshape(-1, n)
                h *= 2
            return (x / jnp.sqrt(jnp.asarray(n, x.dtype))).reshape(orig_shape)
        key = jax.random.key(seed)
        ks = jax.random.split(key, 8)
        inp = jax.random.normal(ks[0], (4, 512, HIDDEN), dtype=jnp.float32)
        SU_ug = jnp.where(jax.random.bernoulli(ks[1], 0.5, (HIDDEN,)), 1.0, -1.0).astype(jnp.float32)
        SU_dp = jnp.where(jax.random.bernoulli(ks[2], 0.5, (INTER,)), 1.0, -1.0).astype(jnp.float32)
        Wscale_ug = jax.random.uniform(ks[3], (2 * INTER,), jnp.float32, 0.5, 1.5)
        Wscale_dp = jax.random.uniform(ks[4], (HIDDEN,), jnp.float32, 0.5, 1.5)
        W_up = jax.random.normal(ks[5], (INTER, HIDDEN), dtype=jnp.float32) * 0.02
        W_gate = jax.random.normal(ks[6], (INTER, HIDDEN), dtype=jnp.float32) * 0.02
        W_down = jax.random.normal(ks[7], (HIDDEN, INTER), dtype=jnp.float32) * 0.02
        return {'input': inp, 'SU_ug': SU_ug, 'SU_dp': SU_dp, 'Wscale_ug': Wscale_ug, 'Wscale_dp': Wscale_dp, 'W_up': W_up, 'W_gate': W_gate, 'W_down': W_down}
    _L1_ffn_in = _L1_ffn_setup()
    _d = {'L0_attn_hidden_states': _L0_attn_in['hidden_states'], 'L0_attn_Wq': _L0_attn_in['Wq'], 'L0_attn_bq': _L0_attn_in['bq'], 'L0_attn_Wk': _L0_attn_in['Wk'], 'L0_attn_bk': _L0_attn_in['bk'], 'L0_attn_Wv': _L0_attn_in['Wv'], 'L0_attn_bv': _L0_attn_in['bv'], 'L0_attn_Wo': _L0_attn_in['Wo'], 'L0_attn_bo': _L0_attn_in['bo'], 'L0_attn_rand_matrix': _L0_attn_in['rand_matrix'], 'L0_ffn_ln_gamma': _L0_ffn_in['ln_gamma'], 'L0_ffn_ln_beta': _L0_ffn_in['ln_beta'], 'L0_ffn_spline_bases': _L0_ffn_in['spline_bases'], 'L0_ffn_spline_slopes': _L0_ffn_in['spline_slopes'], 'L0_ffn_output_scale': _L0_ffn_in['output_scale'], 'L1_attn_Wq': _L1_attn_in['Wq'], 'L1_attn_Wk': _L1_attn_in['Wk'], 'L1_attn_Wv': _L1_attn_in['Wv'], 'L1_attn_Wo': _L1_attn_in['Wo'], 'L1_attn_lambda_q1': _L1_attn_in['lambda_q1'], 'L1_attn_lambda_k1': _L1_attn_in['lambda_k1'], 'L1_attn_lambda_q2': _L1_attn_in['lambda_q2'], 'L1_attn_lambda_k2': _L1_attn_in['lambda_k2'], 'L1_attn_g': _L1_attn_in['g'], 'L1_ffn_SU_ug': _L1_ffn_in['SU_ug'], 'L1_ffn_SU_dp': _L1_ffn_in['SU_dp'], 'L1_ffn_Wscale_ug': _L1_ffn_in['Wscale_ug'], 'L1_ffn_Wscale_dp': _L1_ffn_in['Wscale_dp'], 'L1_ffn_W_up': _L1_ffn_in['W_up'], 'L1_ffn_W_gate': _L1_ffn_in['W_gate'], 'L1_ffn_W_down': _L1_ffn_in['W_down']}
    _x0 = _d['L0_attn_hidden_states']
    _d['L0_attn_hidden_states'] = jax.random.normal(jax.random.fold_in(jax.random.key(seed), 1), (4, 512, 512), dtype=_x0.dtype)
    del _x0
    return _d

def reference(L0_attn_hidden_states, L0_attn_Wq, L0_attn_bq, L0_attn_Wk, L0_attn_bk, L0_attn_Wv, L0_attn_bv, L0_attn_Wo, L0_attn_bo, L0_attn_rand_matrix, L0_ffn_ln_gamma, L0_ffn_ln_beta, L0_ffn_spline_bases, L0_ffn_spline_slopes, L0_ffn_output_scale, L1_attn_Wq, L1_attn_Wk, L1_attn_Wv, L1_attn_Wo, L1_attn_lambda_q1, L1_attn_lambda_k1, L1_attn_lambda_q2, L1_attn_lambda_k2, L1_attn_g, L1_ffn_SU_ug, L1_ffn_SU_dp, L1_ffn_Wscale_ug, L1_ffn_Wscale_dp, L1_ffn_W_up, L1_ffn_W_gate, L1_ffn_W_down):

    def _L0_attn_ref(hidden_states, Wq, bq, Wk, bk, Wv, bv, Wo, bo, rand_matrix):
        import math
        import jax, jax.numpy as jnp
        import numpy as np
        HID = 512
        H = 16
        HKV = 8
        D = HID // H
        F = D
        SEQ = 512
        BATCH = 2
        THETA = 10000.0

        def _rotate_half(x):
            x1, x2 = (x[..., :x.shape[-1] // 2], x[..., x.shape[-1] // 2:])
            return jnp.concatenate((-x2, x1), axis=-1)

        def _softmax_kernel(x, R):
            n = jnp.sqrt(jnp.sum(x * x, axis=-1, keepdims=True))
            x = x / jnp.maximum(n, 1e-06)
            p = jnp.einsum('...d,ed->...e', x, R)
            feats = jnp.concatenate([jnp.sin(p), jnp.cos(p)], axis=-1)
            return feats / math.sqrt(F)
        b, s, _ = hidden_states.shape
        q = (hidden_states @ Wq.T + bq).reshape(b, s, H, D).transpose(0, 2, 1, 3)
        k = (hidden_states @ Wk.T + bk).reshape(b, s, HKV, D).transpose(0, 2, 1, 3)
        v = (hidden_states @ Wv.T + bv).reshape(b, s, HKV, D).transpose(0, 2, 1, 3)
        inv_freq = 1.0 / THETA ** (jnp.arange(0, D, 2, dtype=jnp.float32) / D)
        freqs = jnp.arange(s, dtype=jnp.float32)[:, None] * inv_freq[None, :]
        emb = jnp.concatenate((freqs, freqs), axis=-1)
        cos = jnp.cos(emb)[None, None, :, :]
        sin = jnp.sin(emb)[None, None, :, :]
        q = q * cos + _rotate_half(q) * sin
        k = k * cos + _rotate_half(k) * sin
        rep = H // HKV
        k = jnp.repeat(k, rep, axis=1)
        v = jnp.repeat(v, rep, axis=1)
        qp = _softmax_kernel(q, rand_matrix)
        kp = _softmax_kernel(k, rand_matrix)
        kv = jnp.einsum('bhsf,bhsd->bsfd', kp, v)
        out = jnp.einsum('bhsf,bsfd->bhsd', qp, kv)
        out = out.reshape(b, s, HID)
        return out @ Wo.T + bo

    def _L0_ffn_ref(x, ln_gamma, ln_beta, spline_bases, spline_slopes, output_scale):
        import jax, jax.numpy as jnp
        import numpy as np
        D_MODEL = 512
        NUM_TILES = 64
        D_SLICE = D_MODEL // NUM_TILES
        TILES_PER_CLUSTER = 8
        NUM_CLUSTERS = NUM_TILES // TILES_PER_CLUSTER
        GRID = 16
        LN_EPS = 1e-05
        DIMS = (np.arange(NUM_TILES)[:, None] * D_SLICE + np.arange(D_SLICE)[None, :]) % D_MODEL
        DIMS = jnp.asarray(DIMS, dtype=jnp.int32)

        def _forward(x, ln_gamma, ln_beta, spline_bases, spline_slopes, output_scale):
            B, S, D = x.shape
            N = B * S
            mu = jnp.mean(x, axis=-1, keepdims=True)
            var = jnp.mean(jnp.square(x - mu), axis=-1, keepdims=True)
            xn = (x - mu) * jax.lax.rsqrt(var + LN_EPS) * ln_gamma + ln_beta
            xf = xn.reshape(N, D)
            slope_sign = jnp.sign(jnp.mean(spline_slopes, axis=-1))
            tile_sigs = jnp.zeros((NUM_TILES, D), dtype=x.dtype)
            tile_sigs = tile_sigs.at[jnp.arange(NUM_TILES)[:, None], DIMS].set(slope_sign)
            cluster_sigs = jnp.sign(tile_sigs.reshape(NUM_CLUSTERS, TILES_PER_CLUSTER, D).mean(axis=1))
            cluster_assign = jnp.arange(NUM_TILES, dtype=jnp.int32) // TILES_PER_CLUSTER
            input_sigs = jnp.sign(xf)
            cluster_scores = input_sigs @ cluster_sigs.T
            best_cluster = jnp.argmax(cluster_scores, axis=-1)
            tile_scores = input_sigs @ tile_sigs.T
            in_cluster = cluster_assign[None, :] == best_cluster[:, None]
            tile_idx = jnp.argmax(jnp.where(in_cluster, tile_scores, -jnp.inf), axis=-1)
            tok_dims = DIMS[tile_idx]
            x_slice = jnp.take_along_axis(xf, tok_dims, axis=1)
            tok_min = x_slice.min(axis=1)
            tok_max = x_slice.max(axis=1)
            onehot = tile_idx[None, :] == jnp.arange(NUM_TILES)[:, None]
            tile_min = jnp.where(onehot, tok_min[None, :], jnp.inf).min(axis=1)
            tile_max = jnp.where(onehot, tok_max[None, :], -jnp.inf).max(axis=1)
            mn = tile_min[tile_idx][:, None]
            mx = tile_max[tile_idx][:, None]
            u = jnp.clip((x_slice - mn) / (mx - mn + 1e-08), 0.0, 1.0 - 1e-06)
            gi = jnp.clip((u * GRID).astype(jnp.int32), 0, GRID - 1)
            j = jnp.arange(D_SLICE)[None, :]
            b = spline_bases[tile_idx[:, None], j, gi]
            s = spline_slopes[tile_idx[:, None], j, gi]
            x_local = (u - gi.astype(u.dtype) / GRID) * GRID
            delta = (b + s * x_local) * output_scale[tile_idx][:, None]
            out = jnp.zeros_like(xf).at[jnp.arange(N)[:, None], tok_dims].set(delta)
            return x + out.reshape(B, S, D)
        return _forward(x, ln_gamma, ln_beta, spline_bases, spline_slopes, output_scale)

    def _L1_attn_ref(x, Wq, Wk, Wv, Wo, lambda_q1, lambda_k1, lambda_q2, lambda_k2, g):
        import math
        import jax, jax.numpy as jnp
        import numpy as np
        B, T, E = (2, 512, 512)
        NUM_HEADS = 16
        H = NUM_HEADS // 2
        D = E // NUM_HEADS
        DEPTH = 12
        LAMBDA_INIT = 0.8 - 0.6 * math.exp(-0.3 * DEPTH)
        EPS = 1e-05

        def _forward(x, Wq, Wk, Wv, Wo, lq1, lk1, lq2, lk2, g):
            Bz, Tl, _ = x.shape
            q = (x @ Wq).reshape(Bz, Tl, H, 2, D)
            k = (x @ Wk).reshape(Bz, Tl, H, 2, D)
            v = (x @ Wv).reshape(Bz, Tl, H, 2 * D)
            scale = D ** (-0.5)
            causal = jnp.tril(jnp.ones((Tl, Tl), dtype=bool))

            def attend(qc, kc):
                s = jnp.einsum('bthd,bshd->bhts', qc, kc) * scale
                s = jnp.where(causal, s, -jnp.inf)
                a = jax.nn.softmax(s, axis=-1)
                return jnp.einsum('bhts,bshe->bthe', a, v)
            o1 = attend(q[..., 0, :], k[..., 0, :])
            o2 = attend(q[..., 1, :], k[..., 1, :])
            lam = jnp.exp(jnp.sum(lq1 * lk1)) - jnp.exp(jnp.sum(lq2 * lk2)) + LAMBDA_INIT
            o = o1 - lam * o2
            o = o * jax.lax.rsqrt(jnp.mean(o * o, axis=-1, keepdims=True) + EPS) * g
            o = o * (1.0 - LAMBDA_INIT)
            return o.reshape(Bz, Tl, E) @ Wo
        return _forward(x, Wq, Wk, Wv, Wo, lambda_q1, lambda_k1, lambda_q2, lambda_k2, g)

    def _L1_ffn_ref(input, SU_ug, SU_dp, Wscale_ug, Wscale_dp, W_up, W_gate, W_down):
        import jax, jax.numpy as jnp
        import numpy as np
        HIDDEN = 512
        INTER = 2048
        SCALE = 64.0

        def fwht(x):
            orig_shape = x.shape
            n = orig_shape[-1]
            x = x.reshape(-1, n)
            h = 1
            while h < n:
                x = x.reshape(-1, n // (2 * h), 2, h)
                a, b = (x[:, :, 0, :], x[:, :, 1, :])
                x = jnp.stack([a + b, a - b], axis=2).reshape(-1, n)
                h *= 2
            return (x / jnp.sqrt(jnp.asarray(n, x.dtype))).reshape(orig_shape)
        n = SU_ug.shape[0]
        x = input.reshape(-1, n)
        x = fwht(x * SU_ug) / SCALE
        x_up = x @ W_up.T * (Wscale_ug[:INTER] * SCALE)
        x_gate = x @ W_gate.T * (Wscale_ug[INTER:] * SCALE)
        x = jax.nn.silu(x_gate) * x_up
        x = fwht(x * SU_dp) / SCALE
        x = x @ W_down.T * (Wscale_dp * SCALE)
        return x.reshape(input.shape)
    x = L0_attn_hidden_states
    x = x + 0.5 * _L0_ffn_ref(_layernorm(x, axis=-1), L0_ffn_ln_gamma, L0_ffn_ln_beta, L0_ffn_spline_bases, L0_ffn_spline_slopes, L0_ffn_output_scale)
    x = x + _L0_attn_ref(_layernorm(x, axis=-1), L0_attn_Wq, L0_attn_bq, L0_attn_Wk, L0_attn_bk, L0_attn_Wv, L0_attn_bv, L0_attn_Wo, L0_attn_bo, L0_attn_rand_matrix)
    x = x + 0.5 * _L0_ffn_ref(_layernorm(x, axis=-1), L0_ffn_ln_gamma, L0_ffn_ln_beta, L0_ffn_spline_bases, L0_ffn_spline_slopes, L0_ffn_output_scale)
    x = x + 0.5 * _L1_ffn_ref(_layernorm(x, axis=-1), L1_ffn_SU_ug, L1_ffn_SU_dp, L1_ffn_Wscale_ug, L1_ffn_Wscale_dp, L1_ffn_W_up, L1_ffn_W_gate, L1_ffn_W_down)
    x = x + _L1_attn_ref(_layernorm(x, axis=-1), L1_attn_Wq, L1_attn_Wk, L1_attn_Wv, L1_attn_Wo, L1_attn_lambda_q1, L1_attn_lambda_k1, L1_attn_lambda_q2, L1_attn_lambda_k2, L1_attn_g)
    x = x + 0.5 * _L1_ffn_ref(_layernorm(x, axis=-1), L1_ffn_SU_ug, L1_ffn_SU_dp, L1_ffn_Wscale_ug, L1_ffn_Wscale_dp, L1_ffn_W_up, L1_ffn_W_gate, L1_ffn_W_down)
    return x

_drawn_inputs = setup_inputs


def setup_inputs(seed=0):
    import zlib

    import numpy as np

    out = dict(_drawn_inputs(seed))
    spreads = {'L1_attn_g': (1.0, 0.6)}
    factors = {'L0_attn_bq': 8.0,
     'L0_attn_bk': 8.0,
     'L0_attn_bv': 7.632,
     'L0_attn_bo': 4.216,
     'L0_ffn_ln_gamma': 8.0,
     'L0_ffn_ln_beta': 8.0,
     'L0_ffn_spline_bases': 8.0,
     'L0_ffn_spline_slopes': 8.0,
     'L0_ffn_output_scale': 8.0,
     'L1_attn_lambda_q1': 21.353,
     'L1_attn_lambda_k1': 25.961,
     'L1_attn_lambda_q2': 64.0,
     'L1_attn_lambda_k2': 64.0,
     'L1_ffn_Wscale_dp': 3.775,
     'L1_attn_Wq': 2.93,
     'L1_attn_Wk': 2.906}
    for name, (base, spread) in spreads.items():
        noise = np.random.default_rng([zlib.crc32(name.encode()), seed]).standard_normal(out[name].shape)
        drawn = base * np.exp(spread * noise) if base else spread * noise
        out[name] = jnp.asarray(drawn.astype(out[name].dtype))
    for name, factor in factors.items():
        out[name] = (out[name] * factor).astype(out[name].dtype)
    return out
```

```python
from contextlib import ExitStack

import numpy as np
import concourse.bass as bass
from concourse import mybir

ALU = mybir.AluOpType
ACT = mybir.ActivationFunctionType
AXX = mybir.AxisListType.X
F32 = mybir.dt.float32
F16 = mybir.dt.float16
BF16 = mybir.dt.bfloat16

P = 128
HID = 512
KC = HID // P
NTOK = 2048
NT = NTOK // P
CH = 512
NCH = NTOK // CH
TPC = CH // P
INTER = 2048
FB = INTER // P
NTILE, DSL, GRID = 64, 8, 16
CLUS = 8
LN_EPS = 1e-5
ARENA = 228096
W_SCALE = 1024.0
A_SCALE = 64.0
ROUND = float(1.5 * 2 ** 23)
BIG = 1.0e30


def host_constants():
    r = np.arange(P)
    ident = np.eye(P, dtype=np.float32)
    had = np.array([[1.0 - 2.0 * (bin(a & b).count("1") & 1) for b in range(P)] for a in range(P)], np.float32)
    rot = np.zeros((P, P), np.float32)
    for m in range(P):
        if m % 32 < 16:
            rot[m + 16, m] = -1.0
        else:
            rot[m - 16, m] = 1.0
    inv = (1.0 / (np.float32(10000.0) ** (np.arange(0, 32, 2, dtype=np.float32) / np.float32(32)))).astype(np.float32)
    ang = (np.arange(CH, dtype=np.float32)[None, :] * inv[(r % 16)][:, None]).astype(np.float32)
    t = np.arange(NTILE)
    key = np.broadcast_to(((7 - t // 8) * 256 + (7 - t % 8)).astype(np.float32), (P, NTILE))
    iota = np.broadcast_to(np.arange(GRID, dtype=np.float32), (P, GRID))
    causal = np.where(r[None, :] > r[:, None], np.float32(-1e30), np.float32(0.0)).astype(np.float32)
    pick = (r[:, None] % 16 == np.arange(16)[None, :]).astype(np.float32)
    headcol = (r[:, None] // 32 == np.arange(4)[None, :]).astype(np.float32)
    parts = [("ident", ident), ("had", had), ("rot", rot), ("cos", np.cos(ang)),
             ("sin", np.sin(ang)), ("key", key), ("iota", iota), ("causal", causal),
             ("pick", pick), ("headcol", headcol)]
    where, at = {}, 0
    for name, a in parts:
        where[name] = (at, at + a.shape[1])
        at += a.shape[1]
    return np.ascontiguousarray(np.concatenate([a for _, a in parts], axis=1).astype(np.float32)), where


CONSTS, CONST_AT = host_constants()

SEMAPHORES = """
const_in x_in param_in ones_set gates
nat_in0 nat_in1 nat_scaled nat_turned turned wt_hi wt_lo had_done had_hi had_lo
wd_in wd_scaled wd_mixed wd_step wdt_turned wdt_hi wdt_lo wdh_done wdo_hi wdo_lo wdo_out0 wdo_out1
w1_in w1_scaled w1_hi w1_lo w1_out
ssum_ready ss_signed ss_diag ss_spread ss_row up_scale
v_step
var1 std1 var2 std2 norm z_scaled y_ready y_signed routed
minmax_turned table_ready rt_zeroed b_in down_in
ap_oh ap_turned ap_oht ap_rows
n_var n_std n_norm n_h n_turned n_hi n_lo
b_qk_done b_qf b_rot b_rope b_v_done b_v_in b_sq b_proj b_n2 b_n b_angle b_reduced b_feat b_o b_ot b_ot_hi
b_ot_lo b_out b_o_out b_moved b_res
f_gate f_up f_silu f_prod f_hi f_lo f_down f_out
c_in c_lam_in c_lam_dot c_lam_exp c_mask c_set c_qk_done c_qk_hi c_qk_lo c_v_done c_v_in c_score c_max c_negmax
c_max_turned c_maxt c_scored c_exp c_av c_oo c_back c_head c_ms c_rms c_o c_ot c_ot_hi c_ot_lo c_out_done c_out
x_out
""".split()


class Views:

    def __init__(self, arena):
        self.arena = arena

    def at(self, byte, shape, dt):
        size = 1
        for n in shape[1:]:
            size *= n
        width = 4 if dt == F32 else 2
        words = size * width // 4
        assert byte % 4 == 0 and size * width % 4 == 0
        v = self.arena[0:shape[0], byte // 4:byte // 4 + words]
        if dt != F32:
            v = v.bitcast(dt)
        if len(shape) == 3:
            v = v.rearrange("p (a b) -> p a b", a=shape[1])
        if len(shape) == 4:
            v = v.rearrange("p (a b c) -> p a b c", a=shape[1], b=shape[2])
        return v, byte + size * width


class Steps:

    def __init__(self, eng, sem, gates):
        self.eng, self.sem, self.gates = eng, sem, gates
        self.base, self.i, self.per, self.k = 0, 0, 0, 0

    def enter(self, i, per):
        self.i, self.per, self.k = i, per, 0

    def leave(self, n):
        assert self.k == self.per, (self.k, self.per)
        self.base, self.i, self.per, self.k = self.base + n * self.per, 0, 0, 0

    def link(self, ins):
        self.k += 1
        ins.then_inc(self.sem, 1)
        value = self.base + self.i * self.per + self.k if self.per else self.base + self.k
        if not self.per:
            self.base, self.k = self.base + self.k, 0
        gate(self.eng, self.sem, value, self.gates)


def gate(eng, sem, value, gates):
    eng.wait_ge(sem, value)
    if not isinstance(value, int):
        eng.sem_inc(gates, 1)


def phase_buffers(k, v):
    at = k.free_at
    k.h, at = v.at(at, [P, TPC, HID], F32)
    k.ht_hi, at = v.at(at, [P, KC, CH], F16)
    k.ht_lo, at = v.at(at, [P, KC, CH], F16)
    a = at
    k.qf, a = v.at(a, [P, 6, CH], F32)
    k.qr, a = v.at(a, [P, 6, CH], F32)
    k.v0, a = v.at(a, [P, TPC, 256], F32)
    k.yy, a = v.at(a, [P, 24, 2, 16], F32)
    k.yr, a = v.at(a, [P, 24, 2, 16], F32)
    k.feat, a = v.at(a, [P, 24, 32], F32)
    k.work, a = v.at(a, [P, 4096], F32)
    k.ot_hi, a = v.at(a, [P, KC, CH], F16)
    k.ot_lo, a = v.at(a, [P, KC, CH], F16)
    k.bv, a = v.at(a, [P, 256], F32)
    k.bo, a = v.at(a, [P, HID], F32)
    assert a <= ARENA, a
    k.o0 = k.qf[:, 0:4, :]
    k.q2 = k.work[:, 0:3072].rearrange("p (b t) -> p b t", b=6)
    a = at
    k.wd_hi, a = v.at(a, [P, FB, HID], F16)
    k.wd_lo, a = v.at(a, [P, FB, HID], F16)
    k.act_hi, a = v.at(a, [P, FB, CH], F16)
    k.act_lo, a = v.at(a, [P, FB, CH], F16)
    assert a <= ARENA, a
    b = k.w0_at
    k.silu, b = v.at(b, [P, 2, CH], F32)
    k.prod, b = v.at(b, [P, 2, CH], F32)
    k.work1, b = v.at(b, [P, 4096], F32)
    assert b <= k.free_at
    a = at
    k.w1_hi, a = v.at(a, [P, 4, KC, HID], F16)
    k.w1_lo, a = v.at(a, [P, 4, KC, HID], F16)
    k.qk_hi, a = v.at(a, [P, 8, CH], F16)
    k.qk_lo, a = v.at(a, [P, 8, CH], F16)
    k.v1, a = v.at(a, [P, TPC, 8 * 65], F32)
    k.o1, a = v.at(a, [P, TPC, HID], F32)
    assert a <= ARENA, a
    b = k.w0_at
    k.pt, b = v.at(b, [P, 2, TPC, CH], F32)
    k.nm, _ = v.at(b, [P, TPC, 4, 32], F32)
    k.oo, b = v.at(b, [65, 2, CH], F32)
    k.sel, b = v.at(b, [P, 16, P], BF16)
    assert b <= k.free_at
    b = k.onehot_at
    k.maxt, b = v.at(b, [P, CH], BF16)
    k.causal_ts, b = v.at(b, [P, P], BF16)
    k.causal_st, b = v.at(b, [P, P], BF16)
    k.identb, b = v.at(b, [P, P], BF16)
    k.nmb, b = v.at(b, [P, TPC, 16], BF16)
    k.mx, b = v.at(b, [P, TPC, 16], F32)
    k.g, b = v.at(b, [P, 64], F32)
    assert b <= k.onehot_at + 4096


def use_work(k, work, y):
    k.y = y
    k.masked = work[:, 0:2048].rearrange("p (u c) -> p u c", u=TPC)
    k.sg = work[:, 2048:3072].bitcast(BF16).rearrange("p (u c) -> p u c", u=TPC)
    k.scat = k.masked
    k.m16 = work[:, 2048:2560].rearrange("p (u j g) -> p u j g", u=TPC, j=DSL)
    k.m16p = work[:, 2560:3072].rearrange("p (u j g) -> p u j g", u=TPC, j=DSL)
    k.oh4 = work[:, 3072:3328].rearrange("p (u t) -> p u t", u=TPC)
    k.oht = work[0:NTILE, 3584:4096]


class Kernel:
    pass


def bcast(ap, shape):
    return ap.to_broadcast(shape)


def place(k, nc, ctx):
    arena = ctx.enter_context(nc.sbuf_tensor("arena", [P, ARENA // 4], F32))
    v = Views(arena)
    at = 0
    k.x, at = v.at(at, [P, NT, HID], F32)
    k.const, at = v.at(at, [P, CONSTS.shape[1]], F32)
    k.onehot_at = at
    k.onehot, at = v.at(at, [P, NT, NTILE], F32)
    k.sliced, at = v.at(at, [P, NT, DSL], F32)
    k.mr, at = v.at(at, [P, NT, 2], F32)
    k.gamma, at = v.at(at, [P, HID], F32)
    k.beta, at = v.at(at, [P, HID], F32)
    k.ssrow, at = v.at(at, [P, HID], BF16)
    k.table, at = v.at(at, [NTILE, 260], F32)
    k.small, at = v.at(at, [P, 704], F32)
    k.rt, at = v.at(at, [P, 64], F32)
    k.signs, at = v.at(at, [P, 2, P], F16)
    k.wug_hi, at = v.at(at, [P, KC, 2 * INTER], F16)
    k.wug_lo, at = v.at(at, [P, KC, 2 * INTER], F16)
    k.w0_at = at
    k.w0_hi, at = v.at(at, [P, KC, 1536], F16)
    k.w0_lo, at = v.at(at, [P, KC, 1536], F16)
    k.free_at = at
    k.views = v
    c = {n: k.const[:, a:b] for n, (a, b) in CONST_AT.items()}
    k.c = c
    a = k.free_at
    k.wd_nat, a = v.at(a, [P, 4, INTER], F32)
    k.wd_tmp, a = v.at(a, [P, INTER], F32)
    k.nat, a = v.at(a, [P, 8, HID], F32)
    k.wt_hi, a = v.at(a, [P, KC, HID], F16)
    k.wt_lo, a = v.at(a, [P, KC, HID], F16)
    k.rows, a = v.at(a, [P, TPC, HID], F32)
    assert a <= ARENA, a
    s = k.small
    phase_buffers(k, v)
    k.stats6 = s[:, 0:24].rearrange("p (u c) -> p u c", c=6)
    k.mv = s[:, 24:32].rearrange("p (u c) -> p u c", c=2)
    k.t4 = [s[:, 32 + 4 * n:36 + 4 * n] for n in range(7)]
    k.clus = s[:, 60:92].rearrange("p (u c) -> p u c", c=CLUS)
    k.kmax = s[:, 92:96]
    k.ends = s[:, 96:104].rearrange("p (u a) -> p u a", a=2)
    k.acc = s[:, 104:232].rearrange("p (a t) -> p a t", a=2)
    k.wscale = s[:, 232:264]
    k.su_ug = s[:, 264:268]
    k.su_dp = s[:, 268:284]
    k.wscale_dp = s[:, 284:288]
    k.ssum = s[0:NTILE, 288:296]
    k.ssign = s[0:NTILE, 296:304]
    k.ends2 = s[0:NTILE, 304:306]
    k.bqk = s[:, 306:312]
    k.mr4 = s[:, 312:320].rearrange("p (u c) -> p u c", c=2)
    k.ap = [s[:, 320 + 32 * m:352 + 32 * m].rearrange("p (u j) -> p u j", j=DSL) for m in range(6)]
    k.cols = s[:, 512:524].rearrange("p (u c) -> p u c", c=3)
    k.n2 = [s[:, 524 + 24 * m:548 + 24 * m] for m in range(4)]
    k.lam = s[:, 620:628]
    k.rs = s[:, 628:636].rearrange("p (m u) -> p m u", m=2)
    k.mx2, k.rr, k.rr2, k.rms = [s[:, 320 + 32 * m:352 + 32 * m] for m in range(4)]
    k.had16 = k.signs[:, 0, :]
    k.had16n = k.signs[:, 1, :]
    return k


def rsqrt_vector(V, r, std, var, t):
    e = V.eng
    V.link(e.reciprocal(r, std))
    V.link(e.tensor_tensor(t, var, r, ALU.mult))
    V.link(e.tensor_tensor(t, t, r, ALU.mult))
    V.link(e.tensor_scalar(t, t, -0.5, 1.5, ALU.mult, ALU.add))
    V.link(e.tensor_tensor(r, r, t, ALU.mult))


def nth(i, n, per, at):
    return i * per + ((n - 1) * per + at)


def token_stats_vector(k, V, i, n, p):
    s, e = k.s, V.eng
    for u in range(TPC):
        ins = e.bn_stats(k.stats6[:, u, :], k.x[:, bass.ds(i * TPC + u, 1), :].squeeze(1))
    V.link(ins)
    for u in range(TPC):
        ins = e.bn_aggr(k.mv[:, u, :], k.stats6[:, u, :])
    V.link(ins)
    ve, std, r, t, std2, r2, nm2 = k.t4
    mean, var = k.mv[:, :, 0], k.mv[:, :, 1]
    e.tensor_scalar(ve, var, LN_EPS, None, ALU.add).then_inc(s[p + "var1"], 1)
    gate(e, s[p + "std1"], i + n, s["gates"])
    rsqrt_vector(V, r, std, ve, t)
    V.link(e.tensor_tensor(t, var, r, ALU.mult))
    V.link(e.tensor_tensor(t, t, r, ALU.mult))
    e.tensor_scalar(ve, t, LN_EPS, None, ALU.add).then_inc(s[p + "var2"], 1)
    gate(e, s[p + "std2"], i + n, s["gates"])
    rsqrt_vector(V, r2, std2, ve, t)
    V.link(e.tensor_tensor(r2, r2, r, ALU.mult))
    mr = k.mr[:, bass.ds(i * TPC, TPC), :]
    V.link(e.tensor_copy(mr[:, :, 0], mean))
    V.link(e.tensor_copy(mr[:, :, 1], r))
    e.scalar_tensor_tensor(out=nm2, in0=mean, scalar=-1.0, in1=r2, op0=ALU.mult, op1=ALU.mult)\
        .then_inc(s[p + "norm"], 1)


def token_stats_scalar(k, e, i, n, p):
    s = k.s
    ve, std, r, t, std2, r2, nm2 = k.t4
    gate(e, s[p + "var1"], i + n, s["gates"])
    e.activation(std, ve, ACT.Sqrt).then_inc(s[p + "std1"], 1)
    gate(e, s[p + "var2"], i + n, s["gates"])
    e.activation(std2, ve, ACT.Sqrt).then_inc(s[p + "std2"], 1)
    gate(e, s[p + "norm"], i + n, s["gates"])
    for u in range(TPC):
        ins = e.activation(k.y[:, u, :], k.x[:, bass.ds(i * TPC + u, 1), :].squeeze(1), ACT.Identity,
                           bias=nm2[:, u:u + 1], scale=r2[:, u:u + 1])
    ins.then_inc(s[p + "z_scaled"], 1)
    gate(e, s[p + "y_ready"], i + n, s["gates"])
    e.activation(k.sg, k.y, ACT.Sign).then_inc(s[p + "y_signed"], 1)


def routing_vector(k, V, i, n, p):
    s, e = k.s, V.eng
    full, tiles = [P, TPC, HID], [P, TPC, NTILE]
    gate(e, s[p + "z_scaled"], i + n, s["gates"])
    V.link(e.tensor_tensor(k.y, k.y, bcast(k.gamma.unsqueeze(1), full), ALU.mult))
    e.tensor_tensor(k.y, k.y, bcast(k.beta.unsqueeze(1), full), ALU.add).then_inc(s[p + "y_ready"], 1)
    gate(e, s[p + "y_signed"], i + n, s["gates"])
    V.link(e.tensor_tensor(k.sg, k.sg, bcast(k.ssrow.unsqueeze(1), full), ALU.mult))
    score = k.masked[:, 0, 0:256].rearrange("p (u t) -> p u t", u=TPC)
    key = k.masked[:, 1, 0:256].rearrange("p (u t) -> p u t", u=TPC)
    V.link(e.tensor_reduce(score, k.sg.rearrange("p u (t j) -> p u t j", j=DSL), AXX, ALU.add))
    V.link(e.tensor_reduce(k.clus, score.rearrange("p u (c t) -> p u c t", c=CLUS), AXX, ALU.add))
    V.link(e.scalar_tensor_tensor(out=key, in0=score, scalar=8.0, in1=bcast(k.c["key"].unsqueeze(1), tiles),
                                  op0=ALU.mult, op1=ALU.add))
    for u in range(TPC):
        ins = e.scalar_tensor_tensor(
            out=key[:, u, :].rearrange("p (c t) -> p c t", c=CLUS),
            in0=bcast(k.clus[:, u, :].unsqueeze(2), [P, CLUS, 8]), scalar=2048.0,
            in1=key[:, u, :].rearrange("p (c t) -> p c t", c=CLUS), op0=ALU.mult, op1=ALU.add)
    V.link(ins)
    V.link(e.tensor_reduce(k.kmax, key, AXX, ALU.max))
    hot = k.onehot[:, bass.ds(i * TPC, TPC), :]
    V.link(e.tensor_tensor(hot, key, bcast(k.kmax.unsqueeze(2), tiles), ALU.is_equal))
    V.link(e.tensor_tensor(k.masked.rearrange("p u (t j) -> p u t j", j=DSL),
                           k.y.rearrange("p u (t j) -> p u t j", j=DSL),
                           bcast(hot.unsqueeze(3), [P, TPC, NTILE, DSL]), ALU.mult))
    mine = k.sliced[:, bass.ds(i * TPC, TPC), :]
    V.link(e.tensor_reduce(mine, k.masked.rearrange("p u (t j) -> p u j t", j=DSL), AXX, ALU.add))
    V.link(e.tensor_reduce(k.ends[:, :, 0], mine, AXX, ALU.max))
    V.link(e.tensor_reduce(k.ends[:, :, 1], mine, AXX, ALU.min))
    V.link(e.tensor_scalar(k.ends[:, :, 1], k.ends[:, :, 1], -1.0, None, ALU.mult))
    off = k.masked[:, 0, 0:256].rearrange("p (u t) -> p u t", u=TPC)
    cand = k.masked[:, 1, :].rearrange("p (u a t) -> p u a t", u=TPC, a=2)
    V.link(e.tensor_scalar(off, hot, 1.0, BIG, ALU.subtract, ALU.mult))
    V.link(e.tensor_tensor(cand, bcast(hot.unsqueeze(2), [P, TPC, 2, NTILE]),
                           bcast(k.ends.unsqueeze(3), [P, TPC, 2, NTILE]), ALU.mult))
    V.link(e.tensor_tensor(cand, cand, bcast(off.unsqueeze(2), [P, TPC, 2, NTILE]), ALU.add))
    best = k.masked[:, 0, 256:384].rearrange("p (a t) -> p a t", a=2)
    V.link(e.tensor_reduce(best, cand.rearrange("p u a t -> p a t u"), AXX, ALU.max))
    e.tensor_tensor(k.acc, k.acc, best, ALU.max).then_inc(s[p + "routed"], 1)
    gate(e, s[p + "routed"], i + n, s["gates"])


STATS_STEPS = 17
ROUTE_STEPS = 17


def minmax_tensor(k, pe, n, p):
    s = k.s
    pe.wait_ge(s[p + "routed"], n * NCH)
    for a in range(2):
        ins = pe.transpose(k.ps[0:NTILE, 0, a * P:(a + 1) * P], k.acc[:, a, :], k.c["ident"])
    ins.then_inc(s[p + "minmax_turned"], 1)


def minmax_vector(k, V, n, p):
    s, e = k.s, V.eng
    e.wait_ge(s[p + "minmax_turned"], n)
    V.link(e.tensor_reduce(k.ends2, k.ps[0:NTILE, 0, 0:256].rearrange("p (a t) -> p a t", a=2), AXX, ALU.max))
    V.link(e.tensor_copy(k.table[:, 258:259], k.ends2[:, 0:1]))
    e.tensor_scalar(k.table[:, 257:258], k.ends2[:, 1:2], -1.0, None, ALU.mult).then_inc(s[p + "table_ready"], 1)
    e.wait_ge(s[p + "table_ready"], n)



UG_GROUPS = 2 * INTER // CH
W0_GROUPS = 3


def setup_sync(k, sp):
    s, d = k.s, k.d
    sp.dma_start(k.const[:, 0:CONSTS.shape[1]], d["constants"]).then_inc(s["const_in"], 16)
    for c in range(NCH):
        sp.dma_start(k.x[:, c * TPC:(c + 1) * TPC, :],
                     d["L0_attn_hidden_states"][c].rearrange("(u p) n -> p u n", p=P)).then_inc(s["x_in"], 16)
    rows = [(k.gamma, d["L0_ffn_ln_gamma"]), (k.beta, d["L0_ffn_ln_beta"])]
    for dst, src in rows:
        sp.dma_start(dst, src.partition_broadcast(P)).then_inc(s["param_in"], 16)
    sp.dma_start(k.table[:, 0:128], d["L0_ffn_spline_bases"].rearrange("t j g -> t (j g)")).then_inc(s["param_in"], 16)
    sp.dma_start(k.table[:, 128:256], d["L0_ffn_spline_slopes"].rearrange("t j g -> t (j g)")).then_inc(s["param_in"], 16)
    sp.dma_start(k.table[:, 256:257], d["L0_ffn_output_scale"].unsqueeze(1)).then_inc(s["param_in"], 16)
    sp.dma_start(k.wscale, d["L1_ffn_Wscale_ug"].rearrange("(b p) -> p b", p=P)).then_inc(s["param_in"], 16)
    sp.dma_start(k.su_ug, d["L1_ffn_SU_ug"].rearrange("(b p) -> p b", p=P)).then_inc(s["param_in"], 16)
    sp.dma_start(k.su_dp, d["L1_ffn_SU_dp"].rearrange("(b p) -> p b", p=P)).then_inc(s["param_in"], 16)
    sp.dma_start(k.wscale_dp, d["L1_ffn_Wscale_dp"].rearrange("(b p) -> p b", p=P)).then_inc(s["param_in"], 16)
    sp.dma_start(k.bqk[:, 0:4], d["L0_attn_bq"].rearrange("(b p) -> p b", p=P)).then_inc(s["param_in"], 16)
    sp.dma_start(k.bqk[:, 4:6], d["L0_attn_bk"].rearrange("(b p) -> p b", p=P)).then_inc(s["param_in"], 16)

    def rows_of(w):
        return w.rearrange("(r p) n -> p r n", p=P)

    def load_nat(group, pieces):
        if group >= 2:
            sp.wait_ge(s["nat_turned"], 4 * (group - 1))
        at = 4 * (group % 2)
        for src, n in pieces:
            sp.dma_start(k.nat[:, at:at + n, :], src).then_inc(s[f"nat_in{group % 2}"], 32 // len(pieces))
            at += n

    load_nat(0, [(rows_of(d["L0_attn_Wq"])[:, 0:2], 2), (rows_of(d["L0_attn_Wq"])[:, 2:4], 2)])
    load_nat(1, [(rows_of(d["L0_attn_Wk"]), 2), (rows_of(d["L0_attn_Wv"]), 2)])
    for o in range(4):
        sp.dma_start(k.wd_nat[:, o, :], d["L1_ffn_W_down"][o * P:(o + 1) * P, :]).then_inc(s["wd_in"], 16)
    load_nat(2, [(rows_of(d["L0_attn_Wo"])[:, 0:2], 2), (rows_of(d["L0_attn_Wo"])[:, 2:4], 2)])
    for g in range(UG_GROUPS):
        w = rows_of(d["L1_ffn_W_up"] if g < UG_GROUPS // 2 else d["L1_ffn_W_gate"])
        r = 4 * (g % (UG_GROUPS // 2))
        load_nat(W0_GROUPS + g, [(w[:, r:r + 2], 2), (w[:, r + 2:r + 4], 2)])
    for m, name in enumerate(["L1_attn_Wq", "L1_attn_Wk", "L1_attn_Wv", "L1_attn_Wo"]):
        group = W0_GROUPS + UG_GROUPS + m
        if m < 2:
            sp.wait_ge(s["nat_turned"], 4 * (group - 1))
        else:
            sp.wait_ge(s["w1_lo"], m - 1)
        at = 4 * (group % 2)
        sp.dma_start(k.nat[:, at:at + 4, :], rows_of(d[name])).then_inc(s["w1_in"], 16)
        sp.wait_ge(s["w1_lo"], m + 1)
        sp.dma_start(d["w1_hi"][m], k.wt_hi).then_inc(s["w1_out"], 16)
        sp.dma_start(d["w1_lo"][m], k.wt_lo).then_inc(s["w1_out"], 16)
    for o in range(4):
        sp.wait_ge(s["wdo_lo"], 4 * (o + 1))
        for dst, src in ((d["wd_hi"], k.wdo_hi[o % 2]), (d["wd_lo"], k.wdo_lo[o % 2])):
            sp.dma_start(dst[:, :, o * P:(o + 1) * P], src).then_inc(s[f"wdo_out{o % 2}"], 16)


def setup_pool(k, e):
    s = k.s
    n = 0
    for o in range(4):
        e.wait_ge(s["wd_scaled"], o + 1)
        bufs = [k.wd_nat[:, o, :], k.wd_tmp]
        for stage in range(4):
            h = P << stage
            a = bufs[stage % 2].rearrange("p (g two m) -> p g two m", two=2, m=h)
            b = bufs[(stage + 1) % 2].rearrange("p (g two m) -> p g two m", two=2, m=h)
            e.tensor_tensor(b[:, :, 0], a[:, :, 0], a[:, :, 1], ALU.add)
            last = stage == 3
            e.tensor_tensor(b[:, :, 1], a[:, :, 0], a[:, :, 1], ALU.subtract)\
                .then_inc(s["wd_mixed"] if last else s["wd_step"], 1)
            if last:
                e.wait_ge(s["wd_mixed"], o + 1)
            else:
                n += 1
                e.wait_ge(s["wd_step"], n)
    for m in range(4):
        e.wait_ge(s["w1_hi"], m + 1)
        at = 4 * ((W0_GROUPS + UG_GROUPS + m) % 2)
        e.tensor_tensor(k.wt_lo, k.nat[:, at:at + 4, :], k.wt_hi, ALU.subtract).then_inc(s["w1_lo"], 1)


def turn_rows(k, pe, tile, buf, r):
    s = k.s
    for c in range(KC):
        ins = pe.transpose(k.ps[:, r % 2, c * P:(c + 1) * P], k.nat[:, buf + r, c * P:(c + 1) * P], k.c["ident"])
    ins.then_inc(s["nat_turned"], 1)


def setup_tensor(k, pe):
    s = k.s
    pe.wait_ge(s["const_in"], 16)
    pe.wait_ge(s["ss_diag"], 1)
    pe.matmul(k.ps[:, 4, :], k.ones, k.diag, start=True, stop=True).then_inc(s["ss_spread"], 1)
    for g in range(W0_GROUPS):
        pe.wait_ge(s[f"nat_in{g % 2}"], 32 * (g // 2 + 1))
        for r in range(4):
            if 4 * g + r >= 2:
                pe.wait_ge(s["wt_lo"], 4 * g + r - 1)
            turn_rows(k, pe, 4 * g + r, 4 * (g % 2), r)
    with pe.Fori(0, UG_GROUPS // 2) as i:
        for odd in range(2):
            buf = 4 * ((W0_GROUPS + odd) % 2)
            tile = 4 * W0_GROUPS + i * 8 + 4 * odd
            gate(pe, s["nat_scaled"], i * 8 + 4 * odd + 4, s["gates"])
            for r in range(4):
                gate(pe, s["wt_lo"], tile + r - 1, s["gates"])
                turn_rows(k, pe, tile + r, buf, r)
            gate(pe, s["wt_lo"], tile + 4, s["gates"])
            for kc in range(KC):
                gate(pe, s["had_lo"], i * 8 + 4 * odd + kc + 1, s["gates"])
                n = 0
                for jc in range(KC):
                    sign = k.had16n if bin(kc & jc).count("1") & 1 else k.had16
                    for part in (k.wt_hi, k.wt_lo):
                        ins = pe.matmul(k.ps[:, 2 + kc % 2, :], sign, part[:, jc, :], start=(n == 0), stop=(n == 7))
                        n += 1
                ins.then_inc(s["had_done"], 1)
    base = 4 * (W0_GROUPS + UG_GROUPS)
    for o in range(4):
        pe.wait_ge(s["wd_mixed"], o + 1)
        for q in range(4):
            if o or q >= 2:
                pe.wait_ge(s["wdt_lo"], 4 * o + q - 1)
            elif q == 0:
                pe.wait_ge(s["wt_lo"], base)
            for b in range(4):
                c = 4 * q + b
                ins = pe.transpose(k.ps[:, q % 2, b * P:(b + 1) * P], k.wd_nat[:, o, c * P:(c + 1) * P], k.c["ident"])
            ins.then_inc(s["wdt_turned"], 1)
        pe.wait_ge(s["wdt_lo"], 4 * o + 4)
        for q in range(4):
            if o or q >= 2:
                pe.wait_ge(s["wdo_lo"], 4 * o + q - 1)
            else:
                pe.wait_ge(s["had_lo"], 2 + 4 * UG_GROUPS)
            for b in range(4):
                c = 4 * q + b
                pe.matmul(k.ps[:, 2 + q % 2, b * P:(b + 1) * P], k.had16, k.wdt_hi[:, c, :], start=True, stop=False)
                ins = pe.matmul(k.ps[:, 2 + q % 2, b * P:(b + 1) * P], k.had16, k.wdt_lo[:, c, :], start=False, stop=True)
            ins.then_inc(s["wdh_done"], 1)


def setup_scalar(k, e):
    s = k.s
    e.wait_ge(s["const_in"], 16)
    e.activation(k.had16, k.c["had"], ACT.Copy)
    e.activation(k.had16n, k.c["had"], ACT.Copy, scale=-1.0).then_inc(s["ones_set"], 1)
    e.wait_ge(s["ssum_ready"], 1)
    e.activation(k.ssign, k.ssum, ACT.Sign).then_inc(s["ss_signed"], 1)
    e.wait_ge(s["ss_spread"], 1)
    e.activation(k.ssrow, k.ps[:, 4, :], ACT.Copy).then_inc(s["ss_row"], 1)
    for o in range(4):
        e.wait_ge(s["wd_in"], 64)
        e.activation(k.wd_nat[:, o, :], k.wd_nat[:, o, :], ACT.Copy, scale=k.wscale_dp[:, o:o + 1])\
            .then_inc(s["wd_scaled"], 1)
    for g in range(W0_GROUPS):
        for r in range(4):
            e.wait_ge(s["nat_turned"], 4 * g + r + 1)
            c = (4 * g + r) * P
            e.activation(k.w0_hi[:, :, c:c + P], k.ps[:, r % 2, :].rearrange("p (c m) -> p c m", c=KC), ACT.Copy,
                         scale=W_SCALE).then_inc(s["wt_hi"], 1)
    e.wait_ge(s["up_scale"], 2)
    with e.Fori(0, UG_GROUPS // 2) as i:
        for odd in range(2):
            buf = 4 * ((W0_GROUPS + odd) % 2)
            gate(e, s[f"nat_in{(W0_GROUPS + odd) % 2}"], i * 32 + 32 * ((W0_GROUPS + odd) // 2 + 1), s["gates"])
            for r in range(4):
                e.activation(k.nat[:, buf + r, :], k.nat[:, buf + r, :], ACT.Copy,
                             scale=k.wscale[:, bass.ds(i * 8 + 4 * odd + r, 1)]).then_inc(s["nat_scaled"], 1)
            for r in range(4):
                tile = 4 * W0_GROUPS + i * 8 + 4 * odd + r
                gate(e, s["nat_turned"], tile + 1, s["gates"])
                e.activation(k.wt_hi[:, :, r * P:(r + 1) * P], k.ps[:, r % 2, :].rearrange("p (c m) -> p c m", c=KC),
                             ACT.Copy, scale=W_SCALE).then_inc(s["wt_hi"], 1)
            for kc in range(KC):
                gate(e, s["had_done"], i * 8 + 4 * odd + kc + 1, s["gates"])
                e.activation(k.wug_hi[:, kc, bass.ds(i * 1024 + CH * odd, CH)], k.ps[:, 2 + kc % 2, :], ACT.Copy,
                             scale=k.su_ug[:, kc:kc + 1]).then_inc(s["had_hi"], 1)
    for m in range(4):
        e.wait_ge(s["w1_in"], 16 * (m + 1))
        at = 4 * ((W0_GROUPS + UG_GROUPS + m) % 2)
        e.activation(k.nat[:, at:at + 4, :], k.nat[:, at:at + 4, :], ACT.Copy, scale=W_SCALE)\
            .then_inc(s["w1_scaled"], 1)
        e.wait_ge(s["w1_scaled"], m + 1)
        if m == 0:
            e.wait_ge(s["had_done"], 4 * UG_GROUPS)
        else:
            e.wait_ge(s["w1_out"], 32 * m)
        e.activation(k.wt_hi, k.nat[:, at:at + 4, :], ACT.Copy).then_inc(s["w1_hi"], 1)
    e.wait_ge(s["w1_out"], 128)
    for o in range(4):
        for q in range(4):
            e.wait_ge(s["wdt_turned"], 4 * o + q + 1)
            if q == 0 and o:
                e.wait_ge(s["wdh_done"], 4 * o)
            e.activation(k.wdt_hi[:, 4 * q:4 * q + 4, :], k.ps[:, q % 2, :].rearrange("p (c m) -> p c m", c=4),
                         ACT.Copy, scale=W_SCALE).then_inc(s["wdt_hi"], 1)
        for q in range(4):
            e.wait_ge(s["wdh_done"], 4 * o + q + 1)
            if q == 0 and o >= 2:
                e.wait_ge(s[f"wdo_out{o % 2}"], 32)
            e.activation(k.wdo_hi[o % 2][:, 4 * q:4 * q + 4, :], k.ps[:, 2 + q % 2, :].rearrange("p (c m) -> p c m", c=4),
                         ACT.Copy, scale=float(INTER) ** -0.5).then_inc(s["wdo_hi"], 1)


def setup_vector_first(k, V):
    s, e = k.s, V.eng
    e.memset(k.ones, 1.0)
    e.memset(k.rt, 0.0).then_inc(s["rt_zeroed"], 1)
    e.memset(k.acc, -BIG).then_inc(s["had_lo"], 2)
    e.wait_ge(s["const_in"], 16)
    e.wait_ge(s["param_in"], 16 * 11)
    e.tensor_reduce(k.ssum, k.table[:, 128:256].rearrange("t (j g) -> t j g", g=GRID), AXX, ALU.add)\
        .then_inc(s["ssum_ready"], 1)
    e.wait_ge(s["ss_signed"], 1)
    e.tensor_tensor(k.diag.rearrange("p (t j) -> p t j", j=DSL),
                    bcast(k.c["ident"][0:NTILE, 0:NTILE].unsqueeze(2), [NTILE, NTILE, DSL]),
                    bcast(k.ssign.unsqueeze(1), [NTILE, NTILE, DSL]), ALU.mult).then_inc(s["ss_diag"], 1)
    e.tensor_tensor(k.wscale[:, 0:FB], k.wscale[:, 0:FB], k.su_dp, ALU.mult).then_inc(s["up_scale"], 1)
    e.tensor_scalar(k.su_ug, k.su_ug, float(HID) ** -0.5, None, ALU.mult).then_inc(s["up_scale"], 1)
    e.wait_ge(s["up_scale"], 2)
    for g in range(W0_GROUPS):
        for r in range(4):
            e.wait_ge(s["wt_hi"], 4 * g + r + 1)
            c = (4 * g + r) * P
            e.scalar_tensor_tensor(out=k.w0_lo[:, :, c:c + P],
                                   in0=k.ps[:, r % 2, :].rearrange("p (c m) -> p c m", c=KC), scalar=W_SCALE,
                                   in1=k.w0_hi[:, :, c:c + P], op0=ALU.mult, op1=ALU.subtract)\
                .then_inc(s["wt_lo"], 1)


def setup_vector_rest(k, V):
    s, e = k.s, V.eng
    with e.Fori(0, UG_GROUPS // 2) as i:
        for odd in range(2):
            for r in range(4):
                gate(e, s["wt_hi"], 4 * W0_GROUPS + i * 8 + 4 * odd + r + 1, s["gates"])
                e.scalar_tensor_tensor(out=k.wt_lo[:, :, r * P:(r + 1) * P],
                                       in0=k.ps[:, r % 2, :].rearrange("p (c m) -> p c m", c=KC), scalar=W_SCALE,
                                       in1=k.wt_hi[:, :, r * P:(r + 1) * P], op0=ALU.mult, op1=ALU.subtract)\
                    .then_inc(s["wt_lo"], 1)
            for kc in range(KC):
                gate(e, s["had_hi"], i * 8 + 4 * odd + kc + 1, s["gates"])
                cols = bass.ds(i * 1024 + CH * odd, CH)
                e.scalar_tensor_tensor(out=k.wug_lo[:, kc, cols], in0=k.ps[:, 2 + kc % 2, :],
                                       scalar=k.su_ug[:, kc:kc + 1], in1=k.wug_hi[:, kc, cols],
                                       op0=ALU.mult, op1=ALU.subtract).then_inc(s["had_lo"], 1)
    for o in range(4):
        for q in range(4):
            e.wait_ge(s["wdt_hi"], 4 * o + q + 1)
            if q == 0 and o:
                e.wait_ge(s["wdh_done"], 4 * o)
            if q == 0 and o == 0:
                e.wait_ge(s["w1_out"], 128)
            e.scalar_tensor_tensor(out=k.wdt_lo[:, 4 * q:4 * q + 4, :],
                                   in0=k.ps[:, q % 2, :].rearrange("p (c m) -> p c m", c=4), scalar=W_SCALE,
                                   in1=k.wdt_hi[:, 4 * q:4 * q + 4, :], op0=ALU.mult, op1=ALU.subtract)\
                .then_inc(s["wdt_lo"], 1)
        for q in range(4):
            e.wait_ge(s["wdo_hi"], 4 * o + q + 1)
            if q == 0 and o >= 2:
                e.wait_ge(s[f"wdo_out{o % 2}"], 32)
            e.scalar_tensor_tensor(out=k.wdo_lo[o % 2][:, 4 * q:4 * q + 4, :],
                                   in0=k.ps[:, 2 + q % 2, :].rearrange("p (c m) -> p c m", c=4),
                                   scalar=float(INTER) ** -0.5, in1=k.wdo_hi[o % 2][:, 4 * q:4 * q + 4, :],
                                   op0=ALU.mult, op1=ALU.subtract).then_inc(s["wdo_lo"], 1)


def first_scalar(k, e, n, p):
    e.wait_ge(k.s["x_in"], 16 * NCH)
    e.wait_ge(k.s["wdo_out0"], 64)
    e.wait_ge(k.s["wdo_out1"], 64)
    with e.Fori(0, NCH) as i:
        token_stats_scalar(k, e, i, n, p)


def first_vector(k, V, n, p):
    V.eng.wait_ge(k.s["x_in"], 16 * NCH)
    V.eng.wait_ge(k.s["ss_row"], 1)
    V.eng.wait_ge(k.s["wdo_out0"], 64)
    V.eng.wait_ge(k.s["wdo_out1"], 64)
    with V.eng.Fori(0, NCH) as i:
        V.enter(i, STATS_STEPS + ROUTE_STEPS)
        token_stats_vector(k, V, i, n, p)
        routing_vector(k, V, i, n, p)
    V.leave(NCH)




def apply_tensor(k, pe, i, n):
    s = k.s
    gate(pe, s["ap_oh"], i + n, s["gates"])
    for u in range(TPC):
        ins = pe.transpose(k.ps[0:NTILE, 6, u * P:(u + 1) * P], k.oh4[:, u, :], k.c["ident"])
    ins.then_inc(s["ap_turned"], 1)
    gate(pe, s["ap_oht"], i + n, s["gates"])
    for u in range(TPC):
        ins = pe.matmul(k.ps[:, 2 + u, 0:259], k.oht[:, u * P:(u + 1) * P], k.table[:, 0:259], start=True, stop=True)
    ins.then_inc(s["ap_rows"], 1)


def apply_scalar(k, e, i, n):
    s = k.s
    gate(e, s["ap_turned"], i + n, s["gates"])
    e.activation(k.oht, k.ps[0:NTILE, 6, :], ACT.Copy).then_inc(s["ap_oht"], 1)


APPLY_STEPS = 27


def apply_vector(k, V, i, n):
    s, e = k.s, V.eng
    tiles = bass.ds(i * TPC, TPC)
    hot = k.onehot[:, tiles, :]
    e.tensor_copy(k.oh4, hot).then_inc(s["ap_oh"], 1)
    a, b = k.t4[0], k.t4[1]
    mr = k.mr[:, tiles, :]
    V.link(e.tensor_scalar(a, mr[:, :, 1], 0.5, None, ALU.mult))
    V.link(e.tensor_tensor(b, mr[:, :, 0], a, ALU.mult))
    V.link(e.tensor_scalar(a, a, 1.0, None, ALU.add))
    for u in range(TPC):
        xt = k.x[:, bass.ds(i * TPC + u, 1), :].squeeze(1)
        ins = e.tensor_scalar(xt, xt, a[:, u:u + 1], b[:, u:u + 1], ALU.mult, ALU.subtract)
    V.link(ins)
    gate(e, s["ap_rows"], i + n, s["gates"])
    rows = k.ps[:, 2:2 + TPC, :]
    V.link(e.tensor_copy(k.cols, rows[:, :, 256:259]))
    full = [P, TPC, DSL]
    u16, lo, fl, d1, xl, sp = k.ap
    half, span, mn, mx = k.t4[0], k.t4[1], k.cols[:, :, 1], k.cols[:, :, 2]
    V.link(e.tensor_tensor(span, mx, mn, ALU.subtract))
    V.link(e.tensor_scalar(span, span, 1e-8, None, ALU.add))
    V.link(e.reciprocal(span, span))
    V.link(e.tensor_scalar(half, k.cols[:, :, 0], 0.5, None, ALU.mult))
    V.link(e.tensor_tensor(u16, k.sliced[:, tiles, :], bcast(mn.unsqueeze(2), full), ALU.subtract))
    V.link(e.tensor_tensor(u16, u16, bcast(span.unsqueeze(2), full), ALU.mult))
    V.link(e.tensor_scalar(u16, u16, 0.0, 1.0 - 1e-6, ALU.max, ALU.min))
    V.link(e.tensor_scalar(u16, u16, float(GRID), None, ALU.mult))
    V.link(e.tensor_scalar(fl, u16, ROUND, ROUND, ALU.add, ALU.subtract))
    V.link(e.tensor_tensor(lo, fl, u16, ALU.is_gt))
    V.link(e.tensor_tensor(fl, fl, lo, ALU.subtract))
    V.link(e.tensor_tensor(xl, u16, fl, ALU.subtract))
    cells = [P, TPC, DSL, GRID]
    V.link(e.tensor_tensor(k.m16, bcast(k.c["iota"].unsqueeze(1).unsqueeze(1), cells), bcast(fl.unsqueeze(3), cells),
                           ALU.is_equal))
    for dst, at in ((sp, 128), (d1, 0)):
        V.link(e.tensor_tensor(k.m16p, k.m16, rows[:, :, at:at + 128].rearrange("p u (j g) -> p u j g", g=GRID),
                               ALU.mult))
        V.link(e.tensor_reduce(dst, k.m16p, AXX, ALU.add))
    V.link(e.tensor_tensor(sp, sp, xl, ALU.mult))
    V.link(e.tensor_tensor(d1, d1, sp, ALU.add))
    V.link(e.tensor_tensor(d1, d1, bcast(half.unsqueeze(2), full), ALU.mult))
    for u in range(TPC):
        ins = e.tensor_tensor(k.scat[:, u, :].rearrange("p (t j) -> p t j", j=DSL),
                              bcast(k.oh4[:, u, :].unsqueeze(2), [P, NTILE, DSL]),
                              bcast(d1[:, u, :].unsqueeze(1), [P, NTILE, DSL]), ALU.mult)
    V.link(ins)
    xs = k.x[:, tiles, :]
    V.link(e.tensor_tensor(xs, xs, k.scat, ALU.add))




NORM_STEPS = 8


def norm_vector(k, V, i, n):
    s, e = k.s, V.eng
    for u in range(TPC):
        ins = e.bn_stats(k.stats6[:, u, :], k.x[:, bass.ds(i * TPC + u, 1), :].squeeze(1))
    V.link(ins)
    for u in range(TPC):
        ins = e.bn_aggr(k.mv[:, u, :], k.stats6[:, u, :])
    V.link(ins)
    ve, std, r, t, std2, r2, nm2 = k.t4
    mean, var = k.mv[:, :, 0], k.mv[:, :, 1]
    e.tensor_scalar(ve, var, LN_EPS, None, ALU.add).then_inc(s["n_var"], 1)
    gate(e, s["n_std"], i + n, s["gates"])
    rsqrt_vector(V, r, std, ve, t)
    V.link(e.tensor_scalar(r2, r, A_SCALE, None, ALU.mult))
    e.scalar_tensor_tensor(out=nm2, in0=mean, scalar=-1.0, in1=r2, op0=ALU.mult, op1=ALU.mult)\
        .then_inc(s["n_norm"], 1)
    for c in range(KC):
        gate(e, s["n_hi"], nth(i, n, KC, c + 1), s["gates"])
        e.tensor_tensor(k.ht_lo[:, c, :], k.ps[:, c % 2, :], k.ht_hi[:, c, :], ALU.subtract).then_inc(s["n_lo"], 1)


def norm_scalar(k, e, i, n):
    s = k.s
    ve, std, r, t, std2, r2, nm2 = k.t4
    gate(e, s["n_var"], i + n, s["gates"])
    e.activation(std, ve, ACT.Sqrt).then_inc(s["n_std"], 1)
    gate(e, s["n_norm"], i + n, s["gates"])
    for u in range(TPC):
        ins = e.activation(k.h[:, u, :], k.x[:, bass.ds(i * TPC + u, 1), :].squeeze(1), ACT.Identity,
                           bias=nm2[:, u:u + 1], scale=r2[:, u:u + 1])
    ins.then_inc(s["n_h"], 1)
    for c in range(KC):
        gate(e, s["n_turned"], nth(i, n, KC, c + 1), s["gates"])
        e.activation(k.ht_hi[:, c, :], k.ps[:, c % 2, :], ACT.Copy).then_inc(s["n_hi"], 1)


def norm_tensor(k, pe, i, n):
    s = k.s
    gate(pe, s["n_h"], i + n, s["gates"])
    for c in range(KC):
        gate(pe, s["n_lo"], nth(i, n, KC, c + 1), s["gates"])
        for u in range(TPC):
            ins = pe.transpose(k.ps[:, c % 2, u * P:(u + 1) * P], k.h[:, u, c * P:(c + 1) * P], k.c["ident"])
        ins.then_inc(s["n_turned"], 1)
    gate(pe, s["n_lo"], nth(i, n, KC, KC + 2), s["gates"])


def pairs_product(pe, out, left, right, n=KC):
    at = 0
    for c in range(n):
        for a, b in ((0, 0), (0, 1), (1, 0)):
            ins = pe.matmul(out, left[a](c), right[b](c), start=(at == 0), stop=(at == 3 * n - 1))
            at += 1
    return ins


def of(ref, cols, block=None):
    return lambda c: ref[:, c, cols]




def b_tensor(k, pe, i):
    s = k.s
    apply_tensor(k, pe, i, 1)
    norm_tensor(k, pe, i, 1)
    ht = (k.ht_hi, k.ht_lo)
    w0 = (k.w0_hi, k.w0_lo)
    for b in range(6):
        gate(pe, s["b_qf"], nth(i, 1, 6, b + 1), s["gates"])
        cols = slice(b * P, (b + 1) * P)
        pairs_product(pe, k.ps[:, 2 + b % 2, :], [of(w, cols) for w in w0], [of(h, slice(0, CH)) for h in ht])\
            .then_inc(s["b_qk_done"], 1)
    for b in range(6):
        gate(pe, s["b_qf"], nth(i, 1, 6, b + 3), s["gates"])
        gate(pe, s["b_rope"], nth(i, 1, 6, b + 1), s["gates"])
        pe.matmul(k.ps[:, 4 + b % 2, :], k.c["rot"], k.qf[:, b, :], start=True, stop=True).then_inc(s["b_rot"], 1)
    for u in range(TPC):
        gate(pe, s["b_v_in"], nth(i, 1, TPC, u + 1), s["gates"])
        cols = slice(u * P, (u + 1) * P)
        pairs_product(pe, k.ps[:, 6 + u % 2, 0:256], [of(h, cols) for h in ht], [of(w, slice(768, 1024)) for w in w0])\
            .then_inc(s["b_v_done"], 1)
    gate(pe, s["b_rope"], nth(i, 1, 6, 8), s["gates"])
    gate(pe, s["b_sq"], i + 1, s["gates"])
    for u in range(TPC):
        bank = k.ps[:, PROJ_BANK[u], :]
        for b in range(6):
            pe.matmul(bank[:, 64 * b:64 * b + 64], k.qr[:, b, u * P:(u + 1) * P], k.rt, start=True, stop=True)
        for b in range(6):
            ins = pe.matmul(bank[:, 384 + 4 * b:388 + 4 * b], k.q2[:, b, u * P:(u + 1) * P], k.c["headcol"],
                            start=True, stop=True)
    ins.then_inc(s["b_proj"], 1)
    gate(pe, s["b_moved"], nth(i, 1, 16, 16), s["gates"])
    for u in range(TPC):
        if u >= 2:
            gate(pe, s["b_ot_lo"], nth(i, 1, TPC, u - 1), s["gates"])
        for c in range(KC):
            ins = pe.transpose(k.ps[:, 2 + u % 2, c * P:(c + 1) * P], k.h[:, u, c * P:(c + 1) * P], k.c["ident"])
        ins.then_inc(s["b_ot"], 1)
        gate(pe, s["b_ot_lo"], nth(i, 1, TPC, u + 1), s["gates"])
        cols = slice(u * P, (u + 1) * P)
        if u >= 2:
            gate(pe, s["b_res"], nth(i, 1, TPC, u - 1), s["gates"])
        pairs_product(pe, k.ps[:, 6 + u % 2, :], [of(o, cols) for o in (k.ot_hi, k.ot_lo)],
                      [of(w, slice(1024, 1536)) for w in w0]).then_inc(s["b_out"], 1)


def b_scalar(k, e, i):
    s = k.s
    apply_scalar(k, e, i, 1)
    norm_scalar(k, e, i, 1)
    for b in range(6):
        gate(e, s["b_qk_done"], nth(i, 1, 6, b + 1), s["gates"])
        e.activation(k.qf[:, b, :], k.ps[:, 2 + b % 2, :], ACT.Identity, bias=k.bqk[:, b:b + 1],
                     scale=1.0 / (W_SCALE * A_SCALE)).then_inc(s["b_qf"], 1)
    for u in range(TPC):
        gate(e, s["b_n2"], nth(i, 1, TPC, u + 1), s["gates"])
        e.activation(k.n2[1], k.n2[0], ACT.Sqrt).then_inc(s["b_n"], 1)
        gate(e, s["b_reduced"], nth(i, 1, TPC, u + 1), s["gates"])
        e.activation(k.feat, k.yr.rearrange("p h a e -> p h (a e)"), ACT.Sin, scale=float(2 * np.pi))\
            .then_inc(s["b_feat"], 1)
    for u in range(TPC):
        gate(e, s["b_ot"], nth(i, 1, TPC, u + 1), s["gates"])
        e.activation(k.ot_hi[:, :, u * P:(u + 1) * P], k.ps[:, 2 + u % 2, :].rearrange("p (c t) -> p c t", c=KC),
                     ACT.Copy).then_inc(s["b_ot_hi"], 1)


def b_pool(k, e, i):
    s = k.s
    gate(e, s["b_rope"], nth(i, 1, 6, 8), s["gates"])
    e.tensor_tensor(k.q2, k.qr, k.qr, ALU.mult).then_inc(s["b_sq"], 1)


PROJ_BANK = (4, 5, 0, 1)


def b_sync(k, sp, i):
    s, scratch = k.s, k.d["heads"]
    for u in range(TPC):
        gate(sp, s["b_o"], nth(i, 1, TPC, u + 1), s["gates"])
        sp.dma_start(scratch.rearrange("h s d -> s h d")[u * P:(u + 1) * P],
                     k.o0[:, u, :].rearrange("p (h d) -> p h d", d=32)).then_inc(s["b_o_out"], 16)
    gate(sp, s["b_o_out"], nth(i, 1, 64, 64), s["gates"])
    rows = scratch.rearrange("h (a b) d -> (h a) (b d)", b=16)
    sp.dma_start(k.h, rows.rearrange("(u p) n -> p u n", p=P)).then_inc(s["b_moved"], 16)
    gate(sp, s["b_moved"], nth(i, 1, 16, 16), s["gates"])


B_STEPS = 6 * 2 + TPC * 13


def b_vector(k, V, i):
    s, e = k.s, V.eng
    apply_vector(k, V, i, 1)
    norm_vector(k, V, i, 1)
    for b in range(6):
        gate(e, s["b_qf"], nth(i, 1, 6, b + 3), s["gates"])
        V.link(e.tensor_tensor(k.qr[:, b, :], k.qf[:, b, :], k.c["cos"], ALU.mult))
        gate(e, s["b_rot"], nth(i, 1, 6, b + 1), s["gates"])
        V.link(e.tensor_tensor(k.qf[:, b, :], k.ps[:, 4 + b % 2, :], k.c["sin"], ALU.mult))
        e.tensor_tensor(k.qr[:, b, :], k.qr[:, b, :], k.qf[:, b, :], ALU.add).then_inc(s["b_rope"], 1)
    for u in range(TPC):
        gate(e, s["b_v_done"], nth(i, 1, TPC, u + 1), s["gates"])
        e.scalar_tensor_tensor(out=k.v0[:, u, :], in0=k.ps[:, 6 + u % 2, 0:256], scalar=1.0 / (W_SCALE * A_SCALE),
                               in1=k.bv, op0=ALU.mult, op1=ALU.add).then_inc(s["b_v_in"], 1)
    gate(e, s["b_proj"], i + 1, s["gates"])
    for u in range(TPC):
        bank = k.ps[:, PROJ_BANK[u], :]
        n2, nn, r, t = k.n2
        e.tensor_scalar(n2, bank[:, 384:408], 1e-12, None, ALU.max).then_inc(s["b_n2"], 1)
        gate(e, s["b_n"], nth(i, 1, TPC, u + 1), s["gates"])
        rsqrt_vector(V, r, nn, n2, t)
        V.link(e.tensor_scalar(r, r, float(1 / (2 * np.pi)), None, ALU.mult))
        e.tensor_tensor(k.yy[:, :, 0, :], bank[:, 0:384].rearrange("p (h e) -> p h e", e=16),
                        bcast(r.unsqueeze(2), [P, 24, 16]), ALU.mult).then_inc(s["b_angle"], 1)
        gate(e, s["b_angle"], nth(i, 1, TPC, u + 1), s["gates"])
        V.link(e.tensor_scalar(k.yy[:, :, 1, :], k.yy[:, :, 0, :], 0.25, None, ALU.add))
        V.link(e.tensor_scalar(k.yr, k.yy, ROUND, ROUND, ALU.add, ALU.subtract))
        e.tensor_tensor(k.yr, k.yy, k.yr, ALU.subtract).then_inc(s["b_reduced"], 1)
        gate(e, s["b_feat"], nth(i, 1, TPC, u + 1), s["gates"])
        prod = k.work.rearrange("p (h g f) -> p h g f", h=16, g=8)
        ss = k.yy.rearrange("p h a e -> p (h a e)")[:, 0:128].rearrange("p (h g) -> p h g", g=8)
        V.link(e.tensor_tensor(prod, bcast(k.feat[:, 0:16, :].unsqueeze(2), [P, 16, 8, 32]),
                               bcast(k.feat[:, 16:24, :].unsqueeze(1), [P, 16, 8, 32]), ALU.mult))
        V.link(e.tensor_reduce(ss, prod, AXX, ALU.add))
        prod = k.work.rearrange("p (h f g) -> p h f g", h=16, g=8)
        V.link(e.tensor_tensor(prod, bcast(ss.unsqueeze(2), [P, 16, 32, 8]),
                               bcast(k.v0[:, u, :].rearrange("p (g f) -> p f g", g=8).unsqueeze(1), [P, 16, 32, 8]),
                               ALU.mult))
        V.link(e.tensor_reduce(k.o0[:, u, :].rearrange("p (h f) -> p h f", h=16), prod, AXX, ALU.add))
        e.tensor_scalar(k.o0[:, u, :], k.o0[:, u, :], 2 * A_SCALE / 32.0, None, ALU.mult).then_inc(s["b_o"], 1)
    for u in range(TPC):
        gate(e, s["b_ot_hi"], nth(i, 1, TPC, u + 1), s["gates"])
        cols = slice(u * P, (u + 1) * P)
        e.tensor_tensor(k.ot_lo[:, :, cols], k.ps[:, 2 + u % 2, :].rearrange("p (c t) -> p c t", c=KC),
                        k.ot_hi[:, :, cols], ALU.subtract).then_inc(s["b_ot_lo"], 1)
        gate(e, s["b_out"], nth(i, 1, TPC, u + 1), s["gates"])
        xt = k.x[:, bass.ds(i * TPC + u, 1), :].squeeze(1)
        e.scalar_tensor_tensor(out=xt, in0=k.ps[:, 6 + u % 2, :], scalar=1.0 / (W_SCALE * A_SCALE), in1=xt,
                               op0=ALU.mult, op1=ALU.add).then_inc(s["b_res"], 1)
        gate(e, s["b_res"], nth(i, 1, TPC, u + 1), s["gates"])
        V.link(e.tensor_tensor(xt, xt, k.bo, ALU.add))




def ffn_tensor(k, pe, i, n):
    s = k.s
    ht = [of(h, slice(0, CH)) for h in (k.ht_hi, k.ht_lo)]
    for f in range(FB):
        gate(pe, s["f_prod"], nth(i, n, FB, f + 1), s["gates"])
        for which, at in ((0, INTER + f * P), (1, f * P)):
            w = [of(x, slice(at, at + P)) for x in (k.wug_hi, k.wug_lo)]
            pairs_product(pe, k.ps[:, 2 + 2 * (f % 2) + which, :], w, ht).then_inc(s["f_up" if which else "f_gate"], 1)
    gate(pe, s["f_lo"], nth(i, n, FB, FB), s["gates"])
    for u in range(TPC):
        gate(pe, s["f_out"], nth(i, n, TPC, u + 1), s["gates"])
        cols = slice(u * P, (u + 1) * P)
        pairs_product(pe, k.ps[:, 6 + u % 2, :], [of(a, cols) for a in (k.act_hi, k.act_lo)],
                      [of(w, slice(0, HID)) for w in (k.wd_hi, k.wd_lo)], FB).then_inc(s["f_down"], 1)


def ffn_scalar(k, e, i, n):
    s = k.s
    for f in range(FB + 1):
        if f < FB:
            gate(e, s["f_gate"], nth(i, n, FB, f + 1), s["gates"])
            if f >= 2:
                gate(e, s["f_prod"], nth(i, n, FB, f + 1), s["gates"])
            e.activation(k.silu[:, f % 2, :], k.ps[:, 2 + 2 * (f % 2), :], ACT.Silu, scale=1.0 / (W_SCALE * A_SCALE))\
                .then_inc(s["f_silu"], 1)
        if f:
            gate(e, s["f_prod"], nth(i, n, FB, f + 2), s["gates"])
            e.activation(k.act_hi[:, f - 1, :], k.prod[:, (f - 1) % 2, :], ACT.Copy).then_inc(s["f_hi"], 1)


def ffn_vector(k, V, i, n):
    s, e = k.s, V.eng
    for f in range(FB + 1):
        if f < FB:
            gate(e, s["f_up"], nth(i, n, FB, f + 1), s["gates"])
            gate(e, s["f_silu"], nth(i, n, FB, f + 1), s["gates"])
            if f >= 2:
                gate(e, s["f_lo"], nth(i, n, FB, f - 1), s["gates"])
            e.scalar_tensor_tensor(out=k.prod[:, f % 2, :], in0=k.ps[:, 3 + 2 * (f % 2), :], scalar=1.0 / W_SCALE,
                                   in1=k.silu[:, f % 2, :], op0=ALU.mult, op1=ALU.mult).then_inc(s["f_prod"], 1)
        if f:
            gate(e, s["f_hi"], nth(i, n, FB, f), s["gates"])
            e.tensor_tensor(k.act_lo[:, f - 1, :], k.prod[:, (f - 1) % 2, :], k.act_hi[:, f - 1, :], ALU.subtract)\
                .then_inc(s["f_lo"], 1)
    for u in range(TPC):
        gate(e, s["f_down"], nth(i, n, TPC, u + 1), s["gates"])
        xt = k.x[:, bass.ds(i * TPC + u, 1), :].squeeze(1)
        e.scalar_tensor_tensor(out=xt, in0=k.ps[:, 6 + u % 2, :], scalar=0.5 / (W_SCALE * A_SCALE), in1=xt,
                               op0=ALU.mult, op1=ALU.add).then_inc(s["f_out"], 1)
    gate(e, s["f_out"], nth(i, n, TPC, TPC + 2), s["gates"])



COMPS = 16
Q_SCALE = 16.0
SCORE = float(32 ** -0.5) / (Q_SCALE * Q_SCALE)
L1_INIT = 0.8 - 0.6 * float(np.exp(-0.3 * 12))


def c_setup_vector(k, V):
    s, e = k.s, V.eng
    V.link(e.tensor_copy(k.causal_ts, k.c["causal"]))
    e.wait_ge(s["c_mask"], 1)
    V.link(e.tensor_copy(k.causal_st, k.ps[:, 7, 0:P]))
    V.link(e.tensor_copy(k.identb, k.c["ident"]))
    V.link(e.tensor_copy(k.sel, bcast(k.c["pick"].unsqueeze(2), [P, 16, P])))
    V.link(e.memset(k.v1, 1.0))
    e.wait_ge(s["c_lam_in"], 80)
    rows = k.o1[:, 0, 0:128].rearrange("p (a d) -> p a d", a=4)
    prod = k.o1[:, 0, 128:192].rearrange("p (a d) -> p a d", a=2)
    V.link(e.tensor_tensor(prod, rows[:, 0:4:2, :], rows[:, 1:4:2, :], ALU.mult))
    e.tensor_reduce(k.lam[:, 0:2], prod, AXX, ALU.add).then_inc(s["c_lam_dot"], 1)
    e.wait_ge(s["c_lam_exp"], 1)
    V.link(e.tensor_tensor(k.lam[:, 4:5], k.lam[:, 2:3], k.lam[:, 3:4], ALU.subtract))
    V.link(e.tensor_scalar(k.lam[:, 4:5], k.lam[:, 4:5], L1_INIT, None, ALU.add))
    e.tensor_scalar(k.g, k.g, (1.0 - L1_INIT) * A_SCALE, None, ALU.mult).then_inc(s["c_set"], 1)
    e.wait_ge(s["c_set"], 1)


def c_tensor(k, pe, i):
    s = k.s
    norm_tensor(k, pe, i, 1 + 2 * NCH)
    ht = (k.ht_hi, k.ht_lo)
    w1 = (k.w1_hi, k.w1_lo)

    def weight(m, cols):
        return [(lambda c, w=w: w[:, m, c, cols]) for w in w1]

    for b in range(8):
        gate(pe, s["c_qk_lo"], nth(i, 1, 8, b + 1), s["gates"])
        pairs_product(pe, k.ps[:, 2 + b % 2, :], weight(b // 4, slice(b % 4 * P, b % 4 * P + P)),
                      [of(h, slice(0, CH)) for h in ht]).then_inc(s["c_qk_done"], 1)
    for u in range(TPC):
        gate(pe, s["c_v_in"], nth(i, 1, TPC, u + 1), s["gates"])
        pairs_product(pe, k.ps[:, 4 + u % 2, :], [of(h, slice(u * P, u * P + P)) for h in ht],
                      weight(2, slice(0, HID))).then_inc(s["c_v_done"], 1)
    gate(pe, s["c_qk_lo"], nth(i, 1, 8, 10), s["gates"])
    gate(pe, s["c_v_in"], nth(i, 1, TPC, 6), s["gates"])
    for a in range(COMPS):
        b, r = a // 4, slice(32 * (a % 4), 32 * (a % 4) + 32)
        if a >= 2:
            gate(pe, s["c_max"], nth(i, 1, 64, TPC * (a - 1)), s["gates"])
        for u in range(TPC):
            g, w = TPC * a + u, (u + 1) * P
            pe.matmul(k.ps[:, g % 8, 0:w], k.qk_hi[r, b, u * P:w], k.qk_hi[r, 4 + b, 0:w], start=True, stop=False)
            pe.matmul(k.ps[:, g % 8, w - P:w], k.identb, k.causal_ts, start=False, stop=True).then_inc(s["c_score"], 1)
    gate(pe, s["c_negmax"], i + 1, s["gates"])
    for u in range(TPC):
        ins = pe.transpose(k.ps[:, 4, u * P:(u + 1) * P], k.nm[:, u].rearrange("p r c -> p (r c)"), k.c["ident"])
    ins.then_inc(s["c_max_turned"], 1)
    gate(pe, s["c_maxt"], i + 1, s["gates"])
    for a in range(COMPS + 1):
        if a < COMPS:
            b, r = a // 4, slice(32 * (a % 4), 32 * (a % 4) + 32)
            for v in range(TPC):
                g = TPC * a + v
                if g >= 4:
                    gate(pe, s["c_exp"], nth(i, 1, 64, g - 3), s["gates"])
                out = k.ps[:, g % 4, v * P:CH]
                keys, queries = slice(v * P, v * P + P), slice(v * P, CH)
                pe.matmul(out, k.sel[r, a, :], k.maxt[r, queries], start=True, stop=False)
                pe.matmul(k.ps[:, g % 4, keys], k.identb, k.causal_st, start=False, stop=False)
                for x, y in ((k.qk_hi, k.qk_hi), (k.qk_hi, k.qk_lo), (k.qk_lo, k.qk_hi)):
                    ins = pe.matmul(out, x[r, 4 + b, keys], y[r, b, queries], start=False, stop=(x is k.qk_lo))
                ins.then_inc(s["c_scored"], 1)
        if a:
            z = a - 1
            gate(pe, s["c_exp"], nth(i, 1, 64, TPC * a), s["gates"])
            if z >= 1:
                gate(pe, s["c_oo"], nth(i, 1, COMPS, z), s["gates"])
            for v in range(TPC):
                ins = pe.matmul(k.ps[0:65, 4, v * P:CH], k.v1[:, v, (z // 2) * 65:(z // 2) * 65 + 65],
                                k.pt[:, z % 2, v, v * P:CH], start=(v == 0), stop=(v == TPC - 1))
            ins.then_inc(s["c_av"], 1)
            gate(pe, s["c_oo"], nth(i, 1, COMPS, z + 1), s["gates"])
            if z % 2 == 0 and z:
                gate(pe, s["c_head"], nth(i, 1, 8, z // 2), s["gates"])
            for u in range(TPC):
                ins = pe.transpose(k.ps[:, 5 + z % 2, 65 * u:65 * u + 65], k.oo[:, z % 2, u * P:(u + 1) * P],
                                   k.c["ident"][0:65, 0:65])
            ins.then_inc(s["c_back"], 1)
    gate(pe, s["c_o"], i + 1, s["gates"])
    for c in range(KC):
        if c >= 2:
            gate(pe, s["c_ot_lo"], nth(i, 1, KC, c - 1), s["gates"])
        for u in range(TPC):
            ins = pe.transpose(k.ps[:, c % 2, u * P:(u + 1) * P], k.o1[:, u, c * P:(c + 1) * P], k.c["ident"])
        ins.then_inc(s["c_ot"], 1)
    gate(pe, s["c_ot_lo"], nth(i, 1, KC, KC), s["gates"])
    for u in range(TPC):
        gate(pe, s["c_out"], nth(i, 1, TPC, u + 1), s["gates"])
        pairs_product(pe, k.ps[:, 2 + u % 2, :], [of(h, slice(u * P, u * P + P)) for h in ht],
                      weight(3, slice(0, HID))).then_inc(s["c_out_done"], 1)


def c_scalar(k, e, i):
    s = k.s
    norm_scalar(k, e, i, 1 + 2 * NCH)
    for b in range(8):
        gate(e, s["c_qk_done"], nth(i, 1, 8, b + 1), s["gates"])
        e.activation(k.qk_hi[:, b, :], k.ps[:, 2 + b % 2, :], ACT.Copy, scale=Q_SCALE / (W_SCALE * A_SCALE))\
            .then_inc(s["c_qk_hi"], 1)
    gate(e, s["c_max_turned"], i + 1, s["gates"])
    e.activation(k.maxt, k.ps[:, 4, :], ACT.Copy).then_inc(s["c_maxt"], 1)
    for a in range(COMPS):
        if a >= 2:
            gate(e, s["c_av"], nth(i, 1, COMPS, a - 1), s["gates"])
        for v in range(TPC):
            g = TPC * a + v
            gate(e, s["c_scored"], nth(i, 1, 64, g + 1), s["gates"])
            e.activation(k.pt[:, a % 2, v, v * P:CH], k.ps[:, g % 4, v * P:CH], ACT.Exp, scale=SCORE)\
                .then_inc(s["c_exp"], 1)
    gate(e, s["c_ms"], i + 1, s["gates"])
    e.activation(k.rms, k.mx2, ACT.Sqrt).then_inc(s["c_rms"], 1)
    for c in range(KC):
        gate(e, s["c_ot"], nth(i, 1, KC, c + 1), s["gates"])
        e.activation(k.ht_hi[:, c, :], k.ps[:, c % 2, :], ACT.Copy).then_inc(s["c_ot_hi"], 1)


C_STEPS = 2 + 8 * 4 + 9


def c_vector(k, V, i):
    s, e = k.s, V.eng
    norm_vector(k, V, i, 1 + 2 * NCH)
    for b in range(8):
        gate(e, s["c_qk_hi"], nth(i, 1, 8, b + 1), s["gates"])
        e.scalar_tensor_tensor(out=k.qk_lo[:, b, :], in0=k.ps[:, 2 + b % 2, :], scalar=Q_SCALE / (W_SCALE * A_SCALE),
                               in1=k.qk_hi[:, b, :], op0=ALU.mult, op1=ALU.subtract).then_inc(s["c_qk_lo"], 1)
    for u in range(TPC):
        gate(e, s["c_v_done"], nth(i, 1, TPC, u + 1), s["gates"])
        e.tensor_scalar(k.v1[:, u, :].rearrange("p (h d) -> p h d", d=65)[:, :, 0:64],
                        k.ps[:, 4 + u % 2, :].rearrange("p (h d) -> p h d", d=64),
                        1.0 / (W_SCALE * A_SCALE), None, ALU.mult).then_inc(s["c_v_in"], 1)
    for g in range(4 * COMPS):
        a, u = g // 4, g % 4
        gate(e, s["c_score"], nth(i, 1, 64, g + 1), s["gates"])
        e.tensor_reduce(k.mx[:, u, a:a + 1], k.ps[:, g % 8, 0:(u + 1) * P], AXX, ALU.max).then_inc(s["c_max"], 1)
    gate(e, s["c_max"], nth(i, 1, 64, 64), s["gates"])
    V.link(e.tensor_scalar(k.nmb, k.mx, -1.0, None, ALU.mult))
    V.link(e.tensor_tensor(k.mx, k.mx, k.nmb, ALU.add))
    for q in range(4):
        e.tensor_copy(k.nm[:, :, q, 0:16], k.nmb)
        ins = e.tensor_scalar(k.nm[:, :, q, 16:32], k.mx, -1.0, None, ALU.mult)
    ins.then_inc(s["c_negmax"], 1)
    for z in range(COMPS):
        gate(e, s["c_av"], nth(i, 1, COMPS, z + 1), s["gates"])
        if z >= 2:
            gate(e, s["c_back"], nth(i, 1, COMPS, z - 1), s["gates"])
        e.tensor_copy(k.oo[:, z % 2, :], k.ps[0:65, 4, :]).then_inc(s["c_oo"], 1)
        if z % 2:
            gate(e, s["c_back"], nth(i, 1, COMPS, z + 1), s["gates"])
            o = [k.ps[:, 5 + q, 0:260].rearrange("p (u d) -> p u d", d=65) for q in range(2)]
            cols = slice(z // 2 * 64, z // 2 * 64 + 64)
            r = k.rs
            for q in range(2):
                ins = e.reciprocal(r[:, q, :], o[q][:, :, 64])
            V.link(ins)
            V.link(e.tensor_scalar(r[:, 1, :], r[:, 1, :], k.lam[:, 4:5], None, ALU.mult))
            V.link(e.tensor_tensor(k.o1[:, :, cols], o[0][:, :, 0:64], bcast(r[:, 0, :].unsqueeze(2), [P, TPC, 64]),
                                   ALU.mult))
            V.link(e.tensor_tensor(k.h[:, :, cols], o[1][:, :, 0:64], bcast(r[:, 1, :].unsqueeze(2), [P, TPC, 64]),
                                   ALU.mult))
            e.tensor_tensor(k.o1[:, :, cols], k.o1[:, :, cols], k.h[:, :, cols], ALU.subtract)\
                .then_inc(s["c_head"], 1)
    gate(e, s["c_head"], nth(i, 1, 8, 8), s["gates"])
    V.link(e.tensor_tensor(k.h, k.o1, k.o1, ALU.mult))
    V.link(e.tensor_reduce(k.mx2, k.h.rearrange("p u (h d) -> p (u h) d", d=64), AXX, ALU.add))
    e.tensor_scalar(k.mx2, k.mx2, 1.0 / 64, 1e-5, ALU.mult, ALU.add).then_inc(s["c_ms"], 1)
    gate(e, s["c_rms"], i + 1, s["gates"])
    rsqrt_vector(V, k.rr, k.rms, k.mx2, k.rr2)
    heads = k.o1.rearrange("p u (h d) -> p (u h) d", d=64)
    V.link(e.tensor_tensor(heads, heads, bcast(k.rr.unsqueeze(2), [P, 32, 64]), ALU.mult))
    V.link(e.tensor_tensor(heads, heads, bcast(k.g.unsqueeze(1), [P, 32, 64]), ALU.mult))
    e.sem_inc(s["c_o"], 1)
    for c in range(KC):
        gate(e, s["c_ot_hi"], nth(i, 1, KC, c + 1), s["gates"])
        e.tensor_tensor(k.ht_lo[:, c, :], k.ps[:, c % 2, :], k.ht_hi[:, c, :], ALU.subtract).then_inc(s["c_ot_lo"], 1)
    for u in range(TPC):
        gate(e, s["c_out_done"], nth(i, 1, TPC, u + 1), s["gates"])
        xt = k.x[:, bass.ds(i * TPC + u, 1), :].squeeze(1)
        e.scalar_tensor_tensor(out=xt, in0=k.ps[:, 2 + u % 2, :], scalar=1.0 / (W_SCALE * A_SCALE), in1=xt,
                               op0=ALU.mult, op1=ALU.add).then_inc(s["c_out"], 1)
    gate(e, s["c_out"], nth(i, 1, TPC, 6), s["gates"])


def bass_macaron(nc, d):
    with ExitStack() as ctx:
        ctx.enter_context(nc.allow_non_contiguous_dma(reason="a few short vectors laid along the partitions"))
        k = Kernel()
        k.d = d
        place(k, nc, ctx)
        k.ps = ctx.enter_context(nc.psum_tensor("ps", [P, 8, 512], F32))
        k.s = {n: ctx.enter_context(nc.semaphore(n)) for n in SEMAPHORES}
        k.ones, k.diag = k.rows[0:NTILE, 3, 0:P], k.rows[0:NTILE, 0, :]
        k.wdt_hi = k.wt_hi.rearrange("p c (b m) -> p (c b) m", m=P)
        k.wdt_lo = k.wt_lo.rearrange("p c (b m) -> p (c b) m", m=P)
        pairs = k.nat.rearrange("p a b -> p (a b)").bitcast(F16).rearrange("p (n c m) -> p n c m", n=4, m=P)
        k.wdo_hi, k.wdo_lo = [pairs[:, 0], pairs[:, 1]], [pairs[:, 2], pairs[:, 3]]
        s = k.s
        block = ctx.enter_context(nc.Block())

        def load_down(sp):
            for dst, src in ((k.wd_hi, d["wd_hi"]), (k.wd_lo, d["wd_lo"])):
                sp.dma_start(dst, src).then_inc(s["down_in"], 16)

        @block.sync
        def _(sp):
            setup_sync(k, sp)
            sp.wait_ge(s["wdo_out0"], 64)
            sp.wait_ge(s["wdo_out1"], 64)
            sp.wait_ge(s["w1_out"], 128)
            sp.wait_ge(s["rt_zeroed"], 1)
            for j in range(4):
                sp.dma_start(k.rt[32 * j:32 * j + 32, 16 * j:16 * j + 16],
                             d["L0_attn_rand_matrix"].rearrange("e d -> d e")).then_inc(s["b_in"], 16)
            sp.dma_start(k.bv, d["L0_attn_bv"].partition_broadcast(P)).then_inc(s["b_in"], 16)
            sp.dma_start(k.bo, d["L0_attn_bo"].partition_broadcast(P)).then_inc(s["b_in"], 16)
            with sp.Fori(0, NCH) as i:
                b_sync(k, sp, i)
            sp.wait_ge(s["table_ready"], 2)
            load_down(sp)
            sp.wait_ge(s["f_out"], 2 + NT)
            for m in range(4):
                sp.dma_start(k.w1_hi[:, m], d["w1_hi"][m]).then_inc(s["c_in"], 16)
                sp.dma_start(k.w1_lo[:, m], d["w1_lo"][m]).then_inc(s["c_in"], 16)
            for m, name in enumerate(["lambda_q1", "lambda_k1", "lambda_q2", "lambda_k2"]):
                sp.dma_start(k.o1[:, 0, 32 * m:32 * m + 32], d["L1_attn_" + name].partition_broadcast(P))\
                    .then_inc(s["c_lam_in"], 16)
            sp.dma_start(k.g, d["L1_attn_g"].partition_broadcast(P)).then_inc(s["c_lam_in"], 16)
            sp.wait_ge(s["c_out"], 2 + NT)
            load_down(sp)
            for c in range(NCH):
                sp.wait_ge(s["f_out"], 2 + NT + TPC * (c + 1))
                sp.dma_start(d["out"][c].rearrange("(u p) n -> p u n", p=P),
                             k.x[:, c * TPC:(c + 1) * TPC, :]).then_inc(s["x_out"], 16)
            sp.wait_ge(s["x_out"], 16 * NCH)

        @block.gpsimd
        def _(pool):
            setup_pool(k, pool)
            with pool.Fori(0, NCH) as i:
                b_pool(k, pool, i)

        @block.tensor
        def _(pe):
            use_work(k, k.work, k.h)
            setup_tensor(k, pe)
            minmax_tensor(k, pe, 1, "")
            pe.wait_ge(s["b_in"], 96)
            with pe.Fori(0, NCH) as i:
                b_tensor(k, pe, i)
            minmax_tensor(k, pe, 2, "")
            use_work(k, k.work1, k.h)
            pe.wait_ge(s["down_in"], 32)
            with pe.Fori(0, NCH) as i:
                apply_tensor(k, pe, i, 1 + NCH)
                norm_tensor(k, pe, i, 1 + NCH)
                ffn_tensor(k, pe, i, 1)
            pe.wait_ge(s["f_out"], 2 + NT)
            pe.transpose(k.ps[:, 7, 0:P], k.c["causal"], k.c["ident"]).then_inc(s["c_mask"], 1)
            pe.wait_ge(s["c_in"], 128)
            pe.wait_ge(s["c_set"], 1)
            with pe.Fori(0, NCH) as i:
                c_tensor(k, pe, i)
            pe.wait_ge(s["down_in"], 64)
            with pe.Fori(0, NCH) as i:
                norm_tensor(k, pe, i, 1 + 3 * NCH)
                ffn_tensor(k, pe, i, 1 + NCH)

        @block.scalar
        def _(act):
            use_work(k, k.work, k.h)
            setup_scalar(k, act)
            first_scalar(k, act, 1, "")
            with act.Fori(0, NCH) as i:
                b_scalar(k, act, i)
                token_stats_scalar(k, act, i, 1 + NCH, "")
            use_work(k, k.work1, k.h)
            with act.Fori(0, NCH) as i:
                apply_scalar(k, act, i, 1 + NCH)
                norm_scalar(k, act, i, 1 + NCH)
                ffn_scalar(k, act, i, 1)
            act.wait_ge(s["c_lam_dot"], 1)
            act.activation(k.lam[:, 2:4], k.lam[:, 0:2], ACT.Exp).then_inc(s["c_lam_exp"], 1)
            with act.Fori(0, NCH) as i:
                c_scalar(k, act, i)
            with act.Fori(0, NCH) as i:
                norm_scalar(k, act, i, 1 + 3 * NCH)
                ffn_scalar(k, act, i, 1 + NCH)

        @block.vector
        def _(dve):
            use_work(k, k.work, k.h)
            V = Steps(dve, s["v_step"], s["gates"])
            for name in ("n_lo", "b_qf", "b_rope", "b_v_in", "f_prod", "f_out", "c_qk_lo", "c_v_in", "c_out"):
                dve.sem_inc(s[name], 2)
            setup_vector_first(k, V)
            setup_vector_rest(k, V)
            first_vector(k, V, 1, "")
            minmax_vector(k, V, 1, "")
            V.link(dve.memset(k.acc, -BIG))
            dve.wait_ge(s["b_in"], 96)
            with dve.Fori(0, NCH) as i:
                V.enter(i, APPLY_STEPS + NORM_STEPS + B_STEPS + STATS_STEPS + ROUTE_STEPS)
                b_vector(k, V, i)
                token_stats_vector(k, V, i, 1 + NCH, "")
                routing_vector(k, V, i, 1 + NCH, "")
            V.leave(NCH)
            minmax_vector(k, V, 2, "")
            use_work(k, k.work1, k.h)
            with dve.Fori(0, NCH) as i:
                V.enter(i, APPLY_STEPS + NORM_STEPS)
                apply_vector(k, V, i, 1 + NCH)
                norm_vector(k, V, i, 1 + NCH)
                ffn_vector(k, V, i, 1)
            V.leave(NCH)
            c_setup_vector(k, V)
            with dve.Fori(0, NCH) as i:
                V.enter(i, NORM_STEPS + C_STEPS)
                c_vector(k, V, i)
            V.leave(NCH)
            with dve.Fori(0, NCH) as i:
                V.enter(i, NORM_STEPS)
                norm_vector(k, V, i, 1 + 3 * NCH)
                ffn_vector(k, V, i, 1 + NCH)
            V.leave(NCH)


_INS = ["L0_attn_hidden_states", "L0_attn_Wq", "L0_attn_bq", "L0_attn_Wk", "L0_attn_bk", "L0_attn_Wv",
        "L0_attn_bv", "L0_attn_Wo", "L0_attn_bo", "L0_attn_rand_matrix", "L0_ffn_ln_gamma", "L0_ffn_ln_beta",
        "L0_ffn_spline_bases", "L0_ffn_spline_slopes", "L0_ffn_output_scale", "L1_attn_Wq", "L1_attn_Wk",
        "L1_attn_Wv", "L1_attn_Wo", "L1_attn_lambda_q1", "L1_attn_lambda_k1", "L1_attn_lambda_q2",
        "L1_attn_lambda_k2", "L1_attn_g", "L1_ffn_SU_ug", "L1_ffn_SU_dp", "L1_ffn_Wscale_ug",
        "L1_ffn_Wscale_dp", "L1_ffn_W_up", "L1_ffn_W_gate", "L1_ffn_W_down"]


def kernel(**inputs):
    import numpy as _np
    import concourse.bacc as _bacc
    from concourse import mybir as _mybir
    from concourse.bass_utils import run_bass_kernel_spmd as _run

    nc = _bacc.Bacc("TRN2", target_bir_lowering=False, num_devices=1, dynamic_dma_scratch_size=1024)
    arrays, d = {}, {}
    for name in _INS:
        a = _np.ascontiguousarray(inputs[name])
        arrays[f"in_{name}_dram"] = a
        d[name] = nc.dram_tensor(f"in_{name}_dram", a.shape, _mybir.dt.from_np(a.dtype), kind="ExternalInput").ap()
    arrays["constants_dram"] = CONSTS
    d["constants"] = nc.dram_tensor("constants_dram", CONSTS.shape, F32, kind="ExternalInput").ap()
    for part in ("hi", "lo"):
        d["wd_" + part] = nc.dram_tensor(f"wd_{part}_dram", (P, FB, HID), F16).ap()
        d["w1_" + part] = nc.dram_tensor(f"w1_{part}_dram", (4, P, KC, HID), F16).ap()
    d["heads"] = nc.dram_tensor("heads_dram", (16, CH, 32), F32).ap()
    d["out"] = nc.dram_tensor("out_dram", (4, 512, 512), F32, kind="ExternalOutput").ap()
    bass_macaron(nc, d)
    r = _run(nc, [arrays], core_ids=[0])
    return r.results[0]["out_dram"]
```

```python
from contextlib import ExitStack

import numpy as np
import concourse.bass as bass
from concourse import mybir

ALU = mybir.AluOpType
ACT = mybir.ActivationFunctionType
AXX = mybir.AxisListType.X
F32 = mybir.dt.float32
F16 = mybir.dt.float16
BF16 = mybir.dt.bfloat16

P = 128
HID = 512
KC = HID // P
NTOK = 2048
NT = NTOK // P
CH = 512
NCH = NTOK // CH
TPC = CH // P
INTER = 2048
FB = INTER // P
NTILE, DSL, GRID = 64, 8, 16
CLUS = 8
LN_EPS = 1e-5
ARENA = 228096
W_SCALE = 1024.0
A_SCALE = 64.0
ROUND = float(1.5 * 2 ** 23)
BIG = 1.0e30


def host_constants():
    r = np.arange(P)
    ident = np.eye(P, dtype=np.float32)
    had = np.array([[1.0 - 2.0 * (bin(a & b).count("1") & 1) for b in range(P)] for a in range(P)], np.float32)
    rot = np.zeros((P, P), np.float32)
    for m in range(P):
        if m % 32 < 16:
            rot[m + 16, m] = -1.0
        else:
            rot[m - 16, m] = 1.0
    inv = (1.0 / (np.float32(10000.0) ** (np.arange(0, 32, 2, dtype=np.float32) / np.float32(32)))).astype(np.float32)
    ang = (np.arange(CH, dtype=np.float32)[None, :] * inv[(r % 16)][:, None]).astype(np.float32)
    t = np.arange(NTILE)
    key = np.broadcast_to(((7 - t // 8) * 256 + (7 - t % 8)).astype(np.float32), (P, NTILE))
    iota = np.broadcast_to(np.arange(GRID, dtype=np.float32), (P, GRID))
    causal = np.where(r[None, :] > r[:, None], np.float32(-1e30), np.float32(0.0)).astype(np.float32)
    pick = (r[:, None] % 16 == np.arange(16)[None, :]).astype(np.float32)
    headpad = (r[:, None] // 32 + 20 == np.arange(44)[None, :]).astype(np.float32)
    same = (r[:, None] // 8 == np.arange(16)[None, :]).astype(np.float32)
    phase = np.where(r % 32 < 16, np.float32(0.0), np.float32(0.25)).astype(np.float32)[:, None]
    phase2pi = (phase * np.float32(2 * np.pi)).astype(np.float32)
    parts = [("ident", ident), ("had", had), ("rot", rot), ("cos", np.cos(ang)),
             ("sin", np.sin(ang)), ("key", key), ("iota", iota), ("causal", causal),
             ("pick", pick), ("headpad", headpad), ("same", same), ("phase", phase),
             ("phase2pi", phase2pi)]
    where, at = {}, 0
    for name, a in parts:
        where[name] = (at, at + a.shape[1])
        at += a.shape[1]
    return np.ascontiguousarray(np.concatenate([a for _, a in parts], axis=1).astype(np.float32)), where


CONSTS, CONST_AT = host_constants()

SEMAPHORES = """
const_in x_in param_in ones_set gates
nat_in0 nat_in1 nat_scaled nat_turned turned wt_hi wt_lo had_done had_hi had_lo
wd_in wd_scaled wd_mixed wd_step wdt_turned wdt_hi wdt_lo wdh_done wdo_hi wdo_lo wdo_out0 wdo_out1
w1_in w1_scaled w1_hi w1_lo w1_out
ssum_ready ss_signed ss_diag ss_spread ss_row up_scale
v_step
var1 std1 var2 std2 norm z_scaled y_ready y_signed routed
minmax_turned table_ready rt_zeroed b_in down_in
ap_oh ap_turned ap_oht ap_rows
n_var n_std n_norm n_h n_turned n_hi n_lo
b_v_done b_v_in b_v_out b_vr b_qk_done b_qf b_cos b_rot b_rope b_sq b_nsum b_n2 b_n b_r b_p b_spread b_y b_whole
b_reduced b_feat b_f_hi b_f_lo b_ks b_ksg b_qs b_s b_mask b_pv b_ot_hi b_ot_lo b_out b_res
f_gate f_up f_silu f_prod f_hi f_lo f_down f_out
c_in c_lam_in c_lam_dot c_lam_exp c_mask c_set c_qk_done c_qk_hi c_qk_lo c_v_done c_v_in c_score c_max c_negmax
c_max_turned c_maxt c_scored c_exp c_av c_oo c_back c_head c_ms c_rms c_o c_ot c_ot_hi c_ot_lo c_out_done c_out
x_out
""".split()


class Views:

    def __init__(self, arena):
        self.arena = arena

    def at(self, byte, shape, dt):
        size = 1
        for n in shape[1:]:
            size *= n
        width = 4 if dt == F32 else 2
        words = size * width // 4
        assert byte % 4 == 0 and size * width % 4 == 0
        v = self.arena[0:shape[0], byte // 4:byte // 4 + words]
        if dt != F32:
            v = v.bitcast(dt)
        if len(shape) == 3:
            v = v.rearrange("p (a b) -> p a b", a=shape[1])
        if len(shape) == 5:
            v = v.rearrange("p (a b c d) -> p a b c d", a=shape[1], b=shape[2], c=shape[3])
        if len(shape) == 4:
            v = v.rearrange("p (a b c) -> p a b c", a=shape[1], b=shape[2])
        return v, byte + size * width


class Steps:

    def __init__(self, eng, sem, gates):
        self.eng, self.sem, self.gates = eng, sem, gates
        self.base, self.i, self.per, self.k = 0, 0, 0, 0

    def enter(self, i, per):
        self.i, self.per, self.k = i, per, 0

    def leave(self, n):
        assert self.k == self.per, (self.k, self.per)
        self.base, self.i, self.per, self.k = self.base + n * self.per, 0, 0, 0

    def link(self, ins):
        self.k += 1
        ins.then_inc(self.sem, 1)
        value = self.base + self.i * self.per + self.k if self.per else self.base + self.k
        if not self.per:
            self.base, self.k = self.base + self.k, 0
        gate(self.eng, self.sem, value, self.gates)


def gate(eng, sem, value, gates):
    eng.wait_ge(sem, value)
    if not isinstance(value, int):
        eng.sem_inc(gates, 1)


def phase_buffers(k, v):
    at = k.free_at
    k.h, at = v.at(at, [P, TPC, HID], F32)
    k.ht_hi, at = v.at(at, [P, KC, CH], F16)
    k.ht_lo, at = v.at(at, [P, KC, CH], F16)
    a = at
    k.work, _ = v.at(a, [P, 4096], F32)
    k.f_hi, b = v.at(a, [P, 6, CH], F16)
    k.f_lo, b = v.at(b, [P, 6, CH], F16)
    k.qf, a = v.at(a, [P, 6, CH], F32)
    k.qs, _ = v.at(a, [P, 16, CH], F16)
    k.qr, a = v.at(a, [P, 6, CH], F32)
    k.q2, a = v.at(a, [P, 2, CH], F32)
    k.ks, a = v.at(a, [P, 8, CH], F16)
    k.ksg, _ = v.at(a, [P, 32, P], F16)
    k.ang, a = v.at(a, [P, 2, CH], F32)
    k.turns, a = v.at(a, [P, 2, CH], F32)
    k.nr, a = v.at(a, [P, 4, CH], F32)
    k.sm, a = v.at(a, [P, 2, 2, 16, 16], F32)
    k.spread, a = v.at(a, [24, 6 * P], F32)
    k.bv, a = v.at(a, [P, 256], F32)
    k.bo, a = v.at(a, [P, HID], F32)
    assert a <= ARENA, a
    k.v0, b = v.at(k.free_at, [P, TPC, 256], F32)
    k.vr, b = v.at(b, [P, 32, 32], F32)
    a = at
    k.wd_hi, a = v.at(a, [P, FB, HID], F16)
    k.wd_lo, a = v.at(a, [P, FB, HID], F16)
    k.act_hi, a = v.at(a, [P, FB, CH], F16)
    k.act_lo, a = v.at(a, [P, FB, CH], F16)
    assert a <= ARENA, a
    b = k.w0_at
    k.silu, b = v.at(b, [P, 2, CH], F32)
    k.prod, b = v.at(b, [P, 2, CH], F32)
    k.work1, b = v.at(b, [P, 4096], F32)
    assert b <= k.free_at
    a = at
    k.w1_hi, a = v.at(a, [P, 4, KC, HID], F16)
    k.w1_lo, a = v.at(a, [P, 4, KC, HID], F16)
    k.qk_hi, a = v.at(a, [P, 8, CH], F16)
    k.qk_lo, a = v.at(a, [P, 8, CH], F16)
    k.v1, a = v.at(a, [P, TPC, 8 * 65], F32)
    k.o1, a = v.at(a, [P, TPC, HID], F32)
    assert a <= ARENA, a
    b = k.w0_at
    k.pt, b = v.at(b, [P, 2, TPC, CH], F32)
    k.nm, _ = v.at(b, [P, TPC, 4, 32], F32)
    k.oo, b = v.at(b, [65, 2, CH], F32)
    k.sel, b = v.at(b, [P, 16, P], BF16)
    assert b <= k.free_at
    b = k.onehot_at
    k.maxt, b = v.at(b, [P, CH], BF16)
    k.causal_ts, b = v.at(b, [P, P], BF16)
    k.causal_st, b = v.at(b, [P, P], BF16)
    k.identb, b = v.at(b, [P, P], BF16)
    k.nmb, b = v.at(b, [P, TPC, 16], BF16)
    k.mx, b = v.at(b, [P, TPC, 16], F32)
    k.g, b = v.at(b, [P, 64], F32)
    assert b <= k.onehot_at + 4096


def use_work(k, work, y):
    k.y = y
    k.masked = work[:, 0:2048].rearrange("p (u c) -> p u c", u=TPC)
    k.sg = work[:, 2048:3072].bitcast(BF16).rearrange("p (u c) -> p u c", u=TPC)
    k.scat = k.masked
    k.m16 = work[:, 2048:2560].rearrange("p (u j g) -> p u j g", u=TPC, j=DSL)
    k.m16p = work[:, 2560:3072].rearrange("p (u j g) -> p u j g", u=TPC, j=DSL)
    k.oh4 = work[:, 3072:3328].rearrange("p (u t) -> p u t", u=TPC)
    k.oht = work[0:NTILE, 3584:4096]


class Kernel:
    pass


def bcast(ap, shape):
    return ap.to_broadcast(shape)


def place(k, nc, ctx):
    arena = ctx.enter_context(nc.sbuf_tensor("arena", [P, ARENA // 4], F32))
    v = Views(arena)
    at = 0
    k.x, at = v.at(at, [P, NT, HID], F32)
    k.const, at = v.at(at, [P, CONSTS.shape[1]], F32)
    k.onehot_at = at
    k.onehot, at = v.at(at, [P, NT, NTILE], F32)
    k.sliced, at = v.at(at, [P, NT, DSL], F32)
    k.mr, at = v.at(at, [P, NT, 2], F32)
    k.gamma, at = v.at(at, [P, HID], F32)
    k.beta, at = v.at(at, [P, HID], F32)
    k.ssrow, at = v.at(at, [P, HID], BF16)
    k.table, at = v.at(at, [NTILE, 260], F32)
    k.small, at = v.at(at, [P, 704], F32)
    k.rt, at = v.at(at, [P, P], F32)
    k.signs, at = v.at(at, [P, 2, P], F16)
    k.wug_hi, at = v.at(at, [P, KC, 2 * INTER], F16)
    k.wug_lo, at = v.at(at, [P, KC, 2 * INTER], F16)
    k.w0_at = at
    k.w0_hi, at = v.at(at, [P, KC, 1536], F16)
    k.w0_lo, at = v.at(at, [P, KC, 1536], F16)
    k.free_at = at
    k.views = v
    c = {n: k.const[:, a:b] for n, (a, b) in CONST_AT.items()}
    k.c = c
    a = k.free_at
    k.wd_nat, a = v.at(a, [P, 4, INTER], F32)
    k.wd_tmp, a = v.at(a, [P, INTER], F32)
    k.nat, a = v.at(a, [P, 8, HID], F32)
    k.wt_hi, a = v.at(a, [P, KC, HID], F16)
    k.wt_lo, a = v.at(a, [P, KC, HID], F16)
    k.rows, a = v.at(a, [P, TPC, HID], F32)
    assert a <= ARENA, a
    s = k.small
    phase_buffers(k, v)
    k.stats6 = s[:, 0:24].rearrange("p (u c) -> p u c", c=6)
    k.mv = s[:, 24:32].rearrange("p (u c) -> p u c", c=2)
    k.t4 = [s[:, 32 + 4 * n:36 + 4 * n] for n in range(7)]
    k.clus = s[:, 60:92].rearrange("p (u c) -> p u c", c=CLUS)
    k.kmax = s[:, 92:96]
    k.ends = s[:, 96:104].rearrange("p (u a) -> p u a", a=2)
    k.acc = s[:, 104:232].rearrange("p (a t) -> p a t", a=2)
    k.wscale = s[:, 232:264]
    k.su_ug = s[:, 264:268]
    k.su_dp = s[:, 268:284]
    k.wscale_dp = s[:, 284:288]
    k.ssum = s[0:NTILE, 288:296]
    k.ssign = s[0:NTILE, 296:304]
    k.ends2 = s[0:NTILE, 304:306]
    k.bqk = s[:, 306:312]
    k.mr4 = s[:, 312:320].rearrange("p (u c) -> p u c", c=2)
    k.ap = [s[:, 320 + 32 * m:352 + 32 * m].rearrange("p (u j) -> p u j", j=DSL) for m in range(6)]
    k.cols = s[:, 512:524].rearrange("p (u c) -> p u c", c=3)
    k.n2 = [s[:, 524 + 24 * m:548 + 24 * m] for m in range(4)]
    k.lam = s[:, 620:628]
    k.rs = s[:, 628:636].rearrange("p (m u) -> p m u", m=2)
    k.mx2, k.rr, k.rr2, k.rms = [s[:, 320 + 32 * m:352 + 32 * m] for m in range(4)]
    k.had16 = k.signs[:, 0, :]
    k.had16n = k.signs[:, 1, :]
    return k


def rsqrt_vector(V, r, std, var, t):
    e = V.eng
    V.link(e.reciprocal(r, std))
    V.link(e.tensor_tensor(t, var, r, ALU.mult))
    V.link(e.tensor_tensor(t, t, r, ALU.mult))
    V.link(e.tensor_scalar(t, t, -0.5, 1.5, ALU.mult, ALU.add))
    V.link(e.tensor_tensor(r, r, t, ALU.mult))


def nth(i, n, per, at):
    return i * per + ((n - 1) * per + at)


def token_stats_vector(k, V, i, n, p):
    s, e = k.s, V.eng
    for u in range(TPC):
        ins = e.bn_stats(k.stats6[:, u, :], k.x[:, bass.ds(i * TPC + u, 1), :].squeeze(1))
    V.link(ins)
    for u in range(TPC):
        ins = e.bn_aggr(k.mv[:, u, :], k.stats6[:, u, :])
    V.link(ins)
    ve, std, r, t, std2, r2, nm2 = k.t4
    mean, var = k.mv[:, :, 0], k.mv[:, :, 1]
    e.tensor_scalar(ve, var, LN_EPS, None, ALU.add).then_inc(s[p + "var1"], 1)
    gate(e, s[p + "std1"], i + n, s["gates"])
    rsqrt_vector(V, r, std, ve, t)
    V.link(e.tensor_tensor(t, var, r, ALU.mult))
    V.link(e.tensor_tensor(t, t, r, ALU.mult))
    e.tensor_scalar(ve, t, LN_EPS, None, ALU.add).then_inc(s[p + "var2"], 1)
    gate(e, s[p + "std2"], i + n, s["gates"])
    rsqrt_vector(V, r2, std2, ve, t)
    V.link(e.tensor_tensor(r2, r2, r, ALU.mult))
    mr = k.mr[:, bass.ds(i * TPC, TPC), :]
    V.link(e.tensor_copy(mr[:, :, 0], mean))
    V.link(e.tensor_copy(mr[:, :, 1], r))
    e.scalar_tensor_tensor(out=nm2, in0=mean, scalar=-1.0, in1=r2, op0=ALU.mult, op1=ALU.mult)\
        .then_inc(s[p + "norm"], 1)


def token_stats_scalar(k, e, i, n, p):
    s = k.s
    ve, std, r, t, std2, r2, nm2 = k.t4
    gate(e, s[p + "var1"], i + n, s["gates"])
    e.activation(std, ve, ACT.Sqrt).then_inc(s[p + "std1"], 1)
    gate(e, s[p + "var2"], i + n, s["gates"])
    e.activation(std2, ve, ACT.Sqrt).then_inc(s[p + "std2"], 1)
    gate(e, s[p + "norm"], i + n, s["gates"])
    for u in range(TPC):
        ins = e.activation(k.y[:, u, :], k.x[:, bass.ds(i * TPC + u, 1), :].squeeze(1), ACT.Identity,
                           bias=nm2[:, u:u + 1], scale=r2[:, u:u + 1])
    ins.then_inc(s[p + "z_scaled"], 1)
    gate(e, s[p + "y_ready"], i + n, s["gates"])
    e.activation(k.sg, k.y, ACT.Sign).then_inc(s[p + "y_signed"], 1)


def routing_vector(k, V, i, n, p):
    s, e = k.s, V.eng
    full, tiles = [P, TPC, HID], [P, TPC, NTILE]
    gate(e, s[p + "z_scaled"], i + n, s["gates"])
    V.link(e.tensor_tensor(k.y, k.y, bcast(k.gamma.unsqueeze(1), full), ALU.mult))
    e.tensor_tensor(k.y, k.y, bcast(k.beta.unsqueeze(1), full), ALU.add).then_inc(s[p + "y_ready"], 1)
    gate(e, s[p + "y_signed"], i + n, s["gates"])
    V.link(e.tensor_tensor(k.sg, k.sg, bcast(k.ssrow.unsqueeze(1), full), ALU.mult))
    score = k.masked[:, 0, 0:256].rearrange("p (u t) -> p u t", u=TPC)
    key = k.masked[:, 1, 0:256].rearrange("p (u t) -> p u t", u=TPC)
    V.link(e.tensor_reduce(score, k.sg.rearrange("p u (t j) -> p u t j", j=DSL), AXX, ALU.add))
    V.link(e.tensor_reduce(k.clus, score.rearrange("p u (c t) -> p u c t", c=CLUS), AXX, ALU.add))
    V.link(e.scalar_tensor_tensor(out=key, in0=score, scalar=8.0, in1=bcast(k.c["key"].unsqueeze(1), tiles),
                                  op0=ALU.mult, op1=ALU.add))
    for u in range(TPC):
        ins = e.scalar_tensor_tensor(
            out=key[:, u, :].rearrange("p (c t) -> p c t", c=CLUS),
            in0=bcast(k.clus[:, u, :].unsqueeze(2), [P, CLUS, 8]), scalar=2048.0,
            in1=key[:, u, :].rearrange("p (c t) -> p c t", c=CLUS), op0=ALU.mult, op1=ALU.add)
    V.link(ins)
    V.link(e.tensor_reduce(k.kmax, key, AXX, ALU.max))
    hot = k.onehot[:, bass.ds(i * TPC, TPC), :]
    V.link(e.tensor_tensor(hot, key, bcast(k.kmax.unsqueeze(2), tiles), ALU.is_equal))
    V.link(e.tensor_tensor(k.masked.rearrange("p u (t j) -> p u t j", j=DSL),
                           k.y.rearrange("p u (t j) -> p u t j", j=DSL),
                           bcast(hot.unsqueeze(3), [P, TPC, NTILE, DSL]), ALU.mult))
    mine = k.sliced[:, bass.ds(i * TPC, TPC), :]
    V.link(e.tensor_reduce(mine, k.masked.rearrange("p u (t j) -> p u j t", j=DSL), AXX, ALU.add))
    V.link(e.tensor_reduce(k.ends[:, :, 0], mine, AXX, ALU.max))
    V.link(e.tensor_reduce(k.ends[:, :, 1], mine, AXX, ALU.min))
    V.link(e.tensor_scalar(k.ends[:, :, 1], k.ends[:, :, 1], -1.0, None, ALU.mult))
    off = k.masked[:, 0, 0:256].rearrange("p (u t) -> p u t", u=TPC)
    cand = k.masked[:, 1, :].rearrange("p (u a t) -> p u a t", u=TPC, a=2)
    V.link(e.tensor_scalar(off, hot, 1.0, BIG, ALU.subtract, ALU.mult))
    V.link(e.tensor_tensor(cand, bcast(hot.unsqueeze(2), [P, TPC, 2, NTILE]),
                           bcast(k.ends.unsqueeze(3), [P, TPC, 2, NTILE]), ALU.mult))
    V.link(e.tensor_tensor(cand, cand, bcast(off.unsqueeze(2), [P, TPC, 2, NTILE]), ALU.add))
    best = k.masked[:, 0, 256:384].rearrange("p (a t) -> p a t", a=2)
    V.link(e.tensor_reduce(best, cand.rearrange("p u a t -> p a t u"), AXX, ALU.max))
    e.tensor_tensor(k.acc, k.acc, best, ALU.max).then_inc(s[p + "routed"], 1)
    gate(e, s[p + "routed"], i + n, s["gates"])


STATS_STEPS = 17
ROUTE_STEPS = 17


def minmax_tensor(k, pe, n, p):
    s = k.s
    pe.wait_ge(s[p + "routed"], n * NCH)
    for a in range(2):
        ins = pe.transpose(k.ps[0:NTILE, 0, a * P:(a + 1) * P], k.acc[:, a, :], k.c["ident"])
    ins.then_inc(s[p + "minmax_turned"], 1)


def minmax_vector(k, V, n, p):
    s, e = k.s, V.eng
    e.wait_ge(s[p + "minmax_turned"], n)
    V.link(e.tensor_reduce(k.ends2, k.ps[0:NTILE, 0, 0:256].rearrange("p (a t) -> p a t", a=2), AXX, ALU.max))
    V.link(e.tensor_copy(k.table[:, 258:259], k.ends2[:, 0:1]))
    e.tensor_scalar(k.table[:, 257:258], k.ends2[:, 1:2], -1.0, None, ALU.mult).then_inc(s[p + "table_ready"], 1)
    e.wait_ge(s[p + "table_ready"], n)



UG_GROUPS = 2 * INTER // CH
W0_GROUPS = 3


def setup_sync(k, sp):
    s, d = k.s, k.d
    sp.dma_start(k.const[:, 0:CONSTS.shape[1]], d["constants"]).then_inc(s["const_in"], 16)
    for c in range(NCH):
        sp.dma_start(k.x[:, c * TPC:(c + 1) * TPC, :],
                     d["L0_attn_hidden_states"][c].rearrange("(u p) n -> p u n", p=P)).then_inc(s["x_in"], 16)
    rows = [(k.gamma, d["L0_ffn_ln_gamma"]), (k.beta, d["L0_ffn_ln_beta"])]
    for dst, src in rows:
        sp.dma_start(dst, src.partition_broadcast(P)).then_inc(s["param_in"], 16)
    sp.dma_start(k.table[:, 0:128], d["L0_ffn_spline_bases"].rearrange("t j g -> t (j g)")).then_inc(s["param_in"], 16)
    sp.dma_start(k.table[:, 128:256], d["L0_ffn_spline_slopes"].rearrange("t j g -> t (j g)")).then_inc(s["param_in"], 16)
    sp.dma_start(k.table[:, 256:257], d["L0_ffn_output_scale"].unsqueeze(1)).then_inc(s["param_in"], 16)
    sp.dma_start(k.wscale, d["L1_ffn_Wscale_ug"].rearrange("(b p) -> p b", p=P)).then_inc(s["param_in"], 16)
    sp.dma_start(k.su_ug, d["L1_ffn_SU_ug"].rearrange("(b p) -> p b", p=P)).then_inc(s["param_in"], 16)
    sp.dma_start(k.su_dp, d["L1_ffn_SU_dp"].rearrange("(b p) -> p b", p=P)).then_inc(s["param_in"], 16)
    sp.dma_start(k.wscale_dp, d["L1_ffn_Wscale_dp"].rearrange("(b p) -> p b", p=P)).then_inc(s["param_in"], 16)
    sp.dma_start(k.bqk[:, 0:4], d["L0_attn_bq"].rearrange("(b p) -> p b", p=P)).then_inc(s["param_in"], 16)
    sp.dma_start(k.bqk[:, 4:6], d["L0_attn_bk"].rearrange("(b p) -> p b", p=P)).then_inc(s["param_in"], 16)

    def rows_of(w):
        return w.rearrange("(r p) n -> p r n", p=P)

    def load_nat(group, pieces):
        if group >= 2:
            sp.wait_ge(s["nat_turned"], 4 * (group - 1))
        at = 4 * (group % 2)
        for src, n in pieces:
            sp.dma_start(k.nat[:, at:at + n, :], src).then_inc(s[f"nat_in{group % 2}"], 32 // len(pieces))
            at += n

    load_nat(0, [(rows_of(d["L0_attn_Wq"])[:, 0:2], 2), (rows_of(d["L0_attn_Wq"])[:, 2:4], 2)])
    load_nat(1, [(rows_of(d["L0_attn_Wk"]), 2), (rows_of(d["L0_attn_Wv"]), 2)])
    for o in range(4):
        sp.dma_start(k.wd_nat[:, o, :], d["L1_ffn_W_down"][o * P:(o + 1) * P, :]).then_inc(s["wd_in"], 16)
    load_nat(2, [(rows_of(d["L0_attn_Wo"])[:, 0:2], 2), (rows_of(d["L0_attn_Wo"])[:, 2:4], 2)])
    for g in range(UG_GROUPS):
        w = rows_of(d["L1_ffn_W_up"] if g < UG_GROUPS // 2 else d["L1_ffn_W_gate"])
        r = 4 * (g % (UG_GROUPS // 2))
        load_nat(W0_GROUPS + g, [(w[:, r:r + 2], 2), (w[:, r + 2:r + 4], 2)])
    for m, name in enumerate(["L1_attn_Wq", "L1_attn_Wk", "L1_attn_Wv", "L1_attn_Wo"]):
        group = W0_GROUPS + UG_GROUPS + m
        if m < 2:
            sp.wait_ge(s["nat_turned"], 4 * (group - 1))
        else:
            sp.wait_ge(s["w1_lo"], m - 1)
        at = 4 * (group % 2)
        sp.dma_start(k.nat[:, at:at + 4, :], rows_of(d[name])).then_inc(s["w1_in"], 16)
        sp.wait_ge(s["w1_lo"], m + 1)
        sp.dma_start(d["w1_hi"][m], k.wt_hi).then_inc(s["w1_out"], 16)
        sp.dma_start(d["w1_lo"][m], k.wt_lo).then_inc(s["w1_out"], 16)
    for o in range(4):
        sp.wait_ge(s["wdo_lo"], 4 * (o + 1))
        for dst, src in ((d["wd_hi"], k.wdo_hi[o % 2]), (d["wd_lo"], k.wdo_lo[o % 2])):
            sp.dma_start(dst[:, :, o * P:(o + 1) * P], src).then_inc(s[f"wdo_out{o % 2}"], 16)


def setup_pool(k, e):
    s = k.s
    n = 0
    for o in range(4):
        e.wait_ge(s["wd_scaled"], o + 1)
        bufs = [k.wd_nat[:, o, :], k.wd_tmp]
        for stage in range(4):
            h = P << stage
            a = bufs[stage % 2].rearrange("p (g two m) -> p g two m", two=2, m=h)
            b = bufs[(stage + 1) % 2].rearrange("p (g two m) -> p g two m", two=2, m=h)
            e.tensor_tensor(b[:, :, 0], a[:, :, 0], a[:, :, 1], ALU.add)
            last = stage == 3
            e.tensor_tensor(b[:, :, 1], a[:, :, 0], a[:, :, 1], ALU.subtract)\
                .then_inc(s["wd_mixed"] if last else s["wd_step"], 1)
            if last:
                e.wait_ge(s["wd_mixed"], o + 1)
            else:
                n += 1
                e.wait_ge(s["wd_step"], n)
    for m in range(4):
        e.wait_ge(s["w1_hi"], m + 1)
        at = 4 * ((W0_GROUPS + UG_GROUPS + m) % 2)
        e.tensor_tensor(k.wt_lo, k.nat[:, at:at + 4, :], k.wt_hi, ALU.subtract).then_inc(s["w1_lo"], 1)


def turn_rows(k, pe, tile, buf, r):
    s = k.s
    for c in range(KC):
        ins = pe.transpose(k.ps[:, r % 2, c * P:(c + 1) * P], k.nat[:, buf + r, c * P:(c + 1) * P], k.c["ident"])
    ins.then_inc(s["nat_turned"], 1)


def setup_tensor(k, pe):
    s = k.s
    pe.wait_ge(s["const_in"], 16)
    pe.wait_ge(s["ss_diag"], 1)
    pe.matmul(k.ps[:, 4, :], k.ones, k.diag, start=True, stop=True).then_inc(s["ss_spread"], 1)
    for g in range(W0_GROUPS):
        pe.wait_ge(s[f"nat_in{g % 2}"], 32 * (g // 2 + 1))
        for r in range(4):
            if 4 * g + r >= 2:
                pe.wait_ge(s["wt_lo"], 4 * g + r - 1)
            turn_rows(k, pe, 4 * g + r, 4 * (g % 2), r)
    with pe.Fori(0, UG_GROUPS // 2) as i:
        for odd in range(2):
            buf = 4 * ((W0_GROUPS + odd) % 2)
            tile = 4 * W0_GROUPS + i * 8 + 4 * odd
            gate(pe, s["nat_scaled"], i * 8 + 4 * odd + 4, s["gates"])
            for r in range(4):
                gate(pe, s["wt_lo"], tile + r - 1, s["gates"])
                turn_rows(k, pe, tile + r, buf, r)
            gate(pe, s["wt_lo"], tile + 4, s["gates"])
            for kc in range(KC):
                gate(pe, s["had_lo"], i * 8 + 4 * odd + kc + 1, s["gates"])
                n = 0
                for jc in range(KC):
                    sign = k.had16n if bin(kc & jc).count("1") & 1 else k.had16
                    for part in (k.wt_hi, k.wt_lo):
                        ins = pe.matmul(k.ps[:, 2 + kc % 2, :], sign, part[:, jc, :], start=(n == 0), stop=(n == 7))
                        n += 1
                ins.then_inc(s["had_done"], 1)
    base = 4 * (W0_GROUPS + UG_GROUPS)
    for o in range(4):
        pe.wait_ge(s["wd_mixed"], o + 1)
        for q in range(4):
            if o or q >= 2:
                pe.wait_ge(s["wdt_lo"], 4 * o + q - 1)
            elif q == 0:
                pe.wait_ge(s["wt_lo"], base)
            for b in range(4):
                c = 4 * q + b
                ins = pe.transpose(k.ps[:, q % 2, b * P:(b + 1) * P], k.wd_nat[:, o, c * P:(c + 1) * P], k.c["ident"])
            ins.then_inc(s["wdt_turned"], 1)
        pe.wait_ge(s["wdt_lo"], 4 * o + 4)
        for q in range(4):
            if o or q >= 2:
                pe.wait_ge(s["wdo_lo"], 4 * o + q - 1)
            else:
                pe.wait_ge(s["had_lo"], 2 + 4 * UG_GROUPS)
            for b in range(4):
                c = 4 * q + b
                pe.matmul(k.ps[:, 2 + q % 2, b * P:(b + 1) * P], k.had16, k.wdt_hi[:, c, :], start=True, stop=False)
                ins = pe.matmul(k.ps[:, 2 + q % 2, b * P:(b + 1) * P], k.had16, k.wdt_lo[:, c, :], start=False, stop=True)
            ins.then_inc(s["wdh_done"], 1)


def setup_scalar(k, e):
    s = k.s
    e.wait_ge(s["const_in"], 16)
    e.activation(k.had16, k.c["had"], ACT.Copy)
    e.activation(k.had16n, k.c["had"], ACT.Copy, scale=-1.0).then_inc(s["ones_set"], 1)
    e.wait_ge(s["ssum_ready"], 1)
    e.activation(k.ssign, k.ssum, ACT.Sign).then_inc(s["ss_signed"], 1)
    e.wait_ge(s["ss_spread"], 1)
    e.activation(k.ssrow, k.ps[:, 4, :], ACT.Copy).then_inc(s["ss_row"], 1)
    for o in range(4):
        e.wait_ge(s["wd_in"], 64)
        e.activation(k.wd_nat[:, o, :], k.wd_nat[:, o, :], ACT.Copy, scale=k.wscale_dp[:, o:o + 1])\
            .then_inc(s["wd_scaled"], 1)
    for g in range(W0_GROUPS):
        for r in range(4):
            e.wait_ge(s["nat_turned"], 4 * g + r + 1)
            c = (4 * g + r) * P
            e.activation(k.w0_hi[:, :, c:c + P], k.ps[:, r % 2, :].rearrange("p (c m) -> p c m", c=KC), ACT.Copy,
                         scale=W_SCALE).then_inc(s["wt_hi"], 1)
    e.wait_ge(s["up_scale"], 2)
    with e.Fori(0, UG_GROUPS // 2) as i:
        for odd in range(2):
            buf = 4 * ((W0_GROUPS + odd) % 2)
            gate(e, s[f"nat_in{(W0_GROUPS + odd) % 2}"], i * 32 + 32 * ((W0_GROUPS + odd) // 2 + 1), s["gates"])
            for r in range(4):
                e.activation(k.nat[:, buf + r, :], k.nat[:, buf + r, :], ACT.Copy,
                             scale=k.wscale[:, bass.ds(i * 8 + 4 * odd + r, 1)]).then_inc(s["nat_scaled"], 1)
            for r in range(4):
                tile = 4 * W0_GROUPS + i * 8 + 4 * odd + r
                gate(e, s["nat_turned"], tile + 1, s["gates"])
                e.activation(k.wt_hi[:, :, r * P:(r + 1) * P], k.ps[:, r % 2, :].rearrange("p (c m) -> p c m", c=KC),
                             ACT.Copy, scale=W_SCALE).then_inc(s["wt_hi"], 1)
            for kc in range(KC):
                gate(e, s["had_done"], i * 8 + 4 * odd + kc + 1, s["gates"])
                e.activation(k.wug_hi[:, kc, bass.ds(i * 1024 + CH * odd, CH)], k.ps[:, 2 + kc % 2, :], ACT.Copy,
                             scale=k.su_ug[:, kc:kc + 1]).then_inc(s["had_hi"], 1)
    for m in range(4):
        e.wait_ge(s["w1_in"], 16 * (m + 1))
        at = 4 * ((W0_GROUPS + UG_GROUPS + m) % 2)
        e.activation(k.nat[:, at:at + 4, :], k.nat[:, at:at + 4, :], ACT.Copy, scale=W_SCALE)\
            .then_inc(s["w1_scaled"], 1)
        e.wait_ge(s["w1_scaled"], m + 1)
        if m == 0:
            e.wait_ge(s["had_done"], 4 * UG_GROUPS)
        else:
            e.wait_ge(s["w1_out"], 32 * m)
        e.activation(k.wt_hi, k.nat[:, at:at + 4, :], ACT.Copy).then_inc(s["w1_hi"], 1)
    e.wait_ge(s["w1_out"], 128)
    for o in range(4):
        for q in range(4):
            e.wait_ge(s["wdt_turned"], 4 * o + q + 1)
            if q == 0 and o:
                e.wait_ge(s["wdh_done"], 4 * o)
            e.activation(k.wdt_hi[:, 4 * q:4 * q + 4, :], k.ps[:, q % 2, :].rearrange("p (c m) -> p c m", c=4),
                         ACT.Copy, scale=W_SCALE).then_inc(s["wdt_hi"], 1)
        for q in range(4):
            e.wait_ge(s["wdh_done"], 4 * o + q + 1)
            if q == 0 and o >= 2:
                e.wait_ge(s[f"wdo_out{o % 2}"], 32)
            e.activation(k.wdo_hi[o % 2][:, 4 * q:4 * q + 4, :], k.ps[:, 2 + q % 2, :].rearrange("p (c m) -> p c m", c=4),
                         ACT.Copy, scale=float(INTER) ** -0.5).then_inc(s["wdo_hi"], 1)


def setup_vector_first(k, V):
    s, e = k.s, V.eng
    e.memset(k.ones, 1.0)
    e.memset(k.rt, 0.0).then_inc(s["rt_zeroed"], 1)
    e.memset(k.acc, -BIG).then_inc(s["had_lo"], 2)
    e.wait_ge(s["const_in"], 16)
    e.wait_ge(s["param_in"], 16 * 11)
    e.tensor_reduce(k.ssum, k.table[:, 128:256].rearrange("t (j g) -> t j g", g=GRID), AXX, ALU.add)\
        .then_inc(s["ssum_ready"], 1)
    e.wait_ge(s["ss_signed"], 1)
    e.tensor_tensor(k.diag.rearrange("p (t j) -> p t j", j=DSL),
                    bcast(k.c["ident"][0:NTILE, 0:NTILE].unsqueeze(2), [NTILE, NTILE, DSL]),
                    bcast(k.ssign.unsqueeze(1), [NTILE, NTILE, DSL]), ALU.mult).then_inc(s["ss_diag"], 1)
    e.tensor_tensor(k.wscale[:, 0:FB], k.wscale[:, 0:FB], k.su_dp, ALU.mult).then_inc(s["up_scale"], 1)
    e.tensor_scalar(k.su_ug, k.su_ug, float(HID) ** -0.5, None, ALU.mult).then_inc(s["up_scale"], 1)
    e.wait_ge(s["up_scale"], 2)
    for g in range(W0_GROUPS):
        for r in range(4):
            e.wait_ge(s["wt_hi"], 4 * g + r + 1)
            c = (4 * g + r) * P
            e.scalar_tensor_tensor(out=k.w0_lo[:, :, c:c + P],
                                   in0=k.ps[:, r % 2, :].rearrange("p (c m) -> p c m", c=KC), scalar=W_SCALE,
                                   in1=k.w0_hi[:, :, c:c + P], op0=ALU.mult, op1=ALU.subtract)\
                .then_inc(s["wt_lo"], 1)


def setup_vector_rest(k, V):
    s, e = k.s, V.eng
    with e.Fori(0, UG_GROUPS // 2) as i:
        for odd in range(2):
            for r in range(4):
                gate(e, s["wt_hi"], 4 * W0_GROUPS + i * 8 + 4 * odd + r + 1, s["gates"])
                e.scalar_tensor_tensor(out=k.wt_lo[:, :, r * P:(r + 1) * P],
                                       in0=k.ps[:, r % 2, :].rearrange("p (c m) -> p c m", c=KC), scalar=W_SCALE,
                                       in1=k.wt_hi[:, :, r * P:(r + 1) * P], op0=ALU.mult, op1=ALU.subtract)\
                    .then_inc(s["wt_lo"], 1)
            for kc in range(KC):
                gate(e, s["had_hi"], i * 8 + 4 * odd + kc + 1, s["gates"])
                cols = bass.ds(i * 1024 + CH * odd, CH)
                e.scalar_tensor_tensor(out=k.wug_lo[:, kc, cols], in0=k.ps[:, 2 + kc % 2, :],
                                       scalar=k.su_ug[:, kc:kc + 1], in1=k.wug_hi[:, kc, cols],
                                       op0=ALU.mult, op1=ALU.subtract).then_inc(s["had_lo"], 1)
    for o in range(4):
        for q in range(4):
            e.wait_ge(s["wdt_hi"], 4 * o + q + 1)
            if q == 0 and o:
                e.wait_ge(s["wdh_done"], 4 * o)
            if q == 0 and o == 0:
                e.wait_ge(s["w1_out"], 128)
            e.scalar_tensor_tensor(out=k.wdt_lo[:, 4 * q:4 * q + 4, :],
                                   in0=k.ps[:, q % 2, :].rearrange("p (c m) -> p c m", c=4), scalar=W_SCALE,
                                   in1=k.wdt_hi[:, 4 * q:4 * q + 4, :], op0=ALU.mult, op1=ALU.subtract)\
                .then_inc(s["wdt_lo"], 1)
        for q in range(4):
            e.wait_ge(s["wdo_hi"], 4 * o + q + 1)
            if q == 0 and o >= 2:
                e.wait_ge(s[f"wdo_out{o % 2}"], 32)
            e.scalar_tensor_tensor(out=k.wdo_lo[o % 2][:, 4 * q:4 * q + 4, :],
                                   in0=k.ps[:, 2 + q % 2, :].rearrange("p (c m) -> p c m", c=4),
                                   scalar=float(INTER) ** -0.5, in1=k.wdo_hi[o % 2][:, 4 * q:4 * q + 4, :],
                                   op0=ALU.mult, op1=ALU.subtract).then_inc(s["wdo_lo"], 1)


def first_scalar(k, e, n, p):
    e.wait_ge(k.s["x_in"], 16 * NCH)
    e.wait_ge(k.s["wdo_out0"], 64)
    e.wait_ge(k.s["wdo_out1"], 64)
    with e.Fori(0, NCH) as i:
        token_stats_scalar(k, e, i, n, p)


def first_vector(k, V, n, p):
    V.eng.wait_ge(k.s["x_in"], 16 * NCH)
    V.eng.wait_ge(k.s["ss_row"], 1)
    V.eng.wait_ge(k.s["wdo_out0"], 64)
    V.eng.wait_ge(k.s["wdo_out1"], 64)
    with V.eng.Fori(0, NCH) as i:
        V.enter(i, STATS_STEPS + ROUTE_STEPS)
        token_stats_vector(k, V, i, n, p)
        routing_vector(k, V, i, n, p)
    V.leave(NCH)




def apply_tensor(k, pe, i, n):
    s = k.s
    gate(pe, s["ap_oh"], i + n, s["gates"])
    for u in range(TPC):
        ins = pe.transpose(k.ps[0:NTILE, 6, u * P:(u + 1) * P], k.oh4[:, u, :], k.c["ident"])
    ins.then_inc(s["ap_turned"], 1)
    gate(pe, s["ap_oht"], i + n, s["gates"])
    for u in range(TPC):
        ins = pe.matmul(k.ps[:, 2 + u, 0:259], k.oht[:, u * P:(u + 1) * P], k.table[:, 0:259], start=True, stop=True)
    ins.then_inc(s["ap_rows"], 1)


def apply_scalar(k, e, i, n):
    s = k.s
    gate(e, s["ap_turned"], i + n, s["gates"])
    e.activation(k.oht, k.ps[0:NTILE, 6, :], ACT.Copy).then_inc(s["ap_oht"], 1)


APPLY_STEPS = 27


def apply_vector(k, V, i, n):
    s, e = k.s, V.eng
    tiles = bass.ds(i * TPC, TPC)
    hot = k.onehot[:, tiles, :]
    e.tensor_copy(k.oh4, hot).then_inc(s["ap_oh"], 1)
    a, b = k.t4[0], k.t4[1]
    mr = k.mr[:, tiles, :]
    V.link(e.tensor_scalar(a, mr[:, :, 1], 0.5, None, ALU.mult))
    V.link(e.tensor_tensor(b, mr[:, :, 0], a, ALU.mult))
    V.link(e.tensor_scalar(a, a, 1.0, None, ALU.add))
    for u in range(TPC):
        xt = k.x[:, bass.ds(i * TPC + u, 1), :].squeeze(1)
        ins = e.tensor_scalar(xt, xt, a[:, u:u + 1], b[:, u:u + 1], ALU.mult, ALU.subtract)
    V.link(ins)
    gate(e, s["ap_rows"], i + n, s["gates"])
    rows = k.ps[:, 2:2 + TPC, :]
    V.link(e.tensor_copy(k.cols, rows[:, :, 256:259]))
    full = [P, TPC, DSL]
    u16, lo, fl, d1, xl, sp = k.ap
    half, span, mn, mx = k.t4[0], k.t4[1], k.cols[:, :, 1], k.cols[:, :, 2]
    V.link(e.tensor_tensor(span, mx, mn, ALU.subtract))
    V.link(e.tensor_scalar(span, span, 1e-8, None, ALU.add))
    V.link(e.reciprocal(span, span))
    V.link(e.tensor_scalar(half, k.cols[:, :, 0], 0.5, None, ALU.mult))
    V.link(e.tensor_tensor(u16, k.sliced[:, tiles, :], bcast(mn.unsqueeze(2), full), ALU.subtract))
    V.link(e.tensor_tensor(u16, u16, bcast(span.unsqueeze(2), full), ALU.mult))
    V.link(e.tensor_scalar(u16, u16, 0.0, 1.0 - 1e-6, ALU.max, ALU.min))
    V.link(e.tensor_scalar(u16, u16, float(GRID), None, ALU.mult))
    V.link(e.tensor_scalar(fl, u16, ROUND, ROUND, ALU.add, ALU.subtract))
    V.link(e.tensor_tensor(lo, fl, u16, ALU.is_gt))
    V.link(e.tensor_tensor(fl, fl, lo, ALU.subtract))
    V.link(e.tensor_tensor(xl, u16, fl, ALU.subtract))
    cells = [P, TPC, DSL, GRID]
    V.link(e.tensor_tensor(k.m16, bcast(k.c["iota"].unsqueeze(1).unsqueeze(1), cells), bcast(fl.unsqueeze(3), cells),
                           ALU.is_equal))
    for dst, at in ((sp, 128), (d1, 0)):
        V.link(e.tensor_tensor(k.m16p, k.m16, rows[:, :, at:at + 128].rearrange("p u (j g) -> p u j g", g=GRID),
                               ALU.mult))
        V.link(e.tensor_reduce(dst, k.m16p, AXX, ALU.add))
    V.link(e.tensor_tensor(sp, sp, xl, ALU.mult))
    V.link(e.tensor_tensor(d1, d1, sp, ALU.add))
    V.link(e.tensor_tensor(d1, d1, bcast(half.unsqueeze(2), full), ALU.mult))
    for u in range(TPC):
        ins = e.tensor_tensor(k.scat[:, u, :].rearrange("p (t j) -> p t j", j=DSL),
                              bcast(k.oh4[:, u, :].unsqueeze(2), [P, NTILE, DSL]),
                              bcast(d1[:, u, :].unsqueeze(1), [P, NTILE, DSL]), ALU.mult)
    V.link(ins)
    xs = k.x[:, tiles, :]
    V.link(e.tensor_tensor(xs, xs, k.scat, ALU.add))




NORM_STEPS = 8


def norm_vector(k, V, i, n):
    norm_stats_vector(k, V, i, n)
    norm_low_vector(k, i, n, V.eng)


def norm_stats_vector(k, V, i, n):
    s, e = k.s, V.eng
    for u in range(TPC):
        ins = e.bn_stats(k.stats6[:, u, :], k.x[:, bass.ds(i * TPC + u, 1), :].squeeze(1))
    V.link(ins)
    for u in range(TPC):
        ins = e.bn_aggr(k.mv[:, u, :], k.stats6[:, u, :])
    V.link(ins)
    ve, std, r, t, std2, r2, nm2 = k.t4
    mean, var = k.mv[:, :, 0], k.mv[:, :, 1]
    e.tensor_scalar(ve, var, LN_EPS, None, ALU.add).then_inc(s["n_var"], 1)
    gate(e, s["n_std"], i + n, s["gates"])
    rsqrt_vector(V, r, std, ve, t)
    V.link(e.tensor_scalar(r2, r, A_SCALE, None, ALU.mult))
    e.scalar_tensor_tensor(out=nm2, in0=mean, scalar=-1.0, in1=r2, op0=ALU.mult, op1=ALU.mult)\
        .then_inc(s["n_norm"], 1)


def norm_low_vector(k, i, n, e):
    s = k.s
    for c in range(KC):
        gate(e, s["n_hi"], nth(i, n, KC, c + 1), s["gates"])
        e.tensor_tensor(k.ht_lo[:, c, :], k.ps[:, c % 2, :], k.ht_hi[:, c, :], ALU.subtract).then_inc(s["n_lo"], 1)


def norm_scalar(k, e, i, n):
    s = k.s
    ve, std, r, t, std2, r2, nm2 = k.t4
    gate(e, s["n_var"], i + n, s["gates"])
    e.activation(std, ve, ACT.Sqrt).then_inc(s["n_std"], 1)
    gate(e, s["n_norm"], i + n, s["gates"])
    for u in range(TPC):
        ins = e.activation(k.h[:, u, :], k.x[:, bass.ds(i * TPC + u, 1), :].squeeze(1), ACT.Identity,
                           bias=nm2[:, u:u + 1], scale=r2[:, u:u + 1])
    ins.then_inc(s["n_h"], 1)
    for c in range(KC):
        gate(e, s["n_turned"], nth(i, n, KC, c + 1), s["gates"])
        e.activation(k.ht_hi[:, c, :], k.ps[:, c % 2, :], ACT.Copy).then_inc(s["n_hi"], 1)


def norm_tensor(k, pe, i, n):
    s = k.s
    gate(pe, s["n_h"], i + n, s["gates"])
    for c in range(KC):
        gate(pe, s["n_lo"], nth(i, n, KC, c + 1), s["gates"])
        for u in range(TPC):
            ins = pe.transpose(k.ps[:, c % 2, u * P:(u + 1) * P], k.h[:, u, c * P:(c + 1) * P], k.c["ident"])
        ins.then_inc(s["n_turned"], 1)
    gate(pe, s["n_lo"], nth(i, n, KC, KC + 2), s["gates"])


def pairs_product(pe, out, left, right, n=KC):
    at = 0
    for c in range(n):
        for a, b in ((0, 0), (0, 1), (1, 0)):
            ins = pe.matmul(out, left[a](c), right[b](c), start=(at == 0), stop=(at == 3 * n - 1))
            at += 1
    return ins


def of(ref, cols, block=None):
    return lambda c: ref[:, c, cols]



ORDER = (4, 5, 0, 1, 2, 3)
GROUP = 16
PAIRS = CH // GROUP // 2


def b_tensor(k, pe, i):
    s = k.s
    apply_tensor(k, pe, i, 1)
    norm_tensor(k, pe, i, 1)
    ht = (k.ht_hi, k.ht_lo)
    w0 = (k.w0_hi, k.w0_lo)
    for u in range(TPC):
        gate(pe, s["b_v_in"], nth(i, 1, TPC, u + 1), s["gates"])
        cols = slice(u * P, (u + 1) * P)
        pairs_product(pe, k.ps[:, 6 + u % 2, 0:256], [of(h, cols) for h in ht], [of(w, slice(768, 1024)) for w in w0])\
            .then_inc(s["b_v_done"], 1)
    for z in range(8):
        if z < 6:
            gate(pe, s["b_qf"], nth(i, 1, 6, z + 1), s["gates"])
            cols = slice(ORDER[z] * P, (ORDER[z] + 1) * P)
            pairs_product(pe, k.ps[:, 2 + z % 2, :], [of(w, cols) for w in w0], [of(h, slice(0, CH)) for h in ht])\
                .then_inc(s["b_qk_done"], 1)
        if 1 <= z < 7:
            gate(pe, s["b_qf"], nth(i, 1, 6, z + 2), s["gates"])
            gate(pe, s["b_rope"], nth(i, 1, 6, z), s["gates"])
            pe.matmul(k.ps[:, 4 + (z - 1) % 2, :], k.c["rot"], k.qf[:, z - 1, :], start=True, stop=True)\
                .then_inc(s["b_rot"], 1)
        if z >= 2:
            gate(pe, s["b_sq"], nth(i, 1, 6, z - 1), s["gates"])
            at = 20 - 4 * (z - 2)
            pe.matmul(k.ps[0:24, 0, :], k.c["headpad"][:, at:at + 24], k.q2[:, z % 2, :], start=(z == 2), stop=(z == 7))\
                .then_inc(s["b_nsum"], 1)
    gate(pe, s["b_r"], i + 1, s["gates"])
    for z in range(6):
        gate(pe, s["b_y"], nth(i, 1, 6, z + 1), s["gates"])
        pe.matmul(k.ps[:, 6 + z % 2, :], k.spread[:, z * P:(z + 1) * P], k.nr[0:24, 2, :], start=True, stop=True)
        pe.matmul(k.ps[:, 2 + z % 2, :], k.rt, k.qr[:, z, :], start=True, stop=True).then_inc(s["b_p"], 1)
    gate(pe, s["b_qs"], nth(i, 1, 256, 256), s["gates"])
    gate(pe, s["b_vr"], nth(i, 1, 16, 16), s["gates"])
    for y in range(PAIRS + 1):
        if y < PAIRS:
            gate(pe, s["b_mask"], nth(i, 1, PAIRS, y + 1), s["gates"])
            if y % 4 == 0:
                gate(pe, s["b_ksg"], nth(i, 1, 4, y // 4 + 1), s["gates"])
            for q in range(2):
                toks = slice((2 * y + q) * GROUP, (2 * y + q + 1) * GROUP)
                ins = pe.matmul(k.ps[:, 4 + y % 2, 256 * q:256 * q + 256].rearrange("p (t h) -> p t h", h=16),
                                k.ksg[:, 2 * y + q, :], k.qs[:, :, toks].rearrange("p h t -> p t h"),
                                start=True, stop=True)
            ins.then_inc(s["b_s"], 1)
        if y:
            gate(pe, s["b_mask"], nth(i, 1, PAIRS, y + 2), s["gates"])
            if y % 4 == 1:
                gate(pe, s["b_ot_lo"], nth(i, 1, TPC, y // 4 + 1), s["gates"])
            for q in range(2):
                g = 2 * (y - 1) + q
                for j in range(4):
                    ins = pe.matmul(k.ps[32 * j:32 * j + 32, g // 8 % 2, 64 * (g % 8):64 * (g % 8) + 64]
                                    .rearrange("p (a h) -> p a h", h=16), k.vr[:, g, :],
                                    k.sm[:, (y - 1) % 2, q].rearrange("p (a j) h -> p j a h", j=4)[:, j],
                                    start=True, stop=True, tile_position=(0, 32 * j))
            ins.then_inc(s["b_pv"], 1)
    gate(pe, s["b_ot_lo"], nth(i, 1, TPC, TPC + 2), s["gates"])
    for u in range(TPC):
        cols = slice(u * P, (u + 1) * P)
        if u >= 2:
            gate(pe, s["b_res"], nth(i, 1, TPC, u - 1), s["gates"])
        pairs_product(pe, k.ps[:, 6 + u % 2, :], [of(o, cols) for o in (k.ht_hi, k.ht_lo)],
                      [of(w, slice(1024, 1536)) for w in w0]).then_inc(s["b_out"], 1)


def grouped(ref):
    return ref.rearrange("p a (h g) -> p g a h", g=32)


def b_scalar(k, e, i):
    s = k.s
    apply_scalar(k, e, i, 1)
    norm_scalar(k, e, i, 1)
    for z in range(6):
        gate(e, s["b_qk_done"], nth(i, 1, 6, z + 1), s["gates"])
        e.activation(k.qf[:, z, :], k.ps[:, 2 + z % 2, :], ACT.Identity, bias=k.bqk[:, ORDER[z]:ORDER[z] + 1],
                     scale=1.0 / (W_SCALE * A_SCALE)).then_inc(s["b_qf"], 1)
    gate(e, s["b_n2"], i + 1, s["gates"])
    e.activation(k.nr[0:24, 1, :], k.nr[0:24, 0, :], ACT.Sqrt).then_inc(s["b_n"], 1)
    for z in range(6):
        gate(e, s["b_reduced"], nth(i, 1, 6, z + 1), s["gates"])
        e.activation(k.ang[:, z % 2, :], k.ang[:, z % 2, :], ACT.Sin, bias=k.c["phase2pi"], scale=-float(2 * np.pi))\
            .then_inc(s["b_feat"], 1)
        gate(e, s["b_feat"], nth(i, 1, 6, z + 1), s["gates"])
        e.activation(k.f_hi[:, z, :], k.ang[:, z % 2, :], ACT.Copy, scale=A_SCALE).then_inc(s["b_f_hi"], 1)
    gate(e, s["b_ks"], nth(i, 1, 256, 256), s["gates"])
    gate(e, s["b_f_lo"], nth(i, 1, 6, 6), s["gates"])
    for g in range(4):
        e.activation(k.ksg[:, 8 * g:8 * g + 8, :].rearrange("p g (t h) -> p g t h", h=8),
                     k.ks[:, :, P * g:P * g + P].rearrange("p h (g t) -> p g t h", t=GROUP), ACT.Copy)\
            .then_inc(s["b_ksg"], 1)
    for g in range(4):
        gate(e, s["b_pv"], nth(i, 1, PAIRS, 4 * g + 4), s["gates"])
        e.activation(grouped(k.ht_hi)[:, 8 * g:8 * g + 8], k.ps[:, g % 2, :].rearrange("p (g a h) -> p g a h", g=8, a=4),
                     ACT.Copy, scale=O_SCALE).then_inc(s["b_ot_hi"], 1)


O_SCALE = 2.0 / 32 * A_SCALE / (A_SCALE * A_SCALE)


def b_pool(k, e, i):
    s = k.s
    for z in range(6):
        gate(e, s["b_qf"], nth(i, 1, 6, z + 3), s["gates"])
        e.tensor_tensor(k.qr[:, z, :], k.qf[:, z, :], k.c["cos"], ALU.mult).then_inc(s["b_cos"], 1)
        gate(e, s["b_rope"], nth(i, 1, 6, z + 3), s["gates"])
        if z >= 2:
            gate(e, s["b_nsum"], nth(i, 1, 6, z - 1), s["gates"])
        e.tensor_tensor(k.q2[:, z % 2, :], k.qr[:, z, :], k.qr[:, z, :], ALU.mult).then_inc(s["b_sq"], 1)


def b_sync(k, sp, i):
    s, scratch = k.s, k.d["values"]
    gate(sp, s["b_v_in"], nth(i, 1, TPC, TPC + 2), s["gates"])
    sp.dma_start(scratch.rearrange("(u p) n -> p u n", p=P), k.v0).then_inc(s["b_v_out"], 16)
    gate(sp, s["b_v_out"], nth(i, 1, 16, 16), s["gates"])
    sp.dma_start(k.vr, scratch.rearrange("(g t) (h d) -> (t h) g d", t=GROUP, d=32)).then_inc(s["b_vr"], 16)
    f = (k.f_hi, k.f_lo)
    gate(sp, s["b_f_lo"], nth(i, 1, 6, 2), s["gates"])
    for part in range(4):
        for j in range(4):
            dst = k.ks[32 * part:32 * part + 32].rearrange("p (b j) t -> p j b t", j=4)[:, j]
            sp.dma_start(dst, f[part // 2][32 * j:32 * j + 32, 0:2, :]).then_inc(s["b_ks"], 16)
    gate(sp, s["b_f_lo"], nth(i, 1, 6, 6), s["gates"])
    for part in range(4):
        for j in range(4):
            dst = k.qs[32 * part:32 * part + 32].rearrange("p (b j) t -> p j b t", j=4)[:, j]
            sp.dma_start(dst, f[part % 2][32 * j:32 * j + 32, 2:6, :]).then_inc(s["b_qs"], 16)
    gate(sp, s["b_vr"], nth(i, 1, 16, 16), s["gates"])


B_STEPS = 6 + 5 + TPC


def b_vector(k, V, i):
    s, e = k.s, V.eng
    apply_vector(k, V, i, 1)
    norm_vector(k, V, i, 1)
    for u in range(TPC):
        gate(e, s["b_v_done"], nth(i, 1, TPC, u + 1), s["gates"])
        e.scalar_tensor_tensor(out=k.v0[:, u, :], in0=k.ps[:, 6 + u % 2, 0:256], scalar=1.0 / (W_SCALE * A_SCALE),
                               in1=k.bv, op0=ALU.mult, op1=ALU.add).then_inc(s["b_v_in"], 1)
    for z in range(6):
        gate(e, s["b_rot"], nth(i, 1, 6, z + 1), s["gates"])
        gate(e, s["b_cos"], nth(i, 1, 6, z + 1), s["gates"])
        V.link(e.tensor_tensor(k.qf[:, z, :], k.ps[:, 4 + z % 2, :], k.c["sin"], ALU.mult))
        e.tensor_tensor(k.qr[:, z, :], k.qr[:, z, :], k.qf[:, z, :], ALU.add).then_inc(s["b_rope"], 1)
    gate(e, s["b_nsum"], nth(i, 1, 6, 6), s["gates"])
    n2, nn, r, t = [k.nr[0:24, m, :] for m in range(4)]
    e.tensor_scalar(n2, k.ps[0:24, 0, :], 1e-12, None, ALU.max).then_inc(s["b_n2"], 1)
    gate(e, s["b_n"], i + 1, s["gates"])
    rsqrt_vector(V, r, nn, n2, t)
    e.sem_inc(s["b_r"], 1)
    for z in range(7):
        if z < 6:
            ang, turns = k.ang[:, z % 2, :], k.turns[:, z % 2, :]
            gate(e, s["b_p"], nth(i, 1, 6, z + 1), s["gates"])
            e.tensor_copy(turns, k.ps[:, 6 + z % 2, :]).then_inc(s["b_spread"], 1)
            gate(e, s["b_spread"], nth(i, 1, 6, z + 1), s["gates"])
            e.scalar_tensor_tensor(out=turns, in0=k.ps[:, 2 + z % 2, :], scalar=float(1 / (2 * np.pi)), in1=turns,
                                   op0=ALU.mult, op1=ALU.mult).then_inc(s["b_y"], 1)
            gate(e, s["b_y"], nth(i, 1, 6, z + 3), s["gates"])
            if z >= 2:
                gate(e, s["b_f_lo"], nth(i, 1, 6, z - 1), s["gates"])
            e.tensor_scalar(ang, turns, k.c["phase"], ROUND, ALU.add, ALU.add).then_inc(s["b_whole"], 1)
            gate(e, s["b_whole"], nth(i, 1, 6, z + 1), s["gates"])
            e.scalar_tensor_tensor(out=ang, in0=ang, scalar=ROUND, in1=turns, op0=ALU.subtract, op1=ALU.subtract)\
                .then_inc(s["b_reduced"], 1)
        if z:
            gate(e, s["b_f_hi"], nth(i, 1, 6, z), s["gates"])
            e.scalar_tensor_tensor(out=k.f_lo[:, z - 1, :], in0=k.ang[:, (z - 1) % 2, :], scalar=A_SCALE,
                                   in1=k.f_hi[:, z - 1, :], op0=ALU.mult, op1=ALU.subtract).then_inc(s["b_f_lo"], 1)
    for y in range(PAIRS):
        gate(e, s["b_s"], nth(i, 1, PAIRS, y + 1), s["gates"])
        if y >= 2:
            gate(e, s["b_pv"], nth(i, 1, PAIRS, y - 1), s["gates"])
        for q in range(2):
            ins = e.tensor_tensor(k.sm[:, y % 2, q], k.ps[:, 4 + y % 2, 256 * q:256 * q + 256]
                                  .rearrange("p (t h) -> p t h", h=16), bcast(k.c["same"].unsqueeze(2), [P, 16, 16]),
                                  ALU.mult)
        ins.then_inc(s["b_mask"], 1)
        if y % 4 == 1 and y > 4:
            b_low(k, e, i, y // 4 - 1)
    b_low(k, e, i, 3)
    for u in range(TPC):
        gate(e, s["b_out"], nth(i, 1, TPC, u + 1), s["gates"])
        xt = k.x[:, bass.ds(i * TPC + u, 1), :].squeeze(1)
        e.scalar_tensor_tensor(out=xt, in0=k.ps[:, 6 + u % 2, :], scalar=1.0 / (W_SCALE * A_SCALE), in1=xt,
                               op0=ALU.mult, op1=ALU.add).then_inc(s["b_res"], 1)
        gate(e, s["b_res"], nth(i, 1, TPC, u + 1), s["gates"])
        V.link(e.tensor_tensor(xt, xt, k.bo, ALU.add))


def b_low(k, e, i, g):
    s = k.s
    gate(e, s["b_ot_hi"], nth(i, 1, TPC, g + 1), s["gates"])
    out = grouped(k.ht_lo)[:, 8 * g:8 * g + 8]
    e.scalar_tensor_tensor(out=out, in0=k.ps[:, g % 2, :].rearrange("p (g a h) -> p g a h", g=8, a=4), scalar=O_SCALE,
                           in1=grouped(k.ht_hi)[:, 8 * g:8 * g + 8], op0=ALU.mult, op1=ALU.subtract)\
        .then_inc(s["b_ot_lo"], 1)




DOWN_BANK = (6, 7, 0, 1)


def ffn_tensor(k, pe, i, n, after):
    s = k.s
    ht = [of(h, slice(0, CH)) for h in (k.ht_hi, k.ht_lo)]
    for f in range(FB):
        gate(pe, s["f_prod"], nth(i, n, FB, f + 1), s["gates"])
        for which, at in ((0, INTER + f * P), (1, f * P)):
            w = [of(x, slice(at, at + P)) for x in (k.wug_hi, k.wug_lo)]
            pairs_product(pe, k.ps[:, 2 + 2 * (f % 2) + which, :], w, ht).then_inc(s["f_up" if which else "f_gate"], 1)
    gate(pe, s["f_lo"], nth(i, n, FB, FB), s["gates"])
    after()
    for u in range(TPC):
        cols = slice(u * P, (u + 1) * P)
        pairs_product(pe, k.ps[:, DOWN_BANK[u], :], [of(a, cols) for a in (k.act_hi, k.act_lo)],
                      [of(w, slice(0, HID)) for w in (k.wd_hi, k.wd_lo)], FB).then_inc(s["f_down"], 1)
    gate(pe, s["f_out"], nth(i, n, TPC, TPC), s["gates"])


def ffn_scalar(k, e, i, n):
    s = k.s
    for f in range(FB + 1):
        if f < FB:
            gate(e, s["f_gate"], nth(i, n, FB, f + 1), s["gates"])
            if f >= 2:
                gate(e, s["f_prod"], nth(i, n, FB, f + 1), s["gates"])
            e.activation(k.silu[:, f % 2, :], k.ps[:, 2 + 2 * (f % 2), :], ACT.Silu, scale=1.0 / (W_SCALE * A_SCALE))\
                .then_inc(s["f_silu"], 1)
        if f:
            gate(e, s["f_prod"], nth(i, n, FB, f + 2), s["gates"])
            e.activation(k.act_hi[:, f - 1, :], k.prod[:, (f - 1) % 2, :], ACT.Copy).then_inc(s["f_hi"], 1)


def ffn_vector(k, V, i, n, after):
    s, e = k.s, V.eng
    for f in range(FB + 1):
        if f < FB:
            gate(e, s["f_up"], nth(i, n, FB, f + 1), s["gates"])
            gate(e, s["f_silu"], nth(i, n, FB, f + 1), s["gates"])
            if f >= 2:
                gate(e, s["f_lo"], nth(i, n, FB, f - 1), s["gates"])
            e.scalar_tensor_tensor(out=k.prod[:, f % 2, :], in0=k.ps[:, 3 + 2 * (f % 2), :], scalar=1.0 / W_SCALE,
                                   in1=k.silu[:, f % 2, :], op0=ALU.mult, op1=ALU.mult).then_inc(s["f_prod"], 1)
        if f:
            gate(e, s["f_hi"], nth(i, n, FB, f), s["gates"])
            e.tensor_tensor(k.act_lo[:, f - 1, :], k.prod[:, (f - 1) % 2, :], k.act_hi[:, f - 1, :], ALU.subtract)\
                .then_inc(s["f_lo"], 1)
    after()
    for u in range(TPC):
        gate(e, s["f_down"], nth(i, n, TPC, u + 1), s["gates"])
        xt = k.x[:, bass.ds(i * TPC + u, 1), :].squeeze(1)
        e.scalar_tensor_tensor(out=xt, in0=k.ps[:, DOWN_BANK[u], :], scalar=0.5 / (W_SCALE * A_SCALE), in1=xt,
                               op0=ALU.mult, op1=ALU.add).then_inc(s["f_out"], 1)
    gate(e, s["f_out"], nth(i, n, TPC, TPC), s["gates"])


def ffn_phase_tensor(k, pe, n, m, routed):
    def before(i):
        if routed:
            apply_tensor(k, pe, i, 1 + NCH)

    before(0)
    norm_tensor(k, pe, 0, m)
    with pe.Fori(0, NCH - 1) as i:
        ffn_tensor(k, pe, i, n, lambda: before(i + 1))
        norm_tensor(k, pe, i + 1, m)
    ffn_tensor(k, pe, NCH - 1, n, lambda: None)


def ffn_phase_scalar(k, e, n, m, routed):
    def before(i):
        if routed:
            apply_scalar(k, e, i, 1 + NCH)
        norm_scalar(k, e, i, m)

    before(0)
    with e.Fori(0, NCH - 1) as i:
        ffn_scalar(k, e, i, n)
        before(i + 1)
    ffn_scalar(k, e, NCH - 1, n)


def ffn_phase_vector(k, V, n, m, routed):
    e = V.eng

    def before(i):
        if routed:
            apply_vector(k, V, i, 1 + NCH)
        norm_stats_vector(k, V, i, m)

    steps = NORM_STEPS + (APPLY_STEPS if routed else 0)
    V.enter(0, steps)
    before(0)
    V.leave(1)
    norm_low_vector(k, 0, m, e)
    with e.Fori(0, NCH - 1) as i:
        V.enter(i, steps)
        ffn_vector(k, V, i, n, lambda: before(i + 1))
        norm_low_vector(k, i + 1, m, e)
    V.leave(NCH - 1)
    ffn_vector(k, V, NCH - 1, n, lambda: None)



COMPS = 16
Q_SCALE = 16.0
SCORE = float(32 ** -0.5) / (Q_SCALE * Q_SCALE)
L1_INIT = 0.8 - 0.6 * float(np.exp(-0.3 * 12))


def c_setup_vector(k, V):
    s, e = k.s, V.eng
    V.link(e.tensor_copy(k.causal_ts, k.c["causal"]))
    e.wait_ge(s["c_mask"], 1)
    V.link(e.tensor_copy(k.causal_st, k.ps[:, 7, 0:P]))
    V.link(e.tensor_copy(k.identb, k.c["ident"]))
    V.link(e.tensor_copy(k.sel, bcast(k.c["pick"].unsqueeze(2), [P, 16, P])))
    V.link(e.memset(k.v1, 1.0))
    e.wait_ge(s["c_lam_in"], 80)
    rows = k.o1[:, 0, 0:128].rearrange("p (a d) -> p a d", a=4)
    prod = k.o1[:, 0, 128:192].rearrange("p (a d) -> p a d", a=2)
    V.link(e.tensor_tensor(prod, rows[:, 0:4:2, :], rows[:, 1:4:2, :], ALU.mult))
    e.tensor_reduce(k.lam[:, 0:2], prod, AXX, ALU.add).then_inc(s["c_lam_dot"], 1)
    e.wait_ge(s["c_lam_exp"], 1)
    V.link(e.tensor_tensor(k.lam[:, 4:5], k.lam[:, 2:3], k.lam[:, 3:4], ALU.subtract))
    V.link(e.tensor_scalar(k.lam[:, 4:5], k.lam[:, 4:5], L1_INIT, None, ALU.add))
    e.tensor_scalar(k.g, k.g, (1.0 - L1_INIT) * A_SCALE, None, ALU.mult).then_inc(s["c_set"], 1)
    e.wait_ge(s["c_set"], 1)


def c_tensor(k, pe, i):
    s = k.s
    norm_tensor(k, pe, i, 1 + 2 * NCH)
    ht = (k.ht_hi, k.ht_lo)
    w1 = (k.w1_hi, k.w1_lo)

    def weight(m, cols):
        return [(lambda c, w=w: w[:, m, c, cols]) for w in w1]

    for b in range(TPC):
        for q in range(2):
            z = 2 * b + q
            gate(pe, s["c_qk_lo"], nth(i, 1, 8, z + 1), s["gates"])
            pairs_product(pe, k.ps[:, z % 2, :], weight(q, slice(b * P, b * P + P)),
                          [of(h, slice(0, CH)) for h in ht]).then_inc(s["c_qk_done"], 1)
        gate(pe, s["c_qk_lo"], nth(i, 1, 8, 2 * b + 4), s["gates"])
        for a in range(4 * b, 4 * b + 4):
            r = slice(32 * (a % 4), 32 * (a % 4) + 32)
            if a:
                gate(pe, s["c_max"], nth(i, 1, 64, TPC * a - 2), s["gates"])
            for u in range(TPC):
                g, w = TPC * a + u, (u + 1) * P
                bank = 2 + g % 6
                pe.matmul(k.ps[:, bank, 0:w], k.qk_hi[r, b, u * P:w], k.qk_hi[r, 4 + b, 0:w], start=True, stop=False)
                pe.matmul(k.ps[:, bank, w - P:w], k.identb, k.causal_ts, start=False, stop=True)\
                    .then_inc(s["c_score"], 1)
    for u in range(TPC):
        gate(pe, s["c_v_in"], nth(i, 1, TPC, u + 1), s["gates"])
        pairs_product(pe, k.ps[:, u % 2, :], [of(h, slice(u * P, u * P + P)) for h in ht],
                      weight(2, slice(0, HID))).then_inc(s["c_v_done"], 1)
    gate(pe, s["c_v_in"], nth(i, 1, TPC, 6), s["gates"])
    gate(pe, s["c_negmax"], i + 1, s["gates"])
    for u in range(TPC):
        ins = pe.transpose(k.ps[:, 4, u * P:(u + 1) * P], k.nm[:, u].rearrange("p r c -> p (r c)"), k.c["ident"])
    ins.then_inc(s["c_max_turned"], 1)
    gate(pe, s["c_maxt"], i + 1, s["gates"])
    for a in range(COMPS + 2):
        if a < COMPS:
            b, r = a // 4, slice(32 * (a % 4), 32 * (a % 4) + 32)
            for v in range(TPC):
                g = TPC * a + v
                if g >= 4:
                    gate(pe, s["c_exp"], nth(i, 1, 64, g - 3), s["gates"])
                out = k.ps[:, g % 4, v * P:CH]
                keys, queries = slice(v * P, v * P + P), slice(v * P, CH)
                pe.matmul(out, k.sel[r, a, :], k.maxt[r, queries], start=True, stop=False)
                pe.matmul(k.ps[:, g % 4, keys], k.identb, k.causal_st, start=False, stop=False)
                for x, y in ((k.qk_hi, k.qk_hi), (k.qk_hi, k.qk_lo), (k.qk_lo, k.qk_hi)):
                    ins = pe.matmul(out, x[r, 4 + b, keys], y[r, b, queries], start=False, stop=(x is k.qk_lo))
                ins.then_inc(s["c_scored"], 1)
        z = a - 1
        if 0 <= z < COMPS:
            gate(pe, s["c_exp"], nth(i, 1, 64, TPC * a), s["gates"])
            if z >= 2:
                gate(pe, s["c_oo"], nth(i, 1, COMPS, z - 1), s["gates"])
            for v in range(TPC):
                ins = pe.matmul(k.ps[0:65, 4 + z % 2, v * P:CH], k.v1[:, v, (z // 2) * 65:(z // 2) * 65 + 65],
                                k.pt[:, z % 2, v, v * P:CH], start=(v == 0), stop=(v == TPC - 1))
            ins.then_inc(s["c_av"], 1)
        z = a - 2
        if z >= 0:
            gate(pe, s["c_oo"], nth(i, 1, COMPS, z + 1), s["gates"])
            if z % 2 == 0 and z:
                gate(pe, s["c_head"], nth(i, 1, 8, z // 2), s["gates"])
            for u in range(TPC):
                ins = pe.transpose(k.ps[:, 6 + z % 2, 65 * u:65 * u + 65], k.oo[:, z % 2, u * P:(u + 1) * P],
                                   k.c["ident"][0:65, 0:65])
            ins.then_inc(s["c_back"], 1)
    gate(pe, s["c_o"], i + 1, s["gates"])
    for c in range(KC):
        if c >= 2:
            gate(pe, s["c_ot_lo"], nth(i, 1, KC, c - 1), s["gates"])
        for u in range(TPC):
            ins = pe.transpose(k.ps[:, c % 2, u * P:(u + 1) * P], k.o1[:, u, c * P:(c + 1) * P], k.c["ident"])
        ins.then_inc(s["c_ot"], 1)
    gate(pe, s["c_ot_lo"], nth(i, 1, KC, KC), s["gates"])
    for u in range(TPC):
        gate(pe, s["c_out"], nth(i, 1, TPC, u + 1), s["gates"])
        pairs_product(pe, k.ps[:, 2 + u % 2, :], [of(h, slice(u * P, u * P + P)) for h in ht],
                      weight(3, slice(0, HID))).then_inc(s["c_out_done"], 1)


def c_scalar(k, e, i):
    s = k.s
    norm_scalar(k, e, i, 1 + 2 * NCH)
    for z in range(8):
        gate(e, s["c_qk_done"], nth(i, 1, 8, z + 1), s["gates"])
        e.activation(k.qk_hi[:, z // 2 + 4 * (z % 2), :], k.ps[:, z % 2, :], ACT.Copy, scale=Q_SCALE / (W_SCALE * A_SCALE))\
            .then_inc(s["c_qk_hi"], 1)
    gate(e, s["c_max_turned"], i + 1, s["gates"])
    e.activation(k.maxt, k.ps[:, 4, :], ACT.Copy).then_inc(s["c_maxt"], 1)
    for a in range(COMPS):
        if a >= 2:
            gate(e, s["c_av"], nth(i, 1, COMPS, a - 1), s["gates"])
        for v in range(TPC):
            g = TPC * a + v
            gate(e, s["c_scored"], nth(i, 1, 64, g + 1), s["gates"])
            e.activation(k.pt[:, a % 2, v, v * P:CH], k.ps[:, g % 4, v * P:CH], ACT.Exp, scale=SCORE)\
                .then_inc(s["c_exp"], 1)
    gate(e, s["c_ms"], i + 1, s["gates"])
    e.activation(k.rms, k.mx2, ACT.Sqrt).then_inc(s["c_rms"], 1)
    for c in range(KC):
        gate(e, s["c_ot"], nth(i, 1, KC, c + 1), s["gates"])
        e.activation(k.ht_hi[:, c, :], k.ps[:, c % 2, :], ACT.Copy).then_inc(s["c_ot_hi"], 1)


C_STEPS = 2 + 8 * 4 + 9


def c_vector(k, V, i):
    s, e = k.s, V.eng
    norm_vector(k, V, i, 1 + 2 * NCH)
    for b in range(TPC):
        for q in range(2):
            z, to = 2 * b + q, b + 4 * q
            gate(e, s["c_qk_hi"], nth(i, 1, 8, z + 1), s["gates"])
            e.scalar_tensor_tensor(out=k.qk_lo[:, to, :], in0=k.ps[:, z % 2, :], scalar=Q_SCALE / (W_SCALE * A_SCALE),
                                   in1=k.qk_hi[:, to, :], op0=ALU.mult, op1=ALU.subtract).then_inc(s["c_qk_lo"], 1)
        for g in range(16 * b, 16 * b + 16):
            a, u = g // 4, g % 4
            gate(e, s["c_score"], nth(i, 1, 64, g + 1), s["gates"])
            e.tensor_reduce(k.mx[:, u, a:a + 1], k.ps[:, 2 + g % 6, 0:(u + 1) * P], AXX, ALU.max)\
                .then_inc(s["c_max"], 1)
    gate(e, s["c_max"], nth(i, 1, 64, 64), s["gates"])
    V.link(e.tensor_scalar(k.nmb, k.mx, -1.0, None, ALU.mult))
    V.link(e.tensor_tensor(k.mx, k.mx, k.nmb, ALU.add))
    for q in range(4):
        e.tensor_copy(k.nm[:, :, q, 0:16], k.nmb)
        ins = e.tensor_scalar(k.nm[:, :, q, 16:32], k.mx, -1.0, None, ALU.mult)
    ins.then_inc(s["c_negmax"], 1)
    for u in range(TPC):
        gate(e, s["c_v_done"], nth(i, 1, TPC, u + 1), s["gates"])
        e.tensor_scalar(k.v1[:, u, :].rearrange("p (h d) -> p h d", d=65)[:, :, 0:64],
                        k.ps[:, u % 2, :].rearrange("p (h d) -> p h d", d=64),
                        1.0 / (W_SCALE * A_SCALE), None, ALU.mult).then_inc(s["c_v_in"], 1)
    for z in range(COMPS + 1):
        if z < COMPS:
            gate(e, s["c_av"], nth(i, 1, COMPS, z + 1), s["gates"])
            if z >= 2:
                gate(e, s["c_back"], nth(i, 1, COMPS, z - 1), s["gates"])
            e.tensor_copy(k.oo[:, z % 2, :], k.ps[0:65, 4 + z % 2, :]).then_inc(s["c_oo"], 1)
        if z and z % 2 == 0:
            gate(e, s["c_back"], nth(i, 1, COMPS, z), s["gates"])
            o = [k.ps[:, 6 + q, 0:260].rearrange("p (u d) -> p u d", d=65) for q in range(2)]
            cols = slice((z // 2 - 1) * 64, z // 2 * 64)
            r = k.rs
            for q in range(2):
                ins = e.reciprocal(r[:, q, :], o[q][:, :, 64])
            V.link(ins)
            V.link(e.tensor_scalar(r[:, 1, :], r[:, 1, :], k.lam[:, 4:5], None, ALU.mult))
            V.link(e.tensor_tensor(k.o1[:, :, cols], o[0][:, :, 0:64], bcast(r[:, 0, :].unsqueeze(2), [P, TPC, 64]),
                                   ALU.mult))
            V.link(e.tensor_tensor(k.h[:, :, cols], o[1][:, :, 0:64], bcast(r[:, 1, :].unsqueeze(2), [P, TPC, 64]),
                                   ALU.mult))
            e.tensor_tensor(k.o1[:, :, cols], k.o1[:, :, cols], k.h[:, :, cols], ALU.subtract)\
                .then_inc(s["c_head"], 1)
    gate(e, s["c_head"], nth(i, 1, 8, 8), s["gates"])
    V.link(e.tensor_tensor(k.h, k.o1, k.o1, ALU.mult))
    V.link(e.tensor_reduce(k.mx2, k.h.rearrange("p u (h d) -> p (u h) d", d=64), AXX, ALU.add))
    e.tensor_scalar(k.mx2, k.mx2, 1.0 / 64, 1e-5, ALU.mult, ALU.add).then_inc(s["c_ms"], 1)
    gate(e, s["c_rms"], i + 1, s["gates"])
    rsqrt_vector(V, k.rr, k.rms, k.mx2, k.rr2)
    heads = k.o1.rearrange("p u (h d) -> p (u h) d", d=64)
    V.link(e.tensor_tensor(heads, heads, bcast(k.rr.unsqueeze(2), [P, 32, 64]), ALU.mult))
    V.link(e.tensor_tensor(heads, heads, bcast(k.g.unsqueeze(1), [P, 32, 64]), ALU.mult))
    e.sem_inc(s["c_o"], 1)
    for c in range(KC):
        gate(e, s["c_ot_hi"], nth(i, 1, KC, c + 1), s["gates"])
        e.tensor_tensor(k.ht_lo[:, c, :], k.ps[:, c % 2, :], k.ht_hi[:, c, :], ALU.subtract).then_inc(s["c_ot_lo"], 1)
    for u in range(TPC):
        gate(e, s["c_out_done"], nth(i, 1, TPC, u + 1), s["gates"])
        xt = k.x[:, bass.ds(i * TPC + u, 1), :].squeeze(1)
        e.scalar_tensor_tensor(out=xt, in0=k.ps[:, 2 + u % 2, :], scalar=1.0 / (W_SCALE * A_SCALE), in1=xt,
                               op0=ALU.mult, op1=ALU.add).then_inc(s["c_out"], 1)
    gate(e, s["c_out"], nth(i, 1, TPC, 6), s["gates"])


def bass_macaron(nc, d):
    with ExitStack() as ctx:
        ctx.enter_context(nc.allow_non_contiguous_dma(reason="a few short vectors laid along the partitions"))
        k = Kernel()
        k.d = d
        place(k, nc, ctx)
        k.ps = ctx.enter_context(nc.psum_tensor("ps", [P, 8, 512], F32))
        k.s = {n: ctx.enter_context(nc.semaphore(n)) for n in SEMAPHORES}
        k.ones, k.diag = k.rows[0:NTILE, 3, 0:P], k.rows[0:NTILE, 0, :]
        k.wdt_hi = k.wt_hi.rearrange("p c (b m) -> p (c b) m", m=P)
        k.wdt_lo = k.wt_lo.rearrange("p c (b m) -> p (c b) m", m=P)
        pairs = k.nat.rearrange("p a b -> p (a b)").bitcast(F16).rearrange("p (n c m) -> p n c m", n=4, m=P)
        k.wdo_hi, k.wdo_lo = [pairs[:, 0], pairs[:, 1]], [pairs[:, 2], pairs[:, 3]]
        s = k.s
        block = ctx.enter_context(nc.Block())

        def load_down(sp):
            for dst, src in ((k.wd_hi, d["wd_hi"]), (k.wd_lo, d["wd_lo"])):
                sp.dma_start(dst, src).then_inc(s["down_in"], 16)

        @block.sync
        def _(sp):
            setup_sync(k, sp)
            sp.wait_ge(s["wdo_out0"], 64)
            sp.wait_ge(s["wdo_out1"], 64)
            sp.wait_ge(s["w1_out"], 128)
            sp.wait_ge(s["rt_zeroed"], 1)
            for j in range(8):
                sp.dma_start(k.rt[32 * (j // 2):32 * (j // 2) + 32, 16 * j:16 * j + 16],
                             d["L0_attn_rand_matrix"].rearrange("e d -> d e")).then_inc(s["b_in"], 16)
            sp.dma_start(k.bv, d["L0_attn_bv"].partition_broadcast(P)).then_inc(s["b_in"], 16)
            sp.dma_start(k.bo, d["L0_attn_bo"].partition_broadcast(P)).then_inc(s["b_in"], 16)
            with sp.Fori(0, NCH) as i:
                b_sync(k, sp, i)
            sp.wait_ge(s["table_ready"], 2)
            load_down(sp)
            sp.wait_ge(s["f_out"], NT)
            for m in range(4):
                sp.dma_start(k.w1_hi[:, m], d["w1_hi"][m]).then_inc(s["c_in"], 16)
                sp.dma_start(k.w1_lo[:, m], d["w1_lo"][m]).then_inc(s["c_in"], 16)
            for m, name in enumerate(["lambda_q1", "lambda_k1", "lambda_q2", "lambda_k2"]):
                sp.dma_start(k.o1[:, 0, 32 * m:32 * m + 32], d["L1_attn_" + name].partition_broadcast(P))\
                    .then_inc(s["c_lam_in"], 16)
            sp.dma_start(k.g, d["L1_attn_g"].partition_broadcast(P)).then_inc(s["c_lam_in"], 16)
            sp.wait_ge(s["c_out"], 2 + NT)
            load_down(sp)
            for c in range(NCH):
                sp.wait_ge(s["f_out"], NT + TPC * (c + 1))
                sp.dma_start(d["out"][c].rearrange("(u p) n -> p u n", p=P),
                             k.x[:, c * TPC:(c + 1) * TPC, :]).then_inc(s["x_out"], 16)
            sp.wait_ge(s["x_out"], 16 * NCH)

        @block.gpsimd
        def _(pool):
            setup_pool(k, pool)
            with pool.Fori(0, NCH) as i:
                b_pool(k, pool, i)

        @block.tensor
        def _(pe):
            use_work(k, k.work, k.h)
            setup_tensor(k, pe)
            minmax_tensor(k, pe, 1, "")
            pe.wait_ge(s["b_in"], 160)
            with pe.Fori(0, NCH) as i:
                b_tensor(k, pe, i)
            minmax_tensor(k, pe, 2, "")
            use_work(k, k.work1, k.h)
            pe.wait_ge(s["down_in"], 32)
            ffn_phase_tensor(k, pe, 1, 1 + NCH, True)
            pe.wait_ge(s["f_out"], NT)
            pe.transpose(k.ps[:, 7, 0:P], k.c["causal"], k.c["ident"]).then_inc(s["c_mask"], 1)
            pe.wait_ge(s["c_in"], 128)
            pe.wait_ge(s["c_set"], 1)
            with pe.Fori(0, NCH) as i:
                c_tensor(k, pe, i)
            pe.wait_ge(s["down_in"], 64)
            ffn_phase_tensor(k, pe, 1 + NCH, 1 + 3 * NCH, False)

        @block.scalar
        def _(act):
            use_work(k, k.work, k.h)
            setup_scalar(k, act)
            first_scalar(k, act, 1, "")
            with act.Fori(0, NCH) as i:
                b_scalar(k, act, i)
                token_stats_scalar(k, act, i, 1 + NCH, "")
            use_work(k, k.work1, k.h)
            ffn_phase_scalar(k, act, 1, 1 + NCH, True)
            act.wait_ge(s["c_lam_dot"], 1)
            act.activation(k.lam[:, 2:4], k.lam[:, 0:2], ACT.Exp).then_inc(s["c_lam_exp"], 1)
            with act.Fori(0, NCH) as i:
                c_scalar(k, act, i)
            ffn_phase_scalar(k, act, 1 + NCH, 1 + 3 * NCH, False)

        @block.vector
        def _(dve):
            use_work(k, k.work, k.h)
            V = Steps(dve, s["v_step"], s["gates"])
            for name in ("n_lo", "b_qf", "b_rope", "b_v_in", "b_y", "b_mask", "b_ot_lo", "f_prod", "c_qk_lo", "c_v_in", "c_out"):
                dve.sem_inc(s[name], 2)
            setup_vector_first(k, V)
            setup_vector_rest(k, V)
            first_vector(k, V, 1, "")
            minmax_vector(k, V, 1, "")
            V.link(dve.memset(k.acc, -BIG))
            dve.wait_ge(s["b_in"], 160)
            V.link(dve.tensor_copy(k.spread.rearrange("p (h f) -> p h f", f=32),
                                   bcast(k.c["ident"][0:24, 0:24].unsqueeze(2), [24, 24, 32])))
            with dve.Fori(0, NCH) as i:
                V.enter(i, APPLY_STEPS + NORM_STEPS + B_STEPS + STATS_STEPS + ROUTE_STEPS)
                b_vector(k, V, i)
                token_stats_vector(k, V, i, 1 + NCH, "")
                routing_vector(k, V, i, 1 + NCH, "")
            V.leave(NCH)
            minmax_vector(k, V, 2, "")
            use_work(k, k.work1, k.h)
            ffn_phase_vector(k, V, 1, 1 + NCH, True)
            c_setup_vector(k, V)
            with dve.Fori(0, NCH) as i:
                V.enter(i, NORM_STEPS + C_STEPS)
                c_vector(k, V, i)
            V.leave(NCH)
            ffn_phase_vector(k, V, 1 + NCH, 1 + 3 * NCH, False)


_INS = ["L0_attn_hidden_states", "L0_attn_Wq", "L0_attn_bq", "L0_attn_Wk", "L0_attn_bk", "L0_attn_Wv",
        "L0_attn_bv", "L0_attn_Wo", "L0_attn_bo", "L0_attn_rand_matrix", "L0_ffn_ln_gamma", "L0_ffn_ln_beta",
        "L0_ffn_spline_bases", "L0_ffn_spline_slopes", "L0_ffn_output_scale", "L1_attn_Wq", "L1_attn_Wk",
        "L1_attn_Wv", "L1_attn_Wo", "L1_attn_lambda_q1", "L1_attn_lambda_k1", "L1_attn_lambda_q2",
        "L1_attn_lambda_k2", "L1_attn_g", "L1_ffn_SU_ug", "L1_ffn_SU_dp", "L1_ffn_Wscale_ug",
        "L1_ffn_Wscale_dp", "L1_ffn_W_up", "L1_ffn_W_gate", "L1_ffn_W_down"]


def kernel(**inputs):
    import numpy as _np
    import concourse.bacc as _bacc
    from concourse import mybir as _mybir
    from concourse.bass_utils import run_bass_kernel_spmd as _run

    nc = _bacc.Bacc("TRN2", target_bir_lowering=False, num_devices=1, dynamic_dma_scratch_size=1024)
    arrays, d = {}, {}
    for name in _INS:
        a = _np.ascontiguousarray(inputs[name])
        arrays[f"in_{name}_dram"] = a
        d[name] = nc.dram_tensor(f"in_{name}_dram", a.shape, _mybir.dt.from_np(a.dtype), kind="ExternalInput").ap()
    arrays["constants_dram"] = CONSTS
    d["constants"] = nc.dram_tensor("constants_dram", CONSTS.shape, F32, kind="ExternalInput").ap()
    for part in ("hi", "lo"):
        d["wd_" + part] = nc.dram_tensor(f"wd_{part}_dram", (P, FB, HID), F16).ap()
        d["w1_" + part] = nc.dram_tensor(f"w1_{part}_dram", (4, P, KC, HID), F16).ap()
    d["values"] = nc.dram_tensor("values_dram", (CH, 256), F32).ap()
    d["out"] = nc.dram_tensor("out_dram", (4, 512, 512), F32, kind="ExternalOutput").ap()
    bass_macaron(nc, d)
    r = _run(nc, [arrays], core_ids=[0])
    return r.results[0]["out_dram"]
```

```python
from contextlib import ExitStack

import numpy as np
import concourse.bass as bass
from concourse import mybir

ALU = mybir.AluOpType
ACT = mybir.ActivationFunctionType
AXX = mybir.AxisListType.X
F32 = mybir.dt.float32
F16 = mybir.dt.float16
BF16 = mybir.dt.bfloat16

P = 128
HID = 512
KC = HID // P
NTOK = 2048
NT = NTOK // P
CH = 512
NCH = NTOK // CH
TPC = CH // P
INTER = 2048
FB = INTER // P
NTILE, DSL, GRID = 64, 8, 16
CLUS = 8
LN_EPS = 1e-5
ARENA = 228096
W_SCALE = 1024.0
A_SCALE = 64.0
ROUND = float(1.5 * 2 ** 23)
BIG = 1.0e30


def host_constants():
    r = np.arange(P)
    ident = np.eye(P, dtype=np.float32)
    had = np.array([[1.0 - 2.0 * (bin(a & b).count("1") & 1) for b in range(P)] for a in range(P)], np.float32)
    rot = np.zeros((P, P), np.float32)
    for m in range(P):
        if m % 32 < 16:
            rot[m + 16, m] = -1.0
        else:
            rot[m - 16, m] = 1.0
    inv = (1.0 / (np.float32(10000.0) ** (np.arange(0, 32, 2, dtype=np.float32) / np.float32(32)))).astype(np.float32)
    ang = (np.arange(CH, dtype=np.float32)[None, :] * inv[(r % 16)][:, None]).astype(np.float32)
    t = np.arange(NTILE)
    key = np.broadcast_to(((7 - t // 8) * 256 + (7 - t % 8)).astype(np.float32), (P, NTILE))
    iota = np.broadcast_to(np.arange(GRID, dtype=np.float32), (P, GRID))
    causal = np.where(r[None, :] > r[:, None], np.float32(-1e30), np.float32(0.0)).astype(np.float32)
    pick = (r[:, None] % 16 == np.arange(16)[None, :]).astype(np.float32)
    headpad = (r[:, None] // 32 + 20 == np.arange(44)[None, :]).astype(np.float32)
    same = (r[:, None] // 8 == np.arange(16)[None, :]).astype(np.float32)
    phase = np.where(r % 32 < 16, np.float32(0.0), np.float32(0.25)).astype(np.float32)[:, None]
    phase2pi = (phase * np.float32(2 * np.pi)).astype(np.float32)
    parts = [("ident", ident), ("had", had), ("rot", rot), ("cos", np.cos(ang)),
             ("sin", np.sin(ang)), ("key", key), ("iota", iota), ("causal", causal),
             ("pick", pick), ("headpad", headpad), ("same", same), ("phase", phase),
             ("phase2pi", phase2pi)]
    where, at = {}, 0
    for name, a in parts:
        where[name] = (at, at + a.shape[1])
        at += a.shape[1]
    return np.ascontiguousarray(np.concatenate([a for _, a in parts], axis=1).astype(np.float32)), where


CONSTS, CONST_AT = host_constants()

SEMAPHORES = """
const_in x_in param_in gates
nat_in0 nat_in1 nat_scaled nat_turned wt_hi wt_lo had_done had_hi had_lo
wd_in wd_scaled wd_mixed wd_step wdt_turned wdt_hi wdt_lo wdh_done wdo_hi wdo_lo wdo_out0 wdo_out1
ssum_ready ss_signed ss_diag ss_spread ss_row up_scale
v_step
var1 std1 var2 std2 norm z_scaled y_half y_ready y_signed routed
minmax_turned table_ready rt_zeroed b_in down_in
ap_oh ap_turned ap_oht ap_rows ap_read
n_var n_std n_norm n_h n_turned n_hi n_lo
b_v_done b_v_in b_v_out b_vr b_qk_done b_qf b_cos b_rot b_rope b_sq b_nsum b_n2 b_n b_r b_proj b_p b_spread b_y b_whole
b_reduced b_feat b_f_hi b_f_lo b_ks b_ksg b_qs b_s b_mask b_pv b_ot_hi b_ot_lo b_out b_res
f_gate f_up f_silu f_prod f_hi f_lo f_down f_out
c_in c_in_qk c_w_hi c_w_lo c_lam_in c_lam_dot c_lam_exp c_mask c_set c_qk_done c_qk c_qk_hi c_qk_lo c_v_done c_v_in c_score c_max c_negmax
c_max_turned c_maxt c_scored c_exp c_av c_oo c_back c_head c_ms c_rms c_o c_ot c_ot_hi c_ot_lo c_out_done c_out
x_out
""".split()


class Views:

    def __init__(self, arena):
        self.arena = arena

    def at(self, byte, shape, dt):
        size = 1
        for n in shape[1:]:
            size *= n
        width = 4 if dt == F32 else 2
        words = size * width // 4
        assert byte % 4 == 0 and size * width % 4 == 0
        v = self.arena[0:shape[0], byte // 4:byte // 4 + words]
        if dt != F32:
            v = v.bitcast(dt)
        if len(shape) == 3:
            v = v.rearrange("p (a b) -> p a b", a=shape[1])
        if len(shape) == 5:
            v = v.rearrange("p (a b c d) -> p a b c d", a=shape[1], b=shape[2], c=shape[3])
        if len(shape) == 4:
            v = v.rearrange("p (a b c) -> p a b c", a=shape[1], b=shape[2])
        return v, byte + size * width


class Steps:

    def __init__(self, eng, sem, gates):
        self.eng, self.sem, self.gates = eng, sem, gates
        self.base, self.i, self.per, self.k = 0, 0, 0, 0

    def enter(self, i, per):
        self.i, self.per, self.k = i, per, 0

    def leave(self, n):
        assert self.k == self.per, (self.k, self.per)
        self.base, self.i, self.per, self.k = self.base + n * self.per, 0, 0, 0

    def link(self, ins):
        self.k += 1
        ins.then_inc(self.sem, 1)
        value = self.base + self.i * self.per + self.k if self.per else self.base + self.k
        if not self.per:
            self.base, self.k = self.base + self.k, 0
        gate(self.eng, self.sem, value, self.gates)


def gate(eng, sem, value, gates):
    eng.wait_ge(sem, value)
    if not isinstance(value, int):
        eng.sem_inc(gates, 1)


def phase_buffers(k, v):
    at = k.free_at
    k.h, at = v.at(at, [P, TPC, HID], F32)
    k.ht_hi, at = v.at(at, [P, KC, CH], F16)
    k.ht_lo, at = v.at(at, [P, KC, CH], F16)
    a = at
    k.work, _ = v.at(a, [P, 4096], F32)
    k.f_hi, b = v.at(a, [P, 6, CH], F16)
    k.f_lo, b = v.at(b, [P, 6, CH], F16)
    k.qf, a = v.at(a, [P, 6, CH], F32)
    k.qs, _ = v.at(a, [P, 16, CH], F16)
    k.qr, a = v.at(a, [P, 6, CH], F32)
    k.q2, a = v.at(a, [P, 2, CH], F32)
    k.y2, _ = v.at(a, [P, TPC, HID], F32)
    k.ks, a = v.at(a, [P, 8, CH], F16)
    k.masked2, _ = v.at(a, [P, 2048], F32)
    k.ksg, _ = v.at(a, [P, 32, P], F16)
    k.ang, a = v.at(a, [P, 2, CH], F32)
    k.turns, a = v.at(a, [P, 2, CH], F32)
    k.nr, a = v.at(a, [P, 4, CH], F32)
    k.sm, a = v.at(a, [P, 2, 2, 16, 16], F32)
    k.spread, a = v.at(a, [24, 6 * P], F32)
    k.bv, a = v.at(a, [P, 256], F32)
    k.bo, a = v.at(a, [P, HID], F32)
    assert a <= ARENA, a
    k.v0, b = v.at(k.free_at, [P, TPC, 256], F32)
    k.vr, b = v.at(b, [P, 32, 32], F32)
    a = at
    k.wd_hi, a = v.at(a, [P, FB, HID], F16)
    k.wd_lo, a = v.at(a, [P, FB, HID], F16)
    k.act_hi, a = v.at(a, [P, FB, CH], F16)
    k.act_lo, a = v.at(a, [P, FB, CH], F16)
    assert a <= ARENA, a
    b = k.w0_at
    k.silu, b = v.at(b, [P, 2, CH], F32)
    k.prod, b = v.at(b, [P, 2, CH], F32)
    k.work1, b = v.at(b, [P, 4096], F32)
    assert b <= k.free_at
    a = at
    k.w1_hi, a = v.at(a, [P, 4, KC, HID], F16)
    k.w1_lo, a = v.at(a, [P, 4, KC, HID], F16)
    k.qk_hi, a = v.at(a, [P, 8, CH], F16)
    k.qk_lo, a = v.at(a, [P, 8, CH], F16)
    k.w1_nat = [v.at(byte, [P, KC, HID], F32)[0] for byte in (k.w0_at + 8192, k.w0_at + 16384, a, a + 8192)]
    k.v1, a = v.at(a, [P, TPC, 8 * 65], F32)
    k.o1, a = v.at(a, [P, TPC, HID], F32)
    k.o2, a = v.at(a, [P, TPC, 64], F32)
    assert a <= ARENA, a
    b = k.w0_at
    k.pt, b = v.at(b, [P, 2, TPC, CH], F32)
    k.nm, _ = v.at(b, [P, TPC, 4, 32], F32)
    k.oo, b = v.at(b, [65, 2, CH], F32)
    k.sel, b = v.at(b, [P, 16, P], BF16)
    assert b <= k.free_at
    b = k.onehot_at
    k.maxt, b = v.at(b, [P, CH], BF16)
    k.causal_ts, b = v.at(b, [P, P], BF16)
    k.causal_st, b = v.at(b, [P, P], BF16)
    k.identb, b = v.at(b, [P, P], BF16)
    k.nmb, b = v.at(b, [P, TPC, 16], BF16)
    k.mx, b = v.at(b, [P, TPC, 16], F32)
    k.g, b = v.at(b, [P, 64], F32)
    assert b <= k.onehot_at + 4096


def use_rows(k, work, y):
    k.y = y
    k.masked = work[:, 0:2048].rearrange("p (u c) -> p u c", u=TPC)
    k.sg = work[:, 1024:2048].bitcast(BF16).rearrange("p (u c) -> p u c", u=TPC)


def use_work(k, work, y, splines):
    use_rows(k, work, y)
    k.scat = k.masked
    k.oh4 = splines[:, 0:256].rearrange("p (u t) -> p u t", u=TPC)
    k.oht = splines[0:NTILE, 256:768]
    k.m16 = splines[:, 768:1280].rearrange("p (u j g) -> p u j g", u=TPC, j=DSL)
    k.m16p = splines[:, 1280:1792].rearrange("p (u j g) -> p u j g", u=TPC, j=DSL)


class Kernel:
    pass


def bcast(ap, shape):
    return ap.to_broadcast(shape)


def place(k, nc, ctx):
    arena = ctx.enter_context(nc.sbuf_tensor("arena", [P, ARENA // 4], F32))
    v = Views(arena)
    at = 0
    k.x, at = v.at(at, [P, NT, HID], F32)
    k.const, at = v.at(at, [P, CONSTS.shape[1]], F32)
    k.onehot_at = at
    k.onehot, at = v.at(at, [P, NT, NTILE], F32)
    k.sliced, at = v.at(at, [P, NT, DSL], F32)
    k.mr, at = v.at(at, [P, NT, 2], F32)
    k.gamma, at = v.at(at, [P, HID], F32)
    k.beta, at = v.at(at, [P, HID], F32)
    k.ssrow, at = v.at(at, [P, HID], BF16)
    k.table, at = v.at(at, [NTILE, 260], F32)
    k.small, at = v.at(at, [P, 704], F32)
    k.rt, at = v.at(at, [P, P], F32)
    k.signs, at = v.at(at, [P, 2, P], F16)
    k.wug_hi, at = v.at(at, [P, KC, 2 * INTER], F16)
    k.wug_lo, at = v.at(at, [P, KC, 2 * INTER], F16)
    k.w0_at = at
    k.w0_hi, at = v.at(at, [P, KC, 1536], F16)
    k.w0_lo, at = v.at(at, [P, KC, 1536], F16)
    k.free_at = at
    c = {n: k.const[:, a:b] for n, (a, b) in CONST_AT.items()}
    k.c = c
    a, b = CONST_AT["cos"][0], CONST_AT["sin"][1]
    k.qk32 = k.const[:, a:b].rearrange("p (a t) -> p a t", a=2)
    a = k.free_at
    k.wd_nat, a = v.at(a, [P, 4, INTER], F32)
    k.wd_tmp, a = v.at(a, [P, INTER], F32)
    k.nat, a = v.at(a, [P, 8, HID], F32)
    k.wt_hi, a = v.at(a, [P, KC, HID], F16)
    k.wt_lo, a = v.at(a, [P, KC, HID], F16)
    k.rows, a = v.at(a, [P, TPC, HID], F32)
    k.rows2, a = v.at(a, [P, 2048], F32)
    assert a <= ARENA, a
    s = k.small
    phase_buffers(k, v)
    k.stats6 = s[:, 0:24].rearrange("p (u c) -> p u c", c=6)
    k.mv = s[:, 24:32].rearrange("p (u c) -> p u c", c=2)
    k.t4 = [s[:, 32 + 4 * n:36 + 4 * n] for n in range(7)]
    k.clus = s[:, 60:92].rearrange("p (u c) -> p u c", c=CLUS)
    k.kmax = s[:, 92:96]
    k.ends = s[:, 96:104].rearrange("p (u a) -> p u a", a=2)
    k.acc = s[:, 104:232].rearrange("p (a t) -> p a t", a=2)
    k.wscale = s[:, 232:264]
    k.su_ug = s[:, 264:268]
    k.su_dp = s[:, 268:284]
    k.wscale_dp = s[:, 284:288]
    k.ssum = s[0:NTILE, 288:296]
    k.ssign = s[0:NTILE, 296:304]
    k.ends2 = s[0:NTILE, 304:306]
    k.bqk = s[:, 306:312]
    k.ap = [s[:, 320 + 32 * m:352 + 32 * m].rearrange("p (u j) -> p u j", j=DSL) for m in range(6)]
    k.cols = s[:, 512:524].rearrange("p (u c) -> p u c", c=3)
    k.lam = s[:, 620:628]
    k.rs = s[:, 628:636].rearrange("p (m u) -> p m u", m=2)
    k.mx2, k.rr, k.rr2, k.rms = [s[:, 320 + 32 * m:352 + 32 * m] for m in range(4)]
    k.had16 = k.signs[:, 0, :]
    k.had16n = k.signs[:, 1, :]
    return k


def rsqrt_vector(V, r, std, var, t):
    e = V.eng
    V.link(e.reciprocal(r, std))
    V.link(e.tensor_tensor(t, var, r, ALU.mult))
    V.link(e.scalar_tensor_tensor(out=t, in0=t, scalar=-0.5, in1=r, op0=ALU.mult, op1=ALU.mult))
    V.link(e.scalar_tensor_tensor(out=r, in0=t, scalar=1.5, in1=r, op0=ALU.add, op1=ALU.mult))


def nth(i, n, per, at):
    return i * per + ((n - 1) * per + at)


def token_stats_vector(k, V, i, n, p):
    s, e = k.s, V.eng
    for u in range(TPC):
        ins = e.bn_stats(k.stats6[:, u, :], k.x[:, bass.ds(i * TPC + u, 1), :].squeeze(1))
    V.link(ins)
    for u in range(TPC):
        ins = e.bn_aggr(k.mv[:, u, :], k.stats6[:, u, :])
    V.link(ins)
    ve, std, r, t, std2, r2, nm2 = k.t4
    mean, var = k.mv[:, :, 0], k.mv[:, :, 1]
    e.tensor_scalar(ve, var, LN_EPS, None, ALU.add).then_inc(s[p + "var1"], 1)
    gate(e, s[p + "std1"], i + n, s["gates"])
    rsqrt_vector(V, r, std, ve, t)
    V.link(e.tensor_tensor(t, var, r, ALU.mult))
    V.link(e.tensor_tensor(t, t, r, ALU.mult))
    e.tensor_scalar(ve, t, LN_EPS, None, ALU.add).then_inc(s[p + "var2"], 1)
    gate(e, s[p + "std2"], i + n, s["gates"])
    rsqrt_vector(V, r2, std2, ve, t)
    V.link(e.tensor_tensor(r2, r2, r, ALU.mult))
    mr = k.mr[:, bass.ds(i * TPC, TPC), :]
    V.link(e.tensor_copy(mr[:, :, 0], mean))
    V.link(e.tensor_copy(mr[:, :, 1], r))
    e.scalar_tensor_tensor(out=nm2, in0=mean, scalar=-1.0, in1=r2, op0=ALU.mult, op1=ALU.mult)\
        .then_inc(s[p + "norm"], 1)


def token_stats_scalar(k, e, i, n, p):
    s = k.s
    ve, std, r, t, std2, r2, nm2 = k.t4
    gate(e, s[p + "var1"], i + n, s["gates"])
    e.activation(std, ve, ACT.Sqrt).then_inc(s[p + "std1"], 1)
    gate(e, s[p + "var2"], i + n, s["gates"])
    e.activation(std2, ve, ACT.Sqrt).then_inc(s[p + "std2"], 1)
    gate(e, s[p + "norm"], i + n, s["gates"])
    for u in range(TPC):
        ins = e.activation(k.y[:, u, :], k.x[:, bass.ds(i * TPC + u, 1), :].squeeze(1), ACT.Identity,
                           bias=nm2[:, u:u + 1], scale=r2[:, u:u + 1])
    ins.then_inc(s[p + "z_scaled"], 1)


def token_signs_scalar(k, e, i, n, p):
    s = k.s
    gate(e, s[p + "y_ready"], i + n, s["gates"])
    e.activation(k.sg, k.y, ACT.Sign).then_inc(s[p + "y_signed"], 1)


def routing_vector(k, V, i, n, p):
    routing_affine(k, V, i, n, p)
    routing_choice(k, V, i, n, p)
    routing_ends(k, V, i, n, p)


def routing_affine(k, V, i, n, p):
    s, e = k.s, V.eng
    full = [P, TPC, HID]
    gate(e, s[p + "z_scaled"], i + n, s["gates"])
    V.link(e.tensor_tensor(k.y, k.y, bcast(k.gamma.unsqueeze(1), full), ALU.mult))
    e.tensor_tensor(k.y, k.y, bcast(k.beta.unsqueeze(1), full), ALU.add).then_inc(s[p + "y_ready"], 1)


def routing_choice(k, V, i, n, p):
    s, e = k.s, V.eng
    full, tiles = [P, TPC, HID], [P, TPC, NTILE]
    gate(e, s[p + "y_signed"], i + n, s["gates"])
    V.link(e.tensor_tensor(k.sg, k.sg, bcast(k.ssrow.unsqueeze(1), full), ALU.mult))
    score = k.masked[:, 0, 0:256].rearrange("p (u t) -> p u t", u=TPC)
    key = k.masked[:, 1, 0:256].rearrange("p (u t) -> p u t", u=TPC)
    V.link(e.tensor_reduce(score, k.sg.rearrange("p u (t j) -> p u t j", j=DSL), AXX, ALU.add))
    V.link(e.tensor_reduce(k.clus, score.rearrange("p u (c t) -> p u c t", c=CLUS), AXX, ALU.add))
    V.link(e.scalar_tensor_tensor(out=key, in0=score, scalar=8.0, in1=bcast(k.c["key"].unsqueeze(1), tiles),
                                  op0=ALU.mult, op1=ALU.add))
    for u in range(TPC):
        ins = e.scalar_tensor_tensor(
            out=key[:, u, :].rearrange("p (c t) -> p c t", c=CLUS),
            in0=bcast(k.clus[:, u, :].unsqueeze(2), [P, CLUS, 8]), scalar=2048.0,
            in1=key[:, u, :].rearrange("p (c t) -> p c t", c=CLUS), op0=ALU.mult, op1=ALU.add)
    V.link(ins)
    V.link(e.tensor_reduce(k.kmax, key, AXX, ALU.max))
    hot = k.onehot[:, bass.ds(i * TPC, TPC), :]
    V.link(e.tensor_tensor(hot, key, bcast(k.kmax.unsqueeze(2), tiles), ALU.is_equal))


def routing_ends(k, V, i, n, p):
    s, e = k.s, V.eng
    hot = k.onehot[:, bass.ds(i * TPC, TPC), :]
    V.link(e.tensor_tensor(k.masked.rearrange("p u (t j) -> p u t j", j=DSL),
                           k.y.rearrange("p u (t j) -> p u t j", j=DSL),
                           bcast(hot.unsqueeze(3), [P, TPC, NTILE, DSL]), ALU.mult))
    mine = k.sliced[:, bass.ds(i * TPC, TPC), :]
    V.link(e.tensor_reduce(mine, k.masked.rearrange("p u (t j) -> p u j t", j=DSL), AXX, ALU.add))
    V.link(e.tensor_reduce(k.ends[:, :, 0], mine, AXX, ALU.max))
    V.link(e.tensor_reduce(k.ends[:, :, 1], mine, AXX, ALU.min))
    V.link(e.tensor_scalar(k.ends[:, :, 1], k.ends[:, :, 1], -1.0, None, ALU.mult))
    off = k.masked[:, 0, 0:256].rearrange("p (u t) -> p u t", u=TPC)
    cand = k.masked[:, 1, :].rearrange("p (u a t) -> p u a t", u=TPC, a=2)
    V.link(e.tensor_scalar(off, hot, 1.0, BIG, ALU.subtract, ALU.mult))
    V.link(e.tensor_tensor(cand, bcast(hot.unsqueeze(2), [P, TPC, 2, NTILE]),
                           bcast(k.ends.unsqueeze(3), [P, TPC, 2, NTILE]), ALU.mult))
    V.link(e.tensor_tensor(cand, cand, bcast(off.unsqueeze(2), [P, TPC, 2, NTILE]), ALU.add))
    best = k.masked[:, 0, 256:384].rearrange("p (a t) -> p a t", a=2)
    V.link(e.tensor_reduce(best, cand.rearrange("p u a t -> p a t u"), AXX, ALU.max))
    e.tensor_tensor(k.acc, k.acc, best, ALU.max).then_inc(s[p + "routed"], 1)
    gate(e, s[p + "routed"], i + n, s["gates"])


STATS_STEPS = 15
ROUTE_STEPS = 17


def minmax_tensor(k, pe, n, p):
    s = k.s
    pe.wait_ge(s[p + "routed"], n * NCH)
    for a in range(2):
        ins = pe.transpose(k.ps[0:NTILE, 0, a * P:(a + 1) * P], k.acc[:, a, :], k.c["ident"])
    ins.then_inc(s[p + "minmax_turned"], 1)


def minmax_vector(k, V, n, p):
    s, e = k.s, V.eng
    e.wait_ge(s[p + "minmax_turned"], n)
    V.link(e.tensor_reduce(k.ends2, k.ps[0:NTILE, 0, 0:256].rearrange("p (a t) -> p a t", a=2), AXX, ALU.max))
    V.link(e.tensor_copy(k.table[:, 258:259], k.ends2[:, 0:1]))
    e.tensor_scalar(k.table[:, 257:258], k.ends2[:, 1:2], -1.0, None, ALU.mult).then_inc(s[p + "table_ready"], 1)
    e.wait_ge(s[p + "table_ready"], n)



UG_GROUPS = 2 * INTER // CH
W0_GROUPS = 3


def setup_sync(k, sp):
    s, d = k.s, k.d

    def rows_of(w):
        return w.rearrange("(r p) n -> p r n", p=P)

    def load_nat(group, pieces):
        if group >= 2:
            sp.wait_ge(s["nat_turned"], 4 * (group - 1))
        at = 4 * (group % 2)
        for src, n in pieces:
            sp.dma_start(k.nat[:, at:at + n, :], src).then_inc(s[f"nat_in{group % 2}"], 32 // len(pieces))
            at += n

    sp.dma_start(k.const[:, 0:CONSTS.shape[1]], d["constants"]).then_inc(s["const_in"], 16)
    load_nat(0, [(rows_of(d["L0_attn_Wq"])[:, 0:2], 2), (rows_of(d["L0_attn_Wq"])[:, 2:4], 2)])
    for dst, src in ((k.gamma, d["L0_ffn_ln_gamma"]), (k.beta, d["L0_ffn_ln_beta"])):
        sp.dma_start(dst, src.partition_broadcast(P)).then_inc(s["param_in"], 16)
    sp.dma_start(k.table[:, 0:128], d["L0_ffn_spline_bases"].rearrange("t j g -> t (j g)")).then_inc(s["param_in"], 16)
    sp.dma_start(k.table[:, 128:256], d["L0_ffn_spline_slopes"].rearrange("t j g -> t (j g)")).then_inc(s["param_in"], 16)
    sp.dma_start(k.table[:, 256:257], d["L0_ffn_output_scale"].unsqueeze(1)).then_inc(s["param_in"], 16)
    sp.dma_start(k.wscale, d["L1_ffn_Wscale_ug"].rearrange("(b p) -> p b", p=P)).then_inc(s["param_in"], 16)
    sp.dma_start(k.su_ug, d["L1_ffn_SU_ug"].rearrange("(b p) -> p b", p=P)).then_inc(s["param_in"], 16)
    sp.dma_start(k.su_dp, d["L1_ffn_SU_dp"].rearrange("(b p) -> p b", p=P)).then_inc(s["param_in"], 16)
    sp.dma_start(k.wscale_dp, d["L1_ffn_Wscale_dp"].rearrange("(b p) -> p b", p=P)).then_inc(s["param_in"], 16)
    sp.dma_start(k.bqk[:, 0:4], d["L0_attn_bq"].rearrange("(b p) -> p b", p=P)).then_inc(s["param_in"], 16)
    sp.dma_start(k.bqk[:, 4:6], d["L0_attn_bk"].rearrange("(b p) -> p b", p=P)).then_inc(s["param_in"], 16)
    load_nat(1, [(rows_of(d["L0_attn_Wk"]), 2), (rows_of(d["L0_attn_Wv"]), 2)])
    for c in range(NCH):
        sp.dma_start(k.x[:, c * TPC:(c + 1) * TPC, :],
                     d["L0_attn_hidden_states"][c].rearrange("(u p) n -> p u n", p=P)).then_inc(s["x_in"], 16)
    load_nat(2, [(rows_of(d["L0_attn_Wo"])[:, 0:2], 2), (rows_of(d["L0_attn_Wo"])[:, 2:4], 2)])
    for g in range(UG_GROUPS):
        w = rows_of(d["L1_ffn_W_up"] if g < UG_GROUPS // 2 else d["L1_ffn_W_gate"])
        r = 4 * (g % (UG_GROUPS // 2))
        load_nat(W0_GROUPS + g, [(w[:, r:r + 2], 2), (w[:, r + 2:r + 4], 2)])
        if g == 0:
            for o in range(4):
                sp.dma_start(k.wd_nat[:, o, :], d["L1_ffn_W_down"][o * P:(o + 1) * P, :]).then_inc(s["wd_in"], 16)
    sp.wait_ge(s["rt_zeroed"], 1)
    sp.wait_ge(s["routed"], NCH)
    for j in range(8):
        sp.dma_start(k.rt[32 * (j // 2):32 * (j // 2) + 32, 16 * j:16 * j + 16],
                     d["L0_attn_rand_matrix"].rearrange("e d -> d e")).then_inc(s["b_in"], 16)
    sp.dma_start(k.bv, d["L0_attn_bv"].partition_broadcast(P)).then_inc(s["b_in"], 16)
    sp.dma_start(k.bo, d["L0_attn_bo"].partition_broadcast(P)).then_inc(s["b_in"], 16)
    for o in range(4):
        sp.wait_ge(s["wdo_lo"], 4 * (o + 1))
        for dst, src in ((d["wd_hi"], k.wdo_hi[o % 2]), (d["wd_lo"], k.wdo_lo[o % 2])):
            sp.dma_start(dst[:, :, o * P:(o + 1) * P], src).then_inc(s[f"wdo_out{o % 2}"], 16)


def affine_pool(k, e, i):
    s = k.s
    full, y = [P, TPC, HID], k.rows
    gate(e, s["z_scaled"], i + 1, s["gates"])
    e.tensor_tensor(y, y, bcast(k.gamma.unsqueeze(1), full), ALU.mult).then_inc(s["y_half"], 1)
    gate(e, s["y_half"], i + 1, s["gates"])
    e.tensor_tensor(y, y, bcast(k.beta.unsqueeze(1), full), ALU.add).then_inc(s["y_ready"], 1)


def setup_pool(k, e):
    s = k.s
    e.wait_ge(s["param_in"], 16 * 11)
    with e.Fori(0, 4) as o:
        affine_pool(k, e, o)
        gate(e, s["wd_scaled"], o + 1, s["gates"])
        bufs = [k.wd_nat[:, bass.ds(o, 1), :].squeeze(1), k.wd_tmp]
        for stage in range(4):
            h = P << stage
            a = bufs[stage % 2].rearrange("p (g two m) -> p g two m", two=2, m=h)
            b = bufs[(stage + 1) % 2].rearrange("p (g two m) -> p g two m", two=2, m=h)
            e.tensor_tensor(b[:, :, 0], a[:, :, 0], a[:, :, 1], ALU.add)
            done = s["wd_mixed"] if stage == 3 else s["wd_step"]
            e.tensor_tensor(b[:, :, 1], a[:, :, 0], a[:, :, 1], ALU.subtract).then_inc(done, 1)
            gate(e, done, o + 1 if stage == 3 else o * 3 + (stage + 1), s["gates"])


def turn_rows(k, pe, buf, r):
    s = k.s
    for c in range(KC):
        ins = pe.transpose(k.ps[:, r, c * P:(c + 1) * P], k.nat[:, buf + r, c * P:(c + 1) * P], k.c["ident"])
    ins.then_inc(s["nat_turned"], 1)


def setup_tensor(k, pe):
    s = k.s
    pe.wait_ge(s["const_in"], 16)
    for g in range(W0_GROUPS):
        pe.wait_ge(s[f"nat_in{g % 2}"], 32 * (g // 2 + 1))
        for r in range(4):
            if g:
                pe.wait_ge(s["wt_lo"], 4 * g + r - 3)
            turn_rows(k, pe, 4 * (g % 2), r)
        if g == 0:
            pe.wait_ge(s["ss_diag"], 1)
            pe.matmul(k.ps[:, 4, :], k.ones, k.diag, start=True, stop=True).then_inc(s["ss_spread"], 1)

    def group(i, odd):
        buf = 4 * ((W0_GROUPS + odd) % 2)
        tile = i * 8 + (4 * W0_GROUPS + 4 * odd)
        gate(pe, s["nat_scaled"], i * 8 + (4 * odd + 4), s["gates"])
        for r in range(4):
            gate(pe, s["wt_lo"], tile + (r - 3), s["gates"])
            turn_rows(k, pe, buf, r)
        gate(pe, s["wt_lo"], tile + 4, s["gates"])
        for kc in range(KC):
            gate(pe, s["had_lo"], i * 8 + (4 * odd + kc + 1), s["gates"])
            n = 0
            for jc in range(KC):
                sign = k.had16n if bin(kc & jc).count("1") & 1 else k.had16
                for part in (k.wt_hi, k.wt_lo):
                    ins = pe.matmul(k.ps[:, 4 + kc, :], sign, part[:, jc, :], start=(n == 0), stop=(n == 7))
                    n += 1
            ins.then_inc(s["had_done"], 1)

    with pe.Fori(0, UG_GROUPS // 2) as i:
        group(i, 0)
        group(i, 1)
    for o in range(4):
        pe.wait_ge(s["wd_mixed"], o + 1)
        for q in range(4):
            if o:
                pe.wait_ge(s["wdt_lo"], 4 * o + q - 3)
            else:
                pe.wait_ge(s["wt_lo"], 4 * (W0_GROUPS + UG_GROUPS))
            for b in range(4):
                c = 4 * q + b
                ins = pe.transpose(k.ps[:, q, b * P:(b + 1) * P], k.wd_nat[:, o, c * P:(c + 1) * P], k.c["ident"])
            ins.then_inc(s["wdt_turned"], 1)
        pe.wait_ge(s["wdt_lo"], 4 * o + 4)
        for q in range(4):
            if o:
                pe.wait_ge(s["wdo_lo"], 4 * o + q - 3)
            else:
                pe.wait_ge(s["had_lo"], 4 + 4 * UG_GROUPS)
            for b in range(4):
                c = 4 * q + b
                pe.matmul(k.ps[:, 4 + q, b * P:(b + 1) * P], k.had16, k.wdt_hi[:, c, :], start=True, stop=False)
                ins = pe.matmul(k.ps[:, 4 + q, b * P:(b + 1) * P], k.had16, k.wdt_lo[:, c, :], start=False, stop=True)
            ins.then_inc(s["wdh_done"], 1)


def setup_scalar(k, e):
    s = k.s
    e.wait_ge(s["const_in"], 16)
    e.activation(k.had16, k.c["had"], ACT.Copy)
    e.activation(k.had16n, k.c["had"], ACT.Copy, scale=-1.0)
    e.wait_ge(s["ssum_ready"], 1)
    e.activation(k.ssign, k.ssum, ACT.Sign).then_inc(s["ss_signed"], 1)
    for g in range(W0_GROUPS):
        if g == 1:
            e.wait_ge(s["ss_spread"], 1)
            e.activation(k.ssrow, k.ps[:, 4, :], ACT.Copy).then_inc(s["ss_row"], 1)
        for r in range(4):
            e.wait_ge(s["nat_turned"], 4 * g + r + 1)
            c = (4 * g + r) * P
            e.activation(k.w0_hi[:, :, c:c + P], k.ps[:, r, :].rearrange("p (c m) -> p c m", c=KC), ACT.Copy,
                         scale=W_SCALE).then_inc(s["wt_hi"], 1)
    e.wait_ge(s["x_in"], 16 * NCH)
    e.wait_ge(s["wd_in"], 64)

    def group_turned(i, odd):
        tile = i * 8 + (4 * W0_GROUPS + 4 * odd)
        for r in range(4):
            gate(e, s["nat_turned"], tile + (r + 1), s["gates"])
            e.activation(k.wt_hi[:, :, r * P:(r + 1) * P], k.ps[:, r, :].rearrange("p (c m) -> p c m", c=KC),
                         ACT.Copy, scale=W_SCALE).then_inc(s["wt_hi"], 1)

    def group_mixed(i, odd):
        for kc in range(KC):
            gate(e, s["had_done"], i * 8 + (4 * odd + kc + 1), s["gates"])
            e.activation(k.wug_hi[:, kc, bass.ds(i * 1024 + CH * odd, CH)], k.ps[:, 4 + kc, :], ACT.Copy,
                         scale=k.su_ug[:, kc:kc + 1]).then_inc(s["had_hi"], 1)

    with e.Fori(0, NCH) as i:
        group_turned(i, 0)
        row = k.wd_nat[:, bass.ds(i, 1), :].squeeze(1)
        e.activation(row, row, ACT.Copy, scale=k.wscale_dp[:, bass.ds(i, 1)]).then_inc(s["wd_scaled"], 1)
        token_stats_scalar(k, e, i, 1, "")
        group_mixed(i, 0)
        group_turned(i, 1)
        token_signs_scalar(k, e, i, 1, "")
        group_mixed(i, 1)
    for o in range(4):
        for q in range(4):
            e.wait_ge(s["wdt_turned"], 4 * o + q + 1)
            if q == 0 and o:
                e.wait_ge(s["wdh_done"], 4 * o)
            e.activation(k.wdt_hi[:, 4 * q:4 * q + 4, :], k.ps[:, q, :].rearrange("p (c m) -> p c m", c=4),
                         ACT.Copy, scale=W_SCALE).then_inc(s["wdt_hi"], 1)
        for q in range(4):
            e.wait_ge(s["wdh_done"], 4 * o + q + 1)
            if q == 0 and o >= 2:
                e.wait_ge(s[f"wdo_out{o % 2}"], 32)
            e.activation(k.wdo_hi[o % 2][:, 4 * q:4 * q + 4, :], k.ps[:, 4 + q, :].rearrange("p (c m) -> p c m", c=4),
                         ACT.Copy, scale=float(INTER) ** -0.5).then_inc(s["wdo_hi"], 1)


def setup_vector(k, V):
    s, e = k.s, V.eng
    e.memset(k.ones, 1.0)
    e.memset(k.rt, 0.0).then_inc(s["rt_zeroed"], 1)
    e.memset(k.acc, -BIG).then_inc(s["had_lo"], 4)
    e.wait_ge(s["const_in"], 16)
    e.wait_ge(s["param_in"], 16 * 11)
    e.tensor_reduce(k.ssum, k.table[:, 128:256].rearrange("t (j g) -> t j g", g=GRID), AXX, ALU.add)\
        .then_inc(s["ssum_ready"], 1)
    e.tensor_tensor(k.wscale[:, 0:FB], k.wscale[:, 0:FB], k.su_dp, ALU.mult).then_inc(s["up_scale"], 1)
    e.tensor_scalar(k.su_ug, k.su_ug, float(HID) ** -0.5, None, ALU.mult).then_inc(s["up_scale"], 1)
    e.wait_ge(s["up_scale"], 2)
    e.wait_ge(s["ss_signed"], 1)
    e.tensor_tensor(k.diag.rearrange("p (t j) -> p t j", j=DSL),
                    bcast(k.c["ident"][0:NTILE, 0:NTILE].unsqueeze(2), [NTILE, NTILE, DSL]),
                    bcast(k.ssign.unsqueeze(1), [NTILE, NTILE, DSL]), ALU.mult).then_inc(s["ss_diag"], 1)
    for g in range(W0_GROUPS):
        for r in range(4):
            e.wait_ge(s["wt_hi"], 4 * g + r + 1)
            c = (4 * g + r) * P
            e.scalar_tensor_tensor(out=k.w0_lo[:, :, c:c + P],
                                   in0=k.ps[:, r, :].rearrange("p (c m) -> p c m", c=KC), scalar=W_SCALE,
                                   in1=k.w0_hi[:, :, c:c + P], op0=ALU.mult, op1=ALU.subtract)\
                .then_inc(s["wt_lo"], 1)
    e.wait_ge(s["x_in"], 16 * NCH)
    e.wait_ge(s["ss_row"], 1)

    def scale_rows(i, odd):
        buf = 4 * ((W0_GROUPS + odd) % 2)
        gate(e, s[f"nat_in{(W0_GROUPS + odd) % 2}"], i * 32 + 32 * ((W0_GROUPS + odd) // 2 + 1), s["gates"])
        rows = k.nat[:, buf:buf + 4, :]
        e.tensor_tensor(rows, rows, bcast(k.wscale[:, bass.ds(i * 8 + 4 * odd, 4)].unsqueeze(2), [P, 4, HID]),
                        ALU.mult).then_inc(s["nat_scaled"], 4)

    def group_turned(i, odd):
        for r in range(4):
            gate(e, s["wt_hi"], i * 8 + (4 * W0_GROUPS + 4 * odd + r + 1), s["gates"])
            e.scalar_tensor_tensor(out=k.wt_lo[:, :, r * P:(r + 1) * P],
                                   in0=k.ps[:, r, :].rearrange("p (c m) -> p c m", c=KC), scalar=W_SCALE,
                                   in1=k.wt_hi[:, :, r * P:(r + 1) * P], op0=ALU.mult, op1=ALU.subtract)\
                .then_inc(s["wt_lo"], 1)

    def group_mixed(i, odd):
        for kc in range(KC):
            gate(e, s["had_hi"], i * 8 + (4 * odd + kc + 1), s["gates"])
            cols = bass.ds(i * 1024 + CH * odd, CH)
            e.scalar_tensor_tensor(out=k.wug_lo[:, kc, cols], in0=k.ps[:, 4 + kc, :],
                                   scalar=k.su_ug[:, kc:kc + 1], in1=k.wug_hi[:, kc, cols],
                                   op0=ALU.mult, op1=ALU.subtract).then_inc(s["had_lo"], 1)

    def both(i, last):
        V.enter(i, STATS_STEPS + ROUTE_STEPS - 1)
        group_turned(i, 0)
        scale_rows(i, 1)
        token_stats_vector(k, V, i, 1, "")
        group_mixed(i, 0)
        group_turned(i, 1)
        if not last:
            scale_rows(i + 1, 0)
        routing_choice(k, V, i, 1, "")
        group_mixed(i, 1)
        routing_ends(k, V, i, 1, "")

    scale_rows(0, 0)
    with e.Fori(0, NCH - 1) as i:
        both(i, False)
    both(NCH - 1, True)
    V.leave(NCH)
    for o in range(4):
        for q in range(4):
            e.wait_ge(s["wdt_hi"], 4 * o + q + 1)
            if q == 0 and o:
                e.wait_ge(s["wdh_done"], 4 * o)
            e.scalar_tensor_tensor(out=k.wdt_lo[:, 4 * q:4 * q + 4, :],
                                   in0=k.ps[:, q, :].rearrange("p (c m) -> p c m", c=4), scalar=W_SCALE,
                                   in1=k.wdt_hi[:, 4 * q:4 * q + 4, :], op0=ALU.mult, op1=ALU.subtract)\
                .then_inc(s["wdt_lo"], 1)
        for q in range(4):
            e.wait_ge(s["wdo_hi"], 4 * o + q + 1)
            if q == 0 and o >= 2:
                e.wait_ge(s[f"wdo_out{o % 2}"], 32)
            e.scalar_tensor_tensor(out=k.wdo_lo[o % 2][:, 4 * q:4 * q + 4, :],
                                   in0=k.ps[:, 4 + q, :].rearrange("p (c m) -> p c m", c=4),
                                   scalar=float(INTER) ** -0.5, in1=k.wdo_hi[o % 2][:, 4 * q:4 * q + 4, :],
                                   op0=ALU.mult, op1=ALU.subtract).then_inc(s["wdo_lo"], 1)




def apply_tensor(k, pe, i, n):
    s = k.s
    gate(pe, s["ap_oh"], i + n, s["gates"])
    for u in range(TPC):
        ins = pe.transpose(k.ps[0:NTILE, 6, u * P:(u + 1) * P], k.oh4[:, u, :], k.c["ident"])
    ins.then_inc(s["ap_turned"], 1)
    gate(pe, s["ap_oht"], i + n, s["gates"])
    for u in range(TPC):
        ins = pe.matmul(k.ps[:, 2 + u, 0:259], k.oht[:, u * P:(u + 1) * P], k.table[:, 0:259], start=True, stop=True)
    ins.then_inc(s["ap_rows"], 1)


def apply_scalar(k, e, i, n):
    s = k.s
    gate(e, s["ap_turned"], i + n, s["gates"])
    e.activation(k.oht, k.ps[0:NTILE, 6, :], ACT.Copy).then_inc(s["ap_oht"], 1)


ADD_STEPS = 6
SPLINE_STEPS = 21


def add_vector(k, V, i):
    e = V.eng
    tiles = bass.ds(i * TPC, TPC)
    a, b = k.t4[0], k.t4[1]
    mr = k.mr[:, tiles, :]
    V.link(e.tensor_scalar(a, mr[:, :, 1], 0.5, None, ALU.mult))
    V.link(e.tensor_tensor(b, mr[:, :, 0], a, ALU.mult))
    V.link(e.tensor_scalar(a, a, 1.0, None, ALU.add))
    for u in range(TPC):
        xt = k.x[:, bass.ds(i * TPC + u, 1), :].squeeze(1)
        ins = e.tensor_scalar(xt, xt, a[:, u:u + 1], b[:, u:u + 1], ALU.mult, ALU.subtract)
    V.link(ins)
    for u in range(TPC):
        ins = e.tensor_tensor(k.scat[:, u, :].rearrange("p (t j) -> p t j", j=DSL),
                              bcast(k.oh4[:, u, :].unsqueeze(2), [P, NTILE, DSL]),
                              bcast(k.ap[3][:, u, :].unsqueeze(1), [P, NTILE, DSL]), ALU.mult)
    V.link(ins)
    xs = k.x[:, tiles, :]
    V.link(e.tensor_tensor(xs, xs, k.scat, ALU.add))


def spline_vector(k, V, i, n):
    s, e = k.s, V.eng
    tiles = bass.ds(i * TPC, TPC)
    e.tensor_copy(k.oh4, k.onehot[:, tiles, :]).then_inc(s["ap_oh"], 1)
    gate(e, s["ap_rows"], i + n, s["gates"])
    rows = k.ps[:, 2:2 + TPC, :]
    V.link(e.tensor_copy(k.cols, rows[:, :, 256:259]))
    full = [P, TPC, DSL]
    u16, lo, fl, d1, xl, sp = k.ap
    half, span, mn, mx = k.t4[0], k.t4[1], k.cols[:, :, 1], k.cols[:, :, 2]
    V.link(e.tensor_tensor(span, mx, mn, ALU.subtract))
    V.link(e.tensor_scalar(span, span, 1e-8, None, ALU.add))
    V.link(e.reciprocal(span, span))
    V.link(e.tensor_scalar(half, k.cols[:, :, 0], 0.5, None, ALU.mult))
    V.link(e.tensor_tensor(u16, k.sliced[:, tiles, :], bcast(mn.unsqueeze(2), full), ALU.subtract))
    V.link(e.tensor_tensor(u16, u16, bcast(span.unsqueeze(2), full), ALU.mult))
    V.link(e.tensor_scalar(u16, u16, 0.0, 1.0 - 1e-6, ALU.max, ALU.min))
    V.link(e.tensor_scalar(u16, u16, float(GRID), None, ALU.mult))
    V.link(e.tensor_scalar(fl, u16, ROUND, ROUND, ALU.add, ALU.subtract))
    V.link(e.tensor_tensor(lo, fl, u16, ALU.is_gt))
    V.link(e.tensor_tensor(fl, fl, lo, ALU.subtract))
    V.link(e.tensor_tensor(xl, u16, fl, ALU.subtract))
    cells = [P, TPC, DSL, GRID]
    V.link(e.tensor_tensor(k.m16, bcast(k.c["iota"].unsqueeze(1).unsqueeze(1), cells), bcast(fl.unsqueeze(3), cells),
                           ALU.is_equal))
    for dst, at in ((sp, 128), (d1, 0)):
        V.link(e.tensor_tensor(k.m16p, k.m16, rows[:, :, at:at + 128].rearrange("p u (j g) -> p u j g", g=GRID),
                               ALU.mult))
        V.link(e.tensor_reduce(dst, k.m16p, AXX, ALU.add))
    V.link(e.tensor_tensor(sp, sp, xl, ALU.mult))
    V.link(e.tensor_tensor(d1, d1, sp, ALU.add))
    V.link(e.tensor_tensor(d1, d1, bcast(half.unsqueeze(2), full), ALU.mult))
    e.sem_inc(s["ap_read"], 1)




NORM_STEPS = 7


def norm_stats_vector(k, V, i, n):
    s, e = k.s, V.eng
    for u in range(TPC):
        ins = e.bn_stats(k.stats6[:, u, :], k.x[:, bass.ds(i * TPC + u, 1), :].squeeze(1))
    V.link(ins)
    for u in range(TPC):
        ins = e.bn_aggr(k.mv[:, u, :], k.stats6[:, u, :])
    V.link(ins)
    ve, std, r, t, std2, r2, nm2 = k.t4
    mean, var = k.mv[:, :, 0], k.mv[:, :, 1]
    e.tensor_scalar(ve, var, LN_EPS, None, ALU.add).then_inc(s["n_var"], 1)


def norm_scale_vector(k, V, i, n):
    s, e = k.s, V.eng
    ve, std, r, t, std2, r2, nm2 = k.t4
    mean = k.mv[:, :, 0]
    gate(e, s["n_std"], i + n, s["gates"])
    rsqrt_vector(V, r, std, ve, t)
    V.link(e.tensor_scalar(r2, r, A_SCALE, None, ALU.mult))
    e.scalar_tensor_tensor(out=nm2, in0=mean, scalar=-1.0, in1=r2, op0=ALU.mult, op1=ALU.mult)\
        .then_inc(s["n_norm"], 1)


def norm_low_vector(k, i, n, e):
    s = k.s
    for c in range(KC):
        gate(e, s["n_hi"], nth(i, n, KC, c + 1), s["gates"])
        e.tensor_tensor(k.ht_lo[:, c, :], k.ps[:, c % 2, :], k.ht_hi[:, c, :], ALU.subtract).then_inc(s["n_lo"], 1)


def norm_scalar(k, e, i, n):
    norm_std_scalar(k, e, i, n)
    norm_rows_scalar(k, e, i, n)
    norm_high_scalar(k, e, i, n, range(KC))


def norm_std_scalar(k, e, i, n):
    s = k.s
    ve, std, r, t, std2, r2, nm2 = k.t4
    gate(e, s["n_var"], i + n, s["gates"])
    e.activation(std, ve, ACT.Sqrt).then_inc(s["n_std"], 1)


def norm_rows_scalar(k, e, i, n):
    s = k.s
    r2, nm2 = k.t4[5], k.t4[6]
    gate(e, s["n_norm"], i + n, s["gates"])
    for u in range(TPC):
        ins = e.activation(k.h[:, u, :], k.x[:, bass.ds(i * TPC + u, 1), :].squeeze(1), ACT.Identity,
                           bias=nm2[:, u:u + 1], scale=r2[:, u:u + 1])
    ins.then_inc(s["n_h"], 1)


def norm_high_scalar(k, e, i, n, blocks):
    s = k.s
    for c in blocks:
        gate(e, s["n_turned"], nth(i, n, KC, c + 1), s["gates"])
        e.activation(k.ht_hi[:, c, :], k.ps[:, c % 2, :], ACT.Copy).then_inc(s["n_hi"], 1)


def norm_tensor(k, pe, i, n):
    s = k.s
    gate(pe, s["n_h"], i + n, s["gates"])
    for c in range(KC):
        gate(pe, s["n_lo"], nth(i, n, KC, c + 1), s["gates"])
        for u in range(TPC):
            ins = pe.transpose(k.ps[:, c % 2, u * P:(u + 1) * P], k.h[:, u, c * P:(c + 1) * P], k.c["ident"])
        ins.then_inc(s["n_turned"], 1)
    gate(pe, s["n_lo"], nth(i, n, KC, KC + 2), s["gates"])


def pairs_product(pe, out, left, right, n=KC, halfway=None):
    at = 0
    for c in range(n):
        if halfway is not None and 2 * c == n:
            halfway()
        for a, b in ((0, 0), (0, 1), (1, 0)):
            ins = pe.matmul(out, left[a](c), right[b](c), start=(at == 0), stop=(at == 3 * n - 1))
            at += 1
    return ins


def of(ref, cols, block=None):
    return lambda c: ref[:, c, cols]



ORDER = (4, 5, 0, 1, 2, 3)
GROUP = 16
PAIRS = CH // GROUP // 2
OUT_BANK = (6, 7, 4, 5)
PROJ_BANK = (2, 3, 4, 5, 1, 0)


def b_tensor(k, pe, i, next):
    s = k.s
    ht = (k.ht_hi, k.ht_lo)
    w0 = (k.w0_hi, k.w0_lo)
    for u in range(TPC):
        gate(pe, s["b_v_in"], nth(i, 1, TPC, u + 1), s["gates"])
        cols = slice(u * P, (u + 1) * P)
        pairs_product(pe, k.ps[:, 6 + u % 2, 0:256], [of(h, cols) for h in ht], [of(w, slice(768, 1024)) for w in w0])\
            .then_inc(s["b_v_done"], 1)
    for z in range(8):
        if z < 6:
            gate(pe, s["b_qf"], nth(i, 1, 6, z + 1), s["gates"])
            cols = slice(ORDER[z] * P, (ORDER[z] + 1) * P)
            pairs_product(pe, k.ps[:, 2 + z % 2, :], [of(w, cols) for w in w0], [of(h, slice(0, CH)) for h in ht])\
                .then_inc(s["b_qk_done"], 1)
        if 1 <= z < 7:
            gate(pe, s["b_qf"], nth(i, 1, 6, z + 2), s["gates"])
            gate(pe, s["b_rope"], nth(i, 1, 6, z), s["gates"])
            pe.matmul(k.ps[:, 4 + (z - 1) % 2, :], k.c["rot"], k.qf[:, z - 1, :], start=True, stop=True)\
                .then_inc(s["b_rot"], 1)
        if z >= 2:
            gate(pe, s["b_sq"], nth(i, 1, 6, z - 1), s["gates"])
            at = 20 - 4 * (z - 2)
            pe.matmul(k.ps[0:24, 0, :], k.c["headpad"][:, at:at + 24], k.q2[:, z % 2, :], start=(z == 2), stop=(z == 7))\
                .then_inc(s["b_nsum"], 1)
    gate(pe, s["b_rope"], nth(i, 1, 6, 8), s["gates"])
    for z in range(6):
        if z == 5:
            gate(pe, s["b_r"], i + 1, s["gates"])
        pe.matmul(k.ps[:, PROJ_BANK[z], :], k.rt, k.qr[:, z, :], start=True, stop=True).then_inc(s["b_proj"], 1)
    for z in range(6):
        gate(pe, s["b_y"], nth(i, 1, 6, z + 1), s["gates"])
        pe.matmul(k.ps[:, 6 + z % 2, :], k.spread[:, z * P:(z + 1) * P], k.nr[0:24, 2, :], start=True, stop=True)\
            .then_inc(s["b_p"], 1)
    if next is not None:
        apply_tensor(k, pe, next, 1)
        gate(pe, s["ap_read"], next + 1, s["gates"])
    gate(pe, s["b_qs"], nth(i, 1, 384, 384), s["gates"])
    gate(pe, s["b_vr"], nth(i, 1, 16, 16), s["gates"])
    for y in range(PAIRS + 1):
        if y < PAIRS:
            gate(pe, s["b_mask"], nth(i, 1, PAIRS, y + 1), s["gates"])
            if y % 4 == 0:
                gate(pe, s["b_ksg"], nth(i, 1, 4, y // 4 + 1), s["gates"])
            for q in range(2):
                toks = slice((2 * y + q) * GROUP, (2 * y + q + 1) * GROUP)
                ins = pe.matmul(k.ps[:, 4 + y % 2, 256 * q:256 * q + 256].rearrange("p (t h) -> p t h", h=16),
                                k.ksg[0:96, 2 * y + q, :], k.qs[0:96, :, toks].rearrange("p h t -> p t h"),
                                start=True, stop=True)
            ins.then_inc(s["b_s"], 1)
        if y:
            gate(pe, s["b_mask"], nth(i, 1, PAIRS, y + 2), s["gates"])
            if y % 4 == 1:
                gate(pe, s["b_ot_lo"], nth(i, 1, TPC, y // 4 + 1), s["gates"])
            for q in range(2):
                g = 2 * (y - 1) + q
                for j in range(4):
                    ins = pe.matmul(k.ps[32 * j:32 * j + 32, g // 8 % 2, 64 * (g % 8):64 * (g % 8) + 64]
                                    .rearrange("p (a h) -> p a h", h=16), k.vr[:, g, :],
                                    k.sm[:, (y - 1) % 2, q].rearrange("p (a j) h -> p j a h", j=4)[:, j],
                                    start=True, stop=True, tile_position=(0, 32 * j))
            ins.then_inc(s["b_pv"], 1)
    gate(pe, s["b_ot_lo"], nth(i, 1, TPC, TPC + 2), s["gates"])
    for u in range(TPC):
        cols = slice(u * P, (u + 1) * P)
        pairs_product(pe, k.ps[:, OUT_BANK[u], :], [of(o, cols) for o in (k.ht_hi, k.ht_lo)],
                      [of(w, slice(1024, 1536)) for w in w0]).then_inc(s["b_out"], 1)
    if next is not None:
        norm_tensor(k, pe, next, 1)
    gate(pe, s["b_res"], nth(i, 1, TPC, TPC), s["gates"])


def grouped(ref):
    return ref.rearrange("p a (h g) -> p g a h", g=32)


def b_scalar(k, e, i, last, next):
    s = k.s
    norm_high_scalar(k, e, i, 1, range(KC))
    for z in range(6):
        if last is not None and z == 1:
            token_stats_scalar(k, e, last, 1 + NCH, "")
        if last is not None and z == 3:
            token_signs_scalar(k, e, last, 1 + NCH, "")
        gate(e, s["b_qk_done"], nth(i, 1, 6, z + 1), s["gates"])
        e.activation(k.qf[:, z, :], k.ps[:, 2 + z % 2, :], ACT.Identity, bias=k.bqk[:, ORDER[z]:ORDER[z] + 1],
                     scale=1.0 / (W_SCALE * A_SCALE)).then_inc(s["b_qf"], 1)
    def spread(z):
        gate(e, s["b_p"], nth(i, 1, 6, z + 1), s["gates"])
        if z >= 2:
            gate(e, s["b_reduced"], nth(i, 1, 6, z - 1), s["gates"])
        e.activation(k.turns[:, z % 2, :], k.ps[:, 6 + z % 2, :], ACT.Copy).then_inc(s["b_spread"], 1)

    gate(e, s["b_n2"], i + 1, s["gates"])
    e.activation(k.nr[0:24, 1, :], k.nr[0:24, 0, :], ACT.Sqrt).then_inc(s["b_n"], 1)
    for z in range(6):
        if z == 0:
            spread(0)
        if z < 5:
            spread(z + 1)
        gate(e, s["b_reduced"], nth(i, 1, 6, z + 1), s["gates"])
        e.activation(k.ang[:, z % 2, :], k.ang[:, z % 2, :], ACT.Sin, bias=k.c["phase2pi"], scale=-float(2 * np.pi))\
            .then_inc(s["b_feat"], 1)
        gate(e, s["b_feat"], nth(i, 1, 6, z + 1), s["gates"])
        e.activation(k.f_hi[:, z, :], k.ang[:, z % 2, :], ACT.Copy, scale=A_SCALE).then_inc(s["b_f_hi"], 1)
    if next is not None:
        apply_scalar(k, e, next, 1)
    gate(e, s["b_ks"], nth(i, 1, 192, 192), s["gates"])
    gate(e, s["b_f_lo"], nth(i, 1, 6, 6), s["gates"])
    for g in range(4):
        e.activation(k.ksg[0:96, 8 * g:8 * g + 8, :].rearrange("p g (t h) -> p g t h", h=8),
                     k.ks[0:96, :, P * g:P * g + P].rearrange("p h (g t) -> p g t h", t=GROUP), ACT.Copy)\
            .then_inc(s["b_ksg"], 1)
    for g in range(4):
        gate(e, s["b_pv"], nth(i, 1, PAIRS, 4 * g + 4), s["gates"])
        e.activation(grouped(k.ht_hi)[:, 8 * g:8 * g + 8], k.ps[:, g % 2, :].rearrange("p (g a h) -> p g a h", g=8, a=4),
                     ACT.Copy, scale=O_SCALE).then_inc(s["b_ot_hi"], 1)
    if next is not None:
        norm_std_scalar(k, e, next, 1)
        norm_rows_scalar(k, e, next, 1)


O_SCALE = 2.0 / 32 * A_SCALE / (A_SCALE * A_SCALE)


def b_pool(k, e, i):
    s = k.s
    for z in range(6):
        gate(e, s["b_qf"], nth(i, 1, 6, z + 3), s["gates"])
        e.tensor_tensor(k.qr[:, z, :], k.qf[:, z, :], k.c["cos"], ALU.mult).then_inc(s["b_cos"], 1)
        gate(e, s["b_rope"], nth(i, 1, 6, z + 3), s["gates"])
        if z >= 2:
            gate(e, s["b_nsum"], nth(i, 1, 6, z - 1), s["gates"])
        e.tensor_tensor(k.q2[:, z % 2, :], k.qr[:, z, :], k.qr[:, z, :], ALU.mult).then_inc(s["b_sq"], 1)


def b_sync(k, sp, i):
    s, scratch = k.s, k.d["values"]
    gate(sp, s["b_v_in"], nth(i, 1, TPC, TPC + 2), s["gates"])
    sp.dma_start(scratch.rearrange("(u p) n -> p u n", p=P), k.v0).then_inc(s["b_v_out"], 16)
    gate(sp, s["b_v_out"], nth(i, 1, 16, 16), s["gates"])
    sp.dma_start(k.vr, scratch.rearrange("(g t) (h d) -> (t h) g d", t=GROUP, d=32)).then_inc(s["b_vr"], 16)
    f = (k.f_hi, k.f_lo)

    def spread(stack, parts, blocks, heads, sem):
        for part in range(3):
            for j in range(4):
                dst = stack[32 * part:32 * part + 32].rearrange("p (b j) t -> p j b t", j=4)[:, j, heads]
                sp.dma_start(dst, f[parts[part]][32 * j:32 * j + 32, blocks, :]).then_inc(sem, 16)

    gate(sp, s["b_f_lo"], nth(i, 1, 6, 2), s["gates"])
    spread(k.ks, (0, 0, 1), slice(0, 2), slice(0, 2), s["b_ks"])
    gate(sp, s["b_f_lo"], nth(i, 1, 6, 4), s["gates"])
    spread(k.qs, (0, 1, 0), slice(2, 4), slice(0, 2), s["b_qs"])
    gate(sp, s["b_f_lo"], nth(i, 1, 6, 6), s["gates"])
    spread(k.qs, (0, 1, 0), slice(4, 6), slice(2, 4), s["b_qs"])
    gate(sp, s["b_vr"], nth(i, 1, 16, 16), s["gates"])


B_STEPS = 6 + 4 + TPC


def b_vector(k, V, i, last, next):
    s, e = k.s, V.eng
    use_work(k, k.work, k.h, k.nr.rearrange("p a b -> p (a b)"))
    norm_low_vector(k, i, 1, e)
    for u in range(TPC):
        gate(e, s["b_v_done"], nth(i, 1, TPC, u + 1), s["gates"])
        e.scalar_tensor_tensor(out=k.v0[:, u, :], in0=k.ps[:, 6 + u % 2, 0:256], scalar=1.0 / (W_SCALE * A_SCALE),
                               in1=k.bv, op0=ALU.mult, op1=ALU.add).then_inc(s["b_v_in"], 1)
    use_rows(k, k.masked2, k.y2)
    for z in range(6):
        if last is not None and z == 0:
            token_stats_vector(k, V, last, 1 + NCH, "")
        if last is not None and z == 2:
            routing_affine(k, V, last, 1 + NCH, "")
        if last is not None and z == 4:
            routing_choice(k, V, last, 1 + NCH, "")
        gate(e, s["b_rot"], nth(i, 1, 6, z + 1), s["gates"])
        gate(e, s["b_cos"], nth(i, 1, 6, z + 1), s["gates"])
        V.link(e.tensor_tensor(k.qf[:, z, :], k.ps[:, 4 + z % 2, :], k.c["sin"], ALU.mult))
        e.tensor_tensor(k.qr[:, z, :], k.qr[:, z, :], k.qf[:, z, :], ALU.add).then_inc(s["b_rope"], 1)
    if last is not None:
        routing_ends(k, V, last, 1 + NCH, "")
    gate(e, s["b_nsum"], nth(i, 1, 6, 6), s["gates"])
    n2, nn, r, t = [k.nr[0:24, m, :] for m in range(4)]
    e.tensor_scalar(n2, k.ps[0:24, 0, :], 1e-12, None, ALU.max).then_inc(s["b_n2"], 1)
    gate(e, s["b_n"], i + 1, s["gates"])
    rsqrt_vector(V, r, nn, n2, t)
    e.sem_inc(s["b_r"], 1)
    for z in range(7):
        if z < 6:
            ang, turns = k.ang[:, z % 2, :], k.turns[:, z % 2, :]
            gate(e, s["b_proj"], nth(i, 1, 6, z + 1), s["gates"])
            gate(e, s["b_spread"], nth(i, 1, 6, z + 1), s["gates"])
            e.scalar_tensor_tensor(out=turns, in0=k.ps[:, PROJ_BANK[z], :], scalar=float(1 / (2 * np.pi)), in1=turns,
                                   op0=ALU.mult, op1=ALU.mult).then_inc(s["b_y"], 1)
            gate(e, s["b_y"], nth(i, 1, 6, z + 3), s["gates"])
            if z >= 2:
                gate(e, s["b_f_lo"], nth(i, 1, 6, z - 1), s["gates"])
            e.tensor_scalar(ang, turns, k.c["phase"], ROUND, ALU.add, ALU.add).then_inc(s["b_whole"], 1)
            gate(e, s["b_whole"], nth(i, 1, 6, z + 1), s["gates"])
            e.scalar_tensor_tensor(out=ang, in0=ang, scalar=ROUND, in1=turns, op0=ALU.subtract, op1=ALU.subtract)\
                .then_inc(s["b_reduced"], 1)
        if z:
            gate(e, s["b_f_hi"], nth(i, 1, 6, z), s["gates"])
            e.scalar_tensor_tensor(out=k.f_lo[:, z - 1, :], in0=k.ang[:, (z - 1) % 2, :], scalar=A_SCALE,
                                   in1=k.f_hi[:, z - 1, :], op0=ALU.mult, op1=ALU.subtract).then_inc(s["b_f_lo"], 1)
    if next is not None:
        spline_vector(k, V, next, 1)
    for y in range(PAIRS):
        gate(e, s["b_s"], nth(i, 1, PAIRS, y + 1), s["gates"])
        if y >= 2:
            gate(e, s["b_pv"], nth(i, 1, PAIRS, y - 1), s["gates"])
        for q in range(2):
            ins = e.tensor_tensor(k.sm[:, y % 2, q], k.ps[:, 4 + y % 2, 256 * q:256 * q + 256]
                                  .rearrange("p (t h) -> p t h", h=16), bcast(k.c["same"].unsqueeze(2), [P, 16, 16]),
                                  ALU.mult)
        ins.then_inc(s["b_mask"], 1)
        if y % 4 == 1 and y > 4:
            b_low(k, e, i, y // 4 - 1)
    b_low(k, e, i, 3)
    if next is not None:
        use_work(k, k.work, k.h, k.nr.rearrange("p a b -> p (a b)"))
        add_vector(k, V, next)
        norm_stats_vector(k, V, next, 1)
        norm_scale_vector(k, V, next, 1)
    for u in range(TPC):
        gate(e, s["b_out"], nth(i, 1, TPC, u + 1), s["gates"])
        xt = k.x[:, bass.ds(i * TPC + u, 1), :].squeeze(1)
        e.scalar_tensor_tensor(out=xt, in0=k.ps[:, OUT_BANK[u], :], scalar=1.0 / (W_SCALE * A_SCALE), in1=xt,
                               op0=ALU.mult, op1=ALU.add).then_inc(s["b_res"], 1)
        gate(e, s["b_res"], nth(i, 1, TPC, u + 1), s["gates"])
        V.link(e.tensor_tensor(xt, xt, k.bo, ALU.add))


def b_low(k, e, i, g):
    s = k.s
    gate(e, s["b_ot_hi"], nth(i, 1, TPC, g + 1), s["gates"])
    out = grouped(k.ht_lo)[:, 8 * g:8 * g + 8]
    e.scalar_tensor_tensor(out=out, in0=k.ps[:, g % 2, :].rearrange("p (g a h) -> p g a h", g=8, a=4), scalar=O_SCALE,
                           in1=grouped(k.ht_hi)[:, 8 * g:8 * g + 8], op0=ALU.mult, op1=ALU.subtract)\
        .then_inc(s["b_ot_lo"], 1)




DOWN_BANK = (6, 7, 0, 1)


def ffn_tensor(k, pe, i, n, after, down_in):
    s = k.s
    ht = [of(h, slice(0, CH)) for h in (k.ht_hi, k.ht_lo)]
    for f in range(FB):
        gate(pe, s["f_prod"], nth(i, n, FB, f + 1), s["gates"])
        for which, at in ((0, INTER + f * P), (1, f * P)):
            w = [of(x, slice(at, at + P)) for x in (k.wug_hi, k.wug_lo)]
            pairs_product(pe, k.ps[:, 2 + 2 * (f % 2) + which, :], w, ht).then_inc(s["f_up" if which else "f_gate"], 1)
    gate(pe, s["f_lo"], nth(i, n, FB, FB), s["gates"])
    after()
    pe.wait_ge(s["down_in"], down_in)
    for u in range(TPC):
        cols = slice(u * P, (u + 1) * P)
        pairs_product(pe, k.ps[:, DOWN_BANK[u], :], [of(a, cols) for a in (k.act_hi, k.act_lo)],
                      [of(w, slice(0, HID)) for w in (k.wd_hi, k.wd_lo)], FB).then_inc(s["f_down"], 1)
    gate(pe, s["f_out"], nth(i, n, TPC, TPC), s["gates"])


def ffn_scalar(k, e, i, n):
    s = k.s
    for f in range(FB + 1):
        if f < FB:
            gate(e, s["f_gate"], nth(i, n, FB, f + 1), s["gates"])
            if f >= 2:
                gate(e, s["f_prod"], nth(i, n, FB, f + 1), s["gates"])
            e.activation(k.silu[:, f % 2, :], k.ps[:, 2 + 2 * (f % 2), :], ACT.Silu, scale=1.0 / (W_SCALE * A_SCALE))\
                .then_inc(s["f_silu"], 1)
        if f:
            gate(e, s["f_prod"], nth(i, n, FB, f + 2), s["gates"])
            e.activation(k.act_hi[:, f - 1, :], k.prod[:, (f - 1) % 2, :], ACT.Copy).then_inc(s["f_hi"], 1)


def ffn_vector(k, V, i, n, after):
    s, e = k.s, V.eng
    for f in range(FB + 1):
        if f < FB:
            gate(e, s["f_up"], nth(i, n, FB, f + 1), s["gates"])
            gate(e, s["f_silu"], nth(i, n, FB, f + 1), s["gates"])
            if f >= 2:
                gate(e, s["f_lo"], nth(i, n, FB, f - 1), s["gates"])
            e.scalar_tensor_tensor(out=k.prod[:, f % 2, :], in0=k.ps[:, 3 + 2 * (f % 2), :], scalar=1.0 / W_SCALE,
                                   in1=k.silu[:, f % 2, :], op0=ALU.mult, op1=ALU.mult).then_inc(s["f_prod"], 1)
        if f:
            gate(e, s["f_hi"], nth(i, n, FB, f), s["gates"])
            e.tensor_tensor(k.act_lo[:, f - 1, :], k.prod[:, (f - 1) % 2, :], k.act_hi[:, f - 1, :], ALU.subtract)\
                .then_inc(s["f_lo"], 1)
    after()
    for u in range(TPC):
        gate(e, s["f_down"], nth(i, n, TPC, u + 1), s["gates"])
        xt = k.x[:, bass.ds(i * TPC + u, 1), :].squeeze(1)
        e.scalar_tensor_tensor(out=xt, in0=k.ps[:, DOWN_BANK[u], :], scalar=0.5 / (W_SCALE * A_SCALE), in1=xt,
                               op0=ALU.mult, op1=ALU.add).then_inc(s["f_out"], 1)
    gate(e, s["f_out"], nth(i, n, TPC, TPC), s["gates"])


def ffn_phase_tensor(k, pe, n, m, routed):
    def before(i):
        if routed:
            apply_tensor(k, pe, i, 1 + NCH)

    before(0)
    norm_tensor(k, pe, 0, m)
    with pe.Fori(0, NCH - 1) as i:
        ffn_tensor(k, pe, i, n, lambda: before(i + 1), 64 if n > 1 else 32)
        norm_tensor(k, pe, i + 1, m)
    ffn_tensor(k, pe, NCH - 1, n, lambda: None, 64 if n > 1 else 32)


def ffn_phase_scalar(k, e, n, m, routed):
    def before(i):
        if routed:
            apply_scalar(k, e, i, 1 + NCH)
        norm_scalar(k, e, i, m)

    before(0)
    with e.Fori(0, NCH - 1) as i:
        ffn_scalar(k, e, i, n)
        before(i + 1)
    ffn_scalar(k, e, NCH - 1, n)


def ffn_phase_vector(k, V, n, m, routed):
    e = V.eng

    def before(i):
        if routed:
            spline_vector(k, V, i, 1 + NCH)
            add_vector(k, V, i)
        norm_stats_vector(k, V, i, m)
        norm_scale_vector(k, V, i, m)

    steps = NORM_STEPS + (ADD_STEPS + SPLINE_STEPS if routed else 0)
    V.enter(0, steps)
    before(0)
    V.leave(1)
    norm_low_vector(k, 0, m, e)
    with e.Fori(0, NCH - 1) as i:
        V.enter(i, steps)
        ffn_vector(k, V, i, n, lambda: before(i + 1))
        norm_low_vector(k, i + 1, m, e)
    V.leave(NCH - 1)
    ffn_vector(k, V, NCH - 1, n, lambda: None)



COMPS = 16
Q_SCALE = 16.0
SCORE = float(32 ** -0.5) / (Q_SCALE * Q_SCALE)
L1_INIT = 0.8 - 0.6 * float(np.exp(-0.3 * 12))


def c_setup_vector(k, V):
    s, e = k.s, V.eng

    def low(m):
        e.wait_ge(s["c_w_hi"], m + 1)
        e.scalar_tensor_tensor(out=k.w1_lo[:, m], in0=k.w1_nat[m], scalar=W_SCALE, in1=k.w1_hi[:, m],
                               op0=ALU.mult, op1=ALU.subtract).then_inc(s["c_w_lo"], 1)

    norm_stats_vector(k, V, 0, 1 + 2 * NCH)
    norm_scale_vector(k, V, 0, 1 + 2 * NCH)
    low(0)
    low(1)
    norm_low_vector(k, 0, 1 + 2 * NCH, e)
    e.wait_ge(s["c_w_lo"], 2)
    V.link(e.tensor_copy(k.causal_ts, k.c["causal"]))
    e.wait_ge(s["c_mask"], 1)
    V.link(e.tensor_copy(k.causal_st, k.ps[:, 7, 0:P]))
    V.link(e.tensor_copy(k.identb, k.c["ident"]))
    V.link(e.tensor_copy(k.sel, bcast(k.c["pick"].unsqueeze(2), [P, 16, P])))
    e.wait_ge(s["c_lam_in"], 80)
    rows = k.o2.rearrange("p u d -> p (u d)")[:, 0:128].rearrange("p (a d) -> p a d", a=4)
    prod = k.o2.rearrange("p u d -> p (u d)")[:, 128:192].rearrange("p (a d) -> p a d", a=2)
    V.link(e.tensor_tensor(prod, rows[:, 0:4:2, :], rows[:, 1:4:2, :], ALU.mult))
    e.tensor_reduce(k.lam[:, 0:2], prod, AXX, ALU.add).then_inc(s["c_lam_dot"], 1)
    e.tensor_scalar(k.g, k.g, (1.0 - L1_INIT) * A_SCALE, None, ALU.mult).then_inc(s["c_set"], 1)
    low(2)
    low(3)
    e.wait_ge(s["c_w_lo"], 4)
    V.link(e.memset(k.v1, 1.0))
    e.wait_ge(s["c_lam_exp"], 1)
    V.link(e.tensor_tensor(k.lam[:, 4:5], k.lam[:, 2:3], k.lam[:, 3:4], ALU.subtract))
    V.link(e.tensor_scalar(k.lam[:, 4:5], k.lam[:, 4:5], L1_INIT, None, ALU.add))


def c_setup_scalar(k, e):
    s = k.s
    norm_std_scalar(k, e, 0, 1 + 2 * NCH)
    norm_rows_scalar(k, e, 0, 1 + 2 * NCH)
    for m in range(4):
        if m == 0:
            e.wait_ge(s["c_in_qk"], 32)
        if m == 2:
            norm_high_scalar(k, e, 0, 1 + 2 * NCH, range(KC))
            e.wait_ge(s["c_in"], 32)
        e.activation(k.w1_hi[:, m], k.w1_nat[m], ACT.Copy, scale=W_SCALE).then_inc(s["c_w_hi"], 1)
    e.wait_ge(s["c_lam_dot"], 1)
    e.activation(k.lam[:, 2:4], k.lam[:, 0:2], ACT.Exp).then_inc(s["c_lam_exp"], 1)


def c_tensor(k, pe, i, next):
    s = k.s
    ht = (k.ht_hi, k.ht_lo)
    w1 = (k.w1_hi, k.w1_lo)

    def weight(m, cols):
        return [(lambda c, w=w: w[:, m, c, cols]) for w in w1]

    def scores(a):
        b, r = a // 4, slice(32 * (a % 4), 32 * (a % 4) + 32)
        gate(pe, s["c_qk_hi"], nth(i, 1, 8, 2 * b + 2), s["gates"])
        pe.wait_ge(s["c_set"], 1)
        if a:
            gate(pe, s["c_max"], nth(i, 1, 64, TPC * a - 2), s["gates"])
        for u in range(TPC):
            g, w = TPC * a + u, (u + 1) * P
            bank = 2 + g % 6
            pe.matmul(k.ps[:, bank, 0:w], k.qk_hi[r, b, u * P:w], k.qk_hi[r, 4 + b, 0:w], start=True, stop=False)
            pe.matmul(k.ps[:, bank, w - P:w], k.identb, k.causal_ts, start=False, stop=True)\
                .then_inc(s["c_score"], 1)

    def project(z, a):
        b, q = z // 2, z % 2
        gate(pe, s["c_qk"], nth(i, 1, 8, z + 1), s["gates"])
        pairs_product(pe, k.ps[:, z % 2, :], weight(q, slice(b * P, b * P + P)), [of(h, slice(0, CH)) for h in ht],
                      halfway=None if a is None else lambda: scores(a)).then_inc(s["c_qk_done"], 1)
        if a is not None:
            scores(a + 1)

    def value(u, a):
        pe.wait_ge(s["c_w_lo"], 4)
        gate(pe, s["c_v_in"], nth(i, 1, TPC, u + 1), s["gates"])
        pairs_product(pe, k.ps[:, u % 2, :], [of(h, slice(u * P, u * P + P)) for h in ht], weight(2, slice(0, HID)),
                      halfway=None if a is None else lambda: scores(a)).then_inc(s["c_v_done"], 1)
        if a is not None:
            scores(a + 1)

    for z in range(8):
        project(z, None if z < 2 else 2 * z - 4)
    gate(pe, s["c_qk"], nth(i, 1, 8, 10), s["gates"])
    value(0, 12)
    value(1, 14)
    value(2, None)
    gate(pe, s["c_negmax"], i + 1, s["gates"])
    for u in range(TPC):
        ins = pe.transpose(k.ps[:, 4, u * P:(u + 1) * P], k.nm[:, u].rearrange("p r c -> p (r c)"), k.c["ident"])
    ins.then_inc(s["c_max_turned"], 1)
    value(3, None)
    gate(pe, s["c_v_in"], nth(i, 1, TPC, 6), s["gates"])
    gate(pe, s["c_qk_lo"], nth(i, 1, 8, 8), s["gates"])
    gate(pe, s["c_maxt"], i + 1, s["gates"])
    for a in range(COMPS + 2):
        if a < COMPS:
            b, r = a // 4, slice(32 * (a % 4), 32 * (a % 4) + 32)
            for v in range(TPC):
                g = TPC * a + v
                if g >= 4:
                    gate(pe, s["c_exp"], nth(i, 1, 64, g - 3), s["gates"])
                out = k.ps[:, g % 4, v * P:CH]
                keys, queries = slice(v * P, v * P + P), slice(v * P, CH)
                pe.matmul(out, k.sel[r, a, :], k.maxt[r, queries], start=True, stop=False)
                pe.matmul(k.ps[:, g % 4, keys], k.identb, k.causal_st, start=False, stop=False)
                for x, y in ((k.qk_hi, k.qk_hi), (k.qk_hi, k.qk_lo), (k.qk_lo, k.qk_hi)):
                    ins = pe.matmul(out, x[r, 4 + b, keys], y[r, b, queries], start=False, stop=(x is k.qk_lo))
                ins.then_inc(s["c_scored"], 1)
        z = a - 1
        if 0 <= z < COMPS:
            gate(pe, s["c_exp"], nth(i, 1, 64, TPC * a), s["gates"])
            if z >= 2:
                gate(pe, s["c_oo"], nth(i, 1, COMPS, z - 1), s["gates"])
            for v in range(TPC):
                ins = pe.matmul(k.ps[0:65, 4 + z % 2, v * P:CH], k.v1[:, v, (z // 2) * 65:(z // 2) * 65 + 65],
                                k.pt[:, z % 2, v, v * P:CH], start=(v == 0), stop=(v == TPC - 1))
            ins.then_inc(s["c_av"], 1)
        z = a - 2
        if z >= 0:
            gate(pe, s["c_oo"], nth(i, 1, COMPS, z + 1), s["gates"])
            if z % 2 == 0 and z:
                gate(pe, s["c_head"], nth(i, 1, 8, z // 2), s["gates"])
            for u in range(TPC):
                ins = pe.transpose(k.ps[:, 6 + z % 2, 65 * u:65 * u + 65], k.oo[:, z % 2, u * P:(u + 1) * P],
                                   k.c["ident"][0:65, 0:65])
            ins.then_inc(s["c_back"], 1)
    if next is not None:
        norm_tensor(k, pe, next, 1 + 2 * NCH)
    for c in range(KC):
        gate(pe, s["c_o"], nth(i, 1, KC, c + 1), s["gates"])
        if c >= 2:
            gate(pe, s["c_ot_lo"], nth(i, 1, KC, c - 1), s["gates"])
        for u in range(TPC):
            ins = pe.transpose(k.ps[:, 2 + c % 2, u * P:(u + 1) * P], k.o1[:, u, c * P:(c + 1) * P], k.c["ident"])
        ins.then_inc(s["c_ot"], 1)
    gate(pe, s["c_ot_lo"], nth(i, 1, KC, KC), s["gates"])
    for u in range(TPC):
        pairs_product(pe, k.ps[:, 4 + u, :], [of(h, slice(u * P, u * P + P)) for h in (k.qk_hi, k.qk_lo)],
                      weight(3, slice(0, HID))).then_inc(s["c_out_done"], 1)
    gate(pe, s["c_out"], nth(i, 1, TPC, TPC), s["gates"])


def c_scalar(k, e, i, next):
    s = k.s
    for z in range(8):
        gate(e, s["c_qk_done"], nth(i, 1, 8, z + 1), s["gates"])
        if z >= 2:
            gate(e, s["c_qk_lo"], nth(i, 1, 8, z - 1), s["gates"])
        e.activation(k.qk32[:, z % 2, :], k.ps[:, z % 2, :], ACT.Copy, scale=Q_SCALE / (W_SCALE * A_SCALE))\
            .then_inc(s["c_qk"], 1)
        gate(e, s["c_qk"], nth(i, 1, 8, z + 3), s["gates"])
        e.activation(k.qk_hi[:, z // 2 + 4 * (z % 2), :], k.qk32[:, z % 2, :], ACT.Copy).then_inc(s["c_qk_hi"], 1)
    gate(e, s["c_max_turned"], i + 1, s["gates"])
    e.activation(k.maxt, k.ps[:, 4, :], ACT.Copy).then_inc(s["c_maxt"], 1)
    for a in range(COMPS):
        if next is not None and a == 5:
            norm_std_scalar(k, e, next, 1 + 2 * NCH)
        if next is not None and a == 7:
            norm_rows_scalar(k, e, next, 1 + 2 * NCH)
        if a >= 2:
            gate(e, s["c_av"], nth(i, 1, COMPS, a - 1), s["gates"])
        for v in range(TPC):
            g = TPC * a + v
            gate(e, s["c_scored"], nth(i, 1, 64, g + 1), s["gates"])
            e.activation(k.pt[:, a % 2, v, v * P:CH], k.ps[:, g % 4, v * P:CH], ACT.Exp, scale=SCORE)\
                .then_inc(s["c_exp"], 1)
    if next is not None:
        norm_high_scalar(k, e, next, 1 + 2 * NCH, (0, 1))
    gate(e, s["c_ms"], i + 1, s["gates"])
    e.activation(k.rms, k.mx2, ACT.Sqrt).then_inc(s["c_rms"], 1)
    if next is not None:
        norm_high_scalar(k, e, next, 1 + 2 * NCH, (2, 3))
    for c in range(KC):
        gate(e, s["c_ot"], nth(i, 1, KC, c + 1), s["gates"])
        e.activation(k.qk_hi[:, c, :], k.ps[:, 2 + c % 2, :], ACT.Copy).then_inc(s["c_ot_hi"], 1)


def c_pool(k, e, i):
    s = k.s
    for z in range(8):
        to = z // 2 + 4 * (z % 2)
        gate(e, s["c_qk_hi"], nth(i, 1, 8, z + 1), s["gates"])
        e.tensor_tensor(k.qk_lo[:, to, :], k.qk32[:, z % 2, :], k.qk_hi[:, to, :], ALU.subtract)\
            .then_inc(s["c_qk_lo"], 1)


C_STEPS = 2 + 8 * 7 + 4


def c_vector(k, V, i, next):
    s, e = k.s, V.eng
    def maxima(b, first=None):
        for g in range(16 * b, 16 * b + 16) if first is None else range(first, first + 4):
            a, u = g // 4, g % 4
            gate(e, s["c_score"], nth(i, 1, 64, g + 1), s["gates"])
            e.tensor_reduce(k.mx[:, u, a:a + 1], k.ps[:, 2 + g % 6, 0:(u + 1) * P], AXX, ALU.max)\
                .then_inc(s["c_max"], 1)

    def value(u):
        gate(e, s["c_v_done"], nth(i, 1, TPC, u + 1), s["gates"])
        e.tensor_scalar(k.v1[:, u, :].rearrange("p (h d) -> p h d", d=65)[:, :, 0:64],
                        k.ps[:, u % 2, :].rearrange("p (h d) -> p h d", d=64),
                        1.0 / (W_SCALE * A_SCALE), None, ALU.mult).then_inc(s["c_v_in"], 1)

    for b in range(3):
        maxima(b)
    for g in (48, 52, 56, 60):
        maxima(3, g)
        if g == 52 or g == 60:
            value(0 if g == 52 else 1)
    gate(e, s["c_max"], nth(i, 1, 64, 64), s["gates"])
    V.link(e.tensor_scalar(k.nmb, k.mx, -1.0, None, ALU.mult))
    V.link(e.tensor_tensor(k.mx, k.mx, k.nmb, ALU.add))
    for q in range(4):
        e.tensor_copy(k.nm[:, :, q, 0:16], k.nmb)
        ins = e.tensor_scalar(k.nm[:, :, q, 16:32], k.mx, -1.0, None, ALU.mult)
    ins.then_inc(s["c_negmax"], 1)
    value(2)
    value(3)
    for z in range(COMPS + 1):
        if z < COMPS:
            gate(e, s["c_av"], nth(i, 1, COMPS, z + 1), s["gates"])
            if z >= 2:
                gate(e, s["c_back"], nth(i, 1, COMPS, z - 1), s["gates"])
            e.tensor_copy(k.oo[:, z % 2, :], k.ps[0:65, 4 + z % 2, :]).then_inc(s["c_oo"], 1)
        if next is not None and z == 2:
            norm_stats_vector(k, V, next, 1 + 2 * NCH)
        if next is not None and z == 4:
            norm_scale_vector(k, V, next, 1 + 2 * NCH)
        if z and z % 2 == 0:
            gate(e, s["c_back"], nth(i, 1, COMPS, z), s["gates"])
            o = [k.ps[:, 6 + q, 0:260].rearrange("p (u d) -> p u d", d=65) for q in range(2)]
            cols = slice((z // 2 - 1) * 64, z // 2 * 64)
            r = k.rs
            for q in range(2):
                ins = e.reciprocal(r[:, q, :], o[q][:, :, 64])
            V.link(ins)
            V.link(e.tensor_scalar(r[:, 1, :], r[:, 1, :], k.lam[:, 4:5], None, ALU.mult))
            V.link(e.tensor_tensor(k.o1[:, :, cols], o[0][:, :, 0:64], bcast(r[:, 0, :].unsqueeze(2), [P, TPC, 64]),
                                   ALU.mult))
            V.link(e.tensor_tensor(k.o2, o[1][:, :, 0:64], bcast(r[:, 1, :].unsqueeze(2), [P, TPC, 64]), ALU.mult))
            e.tensor_tensor(k.o1[:, :, cols], k.o1[:, :, cols], k.o2, ALU.subtract).then_inc(s["c_head"], 1)
            gate(e, s["c_head"], nth(i, 1, 8, z // 2), s["gates"])
            V.link(e.tensor_tensor(k.o2, k.o1[:, :, cols], k.o1[:, :, cols], ALU.mult))
            V.link(e.tensor_reduce(k.mx2.rearrange("p (u h) -> p u h", h=8)[:, :, z // 2 - 1], k.o2, AXX, ALU.add))
            if z == COMPS:
                e.tensor_scalar(k.mx2, k.mx2, 1.0 / 64, 1e-5, ALU.mult, ALU.add).then_inc(s["c_ms"], 1)
            V.link(e.tensor_tensor(k.o1[:, :, cols], k.o1[:, :, cols], bcast(k.g.unsqueeze(1), [P, TPC, 64]), ALU.mult))
    if next is not None:
        norm_low_vector(k, next, 1 + 2 * NCH, e)
    gate(e, s["c_rms"], i + 1, s["gates"])
    rsqrt_vector(V, k.rr, k.rms, k.mx2, k.rr2)
    rr = k.rr.rearrange("p (u h) -> p u h", h=8)
    for c in range(KC):
        heads = k.o1[:, :, c * P:(c + 1) * P].rearrange("p u (h d) -> p u h d", d=64)
        e.tensor_tensor(heads, heads, bcast(rr[:, :, 2 * c:2 * c + 2].unsqueeze(3), [P, TPC, 2, 64]), ALU.mult)\
            .then_inc(s["c_o"], 1)
    for c in range(KC):
        gate(e, s["c_ot_hi"], nth(i, 1, KC, c + 1), s["gates"])
        e.tensor_tensor(k.qk_lo[:, c, :], k.ps[:, 2 + c % 2, :], k.qk_hi[:, c, :], ALU.subtract)\
            .then_inc(s["c_ot_lo"], 1)
    for u in range(TPC):
        gate(e, s["c_out_done"], nth(i, 1, TPC, u + 1), s["gates"])
        xt = k.x[:, bass.ds(i * TPC + u, 1), :].squeeze(1)
        e.scalar_tensor_tensor(out=xt, in0=k.ps[:, 4 + u, :], scalar=1.0 / (W_SCALE * A_SCALE), in1=xt,
                               op0=ALU.mult, op1=ALU.add).then_inc(s["c_out"], 1)
    gate(e, s["c_out"], nth(i, 1, TPC, TPC), s["gates"])


def bass_macaron(nc, d):
    with ExitStack() as ctx:
        ctx.enter_context(nc.allow_non_contiguous_dma(reason="a few short vectors laid along the partitions"))
        k = Kernel()
        k.d = d
        place(k, nc, ctx)
        k.ps = ctx.enter_context(nc.psum_tensor("ps", [P, 8, 512], F32))
        k.s = {n: ctx.enter_context(nc.semaphore(n)) for n in SEMAPHORES}
        k.ones, k.diag = k.rows[0:NTILE, 3, 0:P], k.rows[0:NTILE, 0, :]
        k.wdt_hi = k.wt_hi.rearrange("p c (b m) -> p (c b) m", m=P)
        k.wdt_lo = k.wt_lo.rearrange("p c (b m) -> p (c b) m", m=P)
        pairs = k.nat.rearrange("p a b -> p (a b)").bitcast(F16).rearrange("p (n c m) -> p n c m", n=4, m=P)
        k.wdo_hi, k.wdo_lo = [pairs[:, 0], pairs[:, 1]], [pairs[:, 2], pairs[:, 3]]
        s = k.s
        block = ctx.enter_context(nc.Block())

        def load_down(sp):
            for dst, src in ((k.wd_hi, d["wd_hi"]), (k.wd_lo, d["wd_lo"])):
                sp.dma_start(dst, src).then_inc(s["down_in"], 16)

        @block.sync
        def _(sp):
            setup_sync(k, sp)
            sp.wait_ge(s["wdo_out0"], 64)
            sp.wait_ge(s["wdo_out1"], 64)
            with sp.Fori(0, NCH) as i:
                b_sync(k, sp, i)
            sp.wait_ge(s["table_ready"], 2)
            load_down(sp)
            sp.wait_ge(s["n_norm"], 2 * NCH)
            w1 = [(m, d["L1_attn_" + name].rearrange("(c p) n -> p c n", p=P))
                  for m, name in enumerate(["Wq", "Wk", "Wv", "Wo"])]
            for m, src in w1[0:2]:
                sp.dma_start(k.w1_nat[m], src).then_inc(s["c_in_qk"], 16)
            for m, name in enumerate(["lambda_q1", "lambda_k1", "lambda_q2", "lambda_k2"]):
                sp.dma_start(k.o2.rearrange("p u d -> p (u d)")[:, 32 * m:32 * m + 32],
                             d["L1_attn_" + name].partition_broadcast(P)).then_inc(s["c_lam_in"], 16)
            sp.dma_start(k.g, d["L1_attn_g"].partition_broadcast(P)).then_inc(s["c_lam_in"], 16)
            sp.wait_ge(s["f_out"], NT)
            for m, src in w1[2:4]:
                sp.dma_start(k.w1_nat[m], src).then_inc(s["c_in"], 16)
            sp.wait_ge(s["c_out"], NT)
            load_down(sp)
            for c in range(NCH):
                sp.wait_ge(s["f_out"], NT + TPC * (c + 1))
                sp.dma_start(d["out"][c].rearrange("(u p) n -> p u n", p=P),
                             k.x[:, c * TPC:(c + 1) * TPC, :]).then_inc(s["x_out"], 16)
            sp.wait_ge(s["x_out"], 16 * NCH)

        @block.gpsimd
        def _(pool):
            setup_pool(k, pool)
            with pool.Fori(0, NCH) as i:
                b_pool(k, pool, i)
            with pool.Fori(0, NCH) as i:
                c_pool(k, pool, i)

        @block.tensor
        def _(pe):
            use_work(k, k.work, k.h, k.nr.rearrange("p a b -> p (a b)"))
            setup_tensor(k, pe)
            minmax_tensor(k, pe, 1, "")
            pe.wait_ge(s["b_in"], 160)
            apply_tensor(k, pe, 0, 1)
            norm_tensor(k, pe, 0, 1)
            with pe.Fori(0, NCH - 1) as i:
                b_tensor(k, pe, i, i + 1)
            b_tensor(k, pe, NCH - 1, None)
            minmax_tensor(k, pe, 2, "")
            use_work(k, k.work1, k.h, k.work1[:, 2048:4096])
            ffn_phase_tensor(k, pe, 1, 1 + NCH, True)
            pe.wait_ge(s["f_out"], NT)
            pe.transpose(k.ps[:, 7, 0:P], k.c["causal"], k.c["ident"]).then_inc(s["c_mask"], 1)
            norm_tensor(k, pe, 0, 1 + 2 * NCH)
            pe.wait_ge(s["c_w_lo"], 2)
            with pe.Fori(0, NCH - 1) as i:
                c_tensor(k, pe, i, i + 1)
            c_tensor(k, pe, NCH - 1, None)
            ffn_phase_tensor(k, pe, 1 + NCH, 1 + 3 * NCH, False)

        @block.scalar
        def _(act):
            use_rows(k, k.rows2, k.rows)
            setup_scalar(k, act)
            use_work(k, k.work, k.h, k.nr.rearrange("p a b -> p (a b)"))
            use_rows(k, k.masked2, k.y2)
            apply_scalar(k, act, 0, 1)
            norm_std_scalar(k, act, 0, 1)
            norm_rows_scalar(k, act, 0, 1)
            act.wait_ge(s["wdo_out0"], 64)
            act.wait_ge(s["wdo_out1"], 64)
            b_scalar(k, act, 0, None, 1)
            with act.Fori(0, NCH - 2) as i:
                b_scalar(k, act, i + 1, i, i + 2)
            b_scalar(k, act, NCH - 1, NCH - 2, None)
            token_stats_scalar(k, act, NCH - 1, 1 + NCH, "")
            token_signs_scalar(k, act, NCH - 1, 1 + NCH, "")
            use_work(k, k.work1, k.h, k.work1[:, 2048:4096])
            ffn_phase_scalar(k, act, 1, 1 + NCH, True)
            c_setup_scalar(k, act)
            with act.Fori(0, NCH - 1) as i:
                c_scalar(k, act, i, i + 1)
            c_scalar(k, act, NCH - 1, None)
            ffn_phase_scalar(k, act, 1 + NCH, 1 + 3 * NCH, False)

        @block.vector
        def _(dve):
            use_rows(k, k.rows2, k.rows)
            V = Steps(dve, s["v_step"], s["gates"])
            for name in ("n_lo", "b_qf", "b_rope", "b_v_in", "b_y", "b_mask", "b_ot_lo", "f_prod", "c_qk", "c_v_in"):
                dve.sem_inc(s[name], 2)
            setup_vector(k, V)
            minmax_vector(k, V, 1, "")
            use_work(k, k.work, k.h, k.nr.rearrange("p a b -> p (a b)"))
            V.link(dve.memset(k.acc, -BIG))
            dve.wait_ge(s["b_in"], 160)
            V.link(dve.tensor_copy(k.spread.rearrange("p (h f) -> p h f", f=32),
                                   bcast(k.c["ident"][0:24, 0:24].unsqueeze(2), [24, 24, 32])))
            spline_vector(k, V, 0, 1)
            add_vector(k, V, 0)
            norm_stats_vector(k, V, 0, 1)
            norm_scale_vector(k, V, 0, 1)
            dve.wait_ge(s["wdo_out0"], 64)
            dve.wait_ge(s["wdo_out1"], 64)
            b_vector(k, V, 0, None, 1)
            with dve.Fori(0, NCH - 2) as i:
                V.enter(i, ADD_STEPS + SPLINE_STEPS + NORM_STEPS + B_STEPS + STATS_STEPS + ROUTE_STEPS)
                b_vector(k, V, i + 1, i, i + 2)
            V.leave(NCH - 2)
            b_vector(k, V, NCH - 1, NCH - 2, None)
            token_stats_vector(k, V, NCH - 1, 1 + NCH, "")
            routing_vector(k, V, NCH - 1, 1 + NCH, "")
            minmax_vector(k, V, 2, "")
            use_work(k, k.work1, k.h, k.work1[:, 2048:4096])
            ffn_phase_vector(k, V, 1, 1 + NCH, True)
            c_setup_vector(k, V)
            with dve.Fori(0, NCH - 1) as i:
                V.enter(i, NORM_STEPS + C_STEPS)
                c_vector(k, V, i, i + 1)
            V.leave(NCH - 1)
            c_vector(k, V, NCH - 1, None)
            ffn_phase_vector(k, V, 1 + NCH, 1 + 3 * NCH, False)


_INS = ["L0_attn_hidden_states", "L0_attn_Wq", "L0_attn_bq", "L0_attn_Wk", "L0_attn_bk", "L0_attn_Wv",
        "L0_attn_bv", "L0_attn_Wo", "L0_attn_bo", "L0_attn_rand_matrix", "L0_ffn_ln_gamma", "L0_ffn_ln_beta",
        "L0_ffn_spline_bases", "L0_ffn_spline_slopes", "L0_ffn_output_scale", "L1_attn_Wq", "L1_attn_Wk",
        "L1_attn_Wv", "L1_attn_Wo", "L1_attn_lambda_q1", "L1_attn_lambda_k1", "L1_attn_lambda_q2",
        "L1_attn_lambda_k2", "L1_attn_g", "L1_ffn_SU_ug", "L1_ffn_SU_dp", "L1_ffn_Wscale_ug",
        "L1_ffn_Wscale_dp", "L1_ffn_W_up", "L1_ffn_W_gate", "L1_ffn_W_down"]


def kernel(**inputs):
    import numpy as _np
    import concourse.bacc as _bacc
    from concourse import mybir as _mybir
    from concourse.bass_utils import run_bass_kernel_spmd as _run

    nc = _bacc.Bacc("TRN2", target_bir_lowering=False, num_devices=1, dynamic_dma_scratch_size=1024)
    arrays, d = {}, {}
    for name in _INS:
        a = _np.ascontiguousarray(inputs[name])
        arrays[f"in_{name}_dram"] = a
        d[name] = nc.dram_tensor(f"in_{name}_dram", a.shape, _mybir.dt.from_np(a.dtype), kind="ExternalInput").ap()
    arrays["constants_dram"] = CONSTS
    d["constants"] = nc.dram_tensor("constants_dram", CONSTS.shape, F32, kind="ExternalInput").ap()
    for part in ("hi", "lo"):
        d["wd_" + part] = nc.dram_tensor(f"wd_{part}_dram", (P, FB, HID), F16).ap()
    d["values"] = nc.dram_tensor("values_dram", (CH, 256), F32).ap()
    d["out"] = nc.dram_tensor("out_dram", (4, 512, 512), F32, kind="ExternalOutput").ap()
    bass_macaron(nc, d)
    r = _run(nc, [arrays], core_ids=[0])
    return r.results[0]["out_dram"]
```
